# Optimizing a Trainium2 kernel written in Bass

```python
import numpy as np
import jax
import jax.numpy as jnp

def _softmax(x, axis=-1):
    return jax.nn.softmax(x, axis=axis)

def _gelu(x):
    return jax.nn.gelu(x, approximate=True)

def _silu(x):
    return jax.nn.silu(x)

def _sigmoid(x):
    return jax.nn.sigmoid(x)

def _layernorm(x, axis=-1, eps=1e-05):
    m = jnp.mean(x, axis=axis, keepdims=True)
    v = jnp.var(x, axis=axis, keepdims=True)
    return (x - m) / jnp.sqrt(v + eps)

def _scatter_add(tgt, idx, src, axis=0):
    return tgt.at[idx].add(src)

def _segment_sum(src, seg, n):
    return jax.ops.segment_sum(src, seg, n)
kernel_name = 'mk_decoder_postln_d2_seqx_r8_6189ea'

def setup_inputs(seed: int=0):
    np.random.seed(seed)
    _w = jnp.asarray

    def _rec_inputs():
        import jax
        import jax.numpy as jnp
        _rk = jax.random.key(seed)
        x = -0.0002928 + 1 * jax.random.normal(jax.random.fold_in(_rk, 1), (4, 256, 512), jnp.float32)
        _lenS = 256 - jax.random.randint(jax.random.fold_in(_rk, 7), (4,), 0, max(1, 256 // 4) + 1, jnp.int32)
        _lenS2 = 64 - jax.random.randint(jax.random.fold_in(_rk, 8), (4,), 0, max(1, 64 // 4) + 1, jnp.int32)
        _ctx_4096P = jax.random.normal(jax.random.fold_in(_rk, 11), (4, 16, 512), jnp.float32)
        _ctx_4096c = jax.random.dirichlet(jax.random.fold_in(_rk, 511), 0.3 * jnp.ones((16,), jnp.float32), (4, 64))
        _ctx_4096t = jnp.einsum('bsk,bkd->bsd', _ctx_4096c, _ctx_4096P)
        _ctx_4096t = _ctx_4096t * jax.lax.rsqrt(jnp.mean(jnp.square(_ctx_4096t)) + 1e-12) * 0.953939
        ctx_4096 = -2.8382e-05 + 0.999851 * (_ctx_4096t + 0.3 * jax.random.normal(jax.random.fold_in(_rk, 611), (4, 64, 512), jnp.float32))
        _validS = jnp.arange(256)[None, :] < _lenS[:, None]
        _validS2 = jnp.arange(64)[None, :] < _lenS2[:, None]
        _causal = jnp.tril(jnp.ones((256, 256), dtype=bool))
        mask_1x1xSxS2_ff0 = jnp.where(jnp.ones((1, 1, 256, 64), dtype=bool), 0.0, -1000000000.0).astype(jnp.float32)
        return (x, ctx_4096, mask_1x1xSxS2_ff0)
    x, ctx_4096, mask_1x1xSxS2_ff0 = _rec_inputs()

    def _L0_attn_setup():
        import jax, jax.numpy as jnp
        import numpy as np
        B, T, D = (2, 256, 512)
        H = 32
        HKV = 1
        HD = D // H
        key = jax.random.key(seed)
        ks = jax.random.split(key, 9)
        s = lambda fan_in: 1.0 / np.sqrt(fan_in)
        return {'x': jax.random.normal(ks[0], (B, T, D), dtype=jnp.float32), 'wq_w': jax.random.normal(ks[1], (H * HD, D), dtype=jnp.float32) * s(D), 'wq_b': jax.random.normal(ks[2], (H * HD,), dtype=jnp.float32) * 0.02, 'wk_w': jax.random.normal(ks[3], (HKV * HD, D), dtype=jnp.float32) * s(D), 'wk_b': jax.random.normal(ks[4], (HKV * HD,), dtype=jnp.float32) * 0.02, 'wv_w': jax.random.normal(ks[5], (HKV * HD, D), dtype=jnp.float32) * s(D), 'wv_b': jax.random.normal(ks[6], (HKV * HD,), dtype=jnp.float32) * 0.02, 'wo_w': jax.random.normal(ks[7], (D, H * HD), dtype=jnp.float32) * s(H * HD), 'wo_b': jax.random.normal(ks[8], (D,), dtype=jnp.float32) * 0.02}
    _L0_attn_all = _L0_attn_setup()
    _L0_attn_in = {k: v for k, v in _L0_attn_all.items() if k in ('wq_w', 'wq_b', 'wk_w', 'wk_b', 'wv_w', 'wv_b', 'wo_w', 'wo_b')}
    del _L0_attn_all

    def _L0_xattn_setup():
        import jax, jax.numpy as jnp
        import numpy as np
        B, Q, K, D = (1, 128, 6404, 512)
        H, KVH, HD = (32, 8, 128)
        GROUPS = H // KVH
        EPS = 1e-05

        def _rmsnorm(x, w):
            xf = x.astype(jnp.float32)
            var = jnp.mean(xf * xf, axis=-1, keepdims=True)
            return (xf * jax.lax.rsqrt(var + EPS)).astype(x.dtype) * w
        key = jax.random.key(seed)
        ks = jax.random.split(key, 8)
        s = 0.02
        return {'hidden_states': jax.random.normal(ks[0], (B, Q, D), jnp.float32), 'cross_attention_states': jax.random.normal(ks[1], (B, K, D), jnp.float32), 'attention_mask': jnp.zeros((B, 1, Q, K), jnp.float32), 'Wq': jax.random.normal(ks[2], (H * HD, D), jnp.float32) * s, 'Wk': jax.random.normal(ks[3], (KVH * HD, D), jnp.float32) * s, 'Wv': jax.random.normal(ks[4], (KVH * HD, D), jnp.float32) * s, 'Wo': jax.random.normal(ks[5], (D, H * HD), jnp.float32) * s, 'q_norm_w': jnp.ones((HD,), jnp.float32), 'k_norm_w': jnp.ones((HD,), jnp.float32)}
    _L0_xattn_all = _L0_xattn_setup()
    _L0_xattn_in = {k: v for k, v in _L0_xattn_all.items() if k in ('Wq', 'Wk', 'Wv', 'Wo', 'q_norm_w', 'k_norm_w')}
    del _L0_xattn_all

    def _L0_ffn_setup():
        import jax, jax.numpy as jnp
        import numpy as np
        BATCH, TOK, DIM, OUT = (4, 256, 512, 512)
        E, R, TOP_K = (8, 16, 2)
        SCALING = 16.0 / R
        key = jax.random.key(seed)
        ks = jax.random.split(key, 6)
        return {'x': jax.random.normal(ks[0], (BATCH, TOK, DIM), dtype=jnp.float32), 'W_base': jax.random.normal(ks[1], (OUT, DIM), dtype=jnp.float32) / np.sqrt(DIM), 'b_base': jax.random.normal(ks[2], (OUT,), dtype=jnp.float32) * 0.01, 'W_gate': jax.random.normal(ks[3], (E, DIM), dtype=jnp.float32) * 0.01, 'A': jax.random.normal(ks[4], (E, R, DIM), dtype=jnp.float32) / np.sqrt(DIM), 'B': jax.random.normal(ks[5], (OUT, OUT // OUT * R * 0 + R), dtype=jnp.float32)[None].repeat(E, 0) * 0.0 + jax.random.normal(ks[5], (E, OUT, R), dtype=jnp.float32) * 0.02}
    _L0_ffn_all = _L0_ffn_setup()
    _L0_ffn_in = {k: v for k, v in _L0_ffn_all.items() if k in ('W_base', 'b_base', 'W_gate', 'A', 'B')}
    del _L0_ffn_all

    def _L1_attn_setup():
        import jax, jax.numpy as jnp
        import numpy as np
        B, S, D = (2, 256, 512)
        NQ, NKV, DK = (32, 4, 128)
        GROUPS = NQ // NKV
        NEG = -1000000000.0
        key = jax.random.key(seed)
        ks = jax.random.split(key, 5)
        return {'x': jax.random.normal(ks[0], (B, S, D), jnp.float32), 'Wq': jax.random.normal(ks[1], (D, NQ * DK), jnp.float32) * 0.02, 'Wk': jax.random.normal(ks[2], (D, NKV * DK), jnp.float32) * 0.02, 'Wv': jax.random.normal(ks[3], (D, NKV * DK), jnp.float32) * 0.02, 'Wo': jax.random.normal(ks[4], (NQ * DK, D), jnp.float32) * 0.02}
    _L1_attn_all = _L1_attn_setup()
    _L1_attn_in = {k: v for k, v in _L1_attn_all.items() if k in ('Wq', 'Wk', 'Wv', 'Wo')}
    del _L1_attn_all

    def _L1_xattn_setup():
        import jax, jax.numpy as jnp
        import numpy as np
        import math
        HIDDEN = 512
        N_HEADS = 32
        HEAD_DIM = 128
        N_KV_HEADS = 4
        N_GROUPS = N_HEADS // N_KV_HEADS
        key = jax.random.key(seed)
        ks = jax.random.split(key, 6)
        B, NL, S = (8, 64, 512)
        latents = jax.random.normal(ks[0], (B, NL, HIDDEN), dtype=jnp.float32)
        context = jax.random.normal(ks[1], (B, S, HIDDEN), dtype=jnp.float32)
        scale = 1.0 / math.sqrt(HIDDEN)
        Wq = jax.random.normal(ks[2], (HIDDEN, N_HEADS * HEAD_DIM), dtype=jnp.float32) * scale
        Wk = jax.random.normal(ks[3], (HIDDEN, N_KV_HEADS * HEAD_DIM), dtype=jnp.float32) * scale
        Wv = jax.random.normal(ks[4], (HIDDEN, N_KV_HEADS * HEAD_DIM), dtype=jnp.float32) * scale
        Wo = jax.random.normal(ks[5], (N_HEADS * HEAD_DIM, HIDDEN), dtype=jnp.float32) * scale
        return {'latents': latents, 'context': context, 'Wq': Wq, 'Wk': Wk, 'Wv': Wv, 'Wo': Wo}
    _L1_xattn_all = _L1_xattn_setup()
    _L1_xattn_in = {k: v for k, v in _L1_xattn_all.items() if k in ('Wq', 'Wk', 'Wv', 'Wo')}
    del _L1_xattn_all

    def _L1_ffn_setup():
        import jax, jax.numpy as jnp
        import numpy as np
        B, S, D, O, E, R = (4, 256, 512, 512, 8, 16)
        SCALING = 32.0 / 16.0
        MAX_THRESHOLD = 0.125
        key = jax.random.key(seed)
        ks = jax.random.split(key, 8)
        return {'x': jax.random.normal(ks[0], (B, S, D), jnp.float32), 'W_base': jax.random.normal(ks[1], (O, D), jnp.float32) * (1.0 / np.sqrt(D)), 'b_base': jax.random.normal(ks[2], (O,), jnp.float32) * 0.02, 'W_gate': jax.random.normal(ks[3], (E, D), jnp.float32) * (1.0 / np.sqrt(D)), 'W_thr': jax.random.normal(ks[4], (D,), jnp.float32) * (1.0 / np.sqrt(D)), 'b_thr': jax.random.normal(ks[5], (1,), jnp.float32) * 0.02, 'A_w': jax.random.normal(ks[6], (E, R, D), jnp.float32) * (1.0 / np.sqrt(D)), 'B_w': jax.random.normal(ks[7], (E, O, R), jnp.float32) * (1.0 / np.sqrt(R))}
    _L1_ffn_all = _L1_ffn_setup()
    _L1_ffn_in = {k: v for k, v in _L1_ffn_all.items() if k in ('W_base', 'b_base', 'W_gate', 'W_thr', 'b_thr', 'A_w', 'B_w')}
    del _L1_ffn_all
    return {'x': x, 'ctx_4096': ctx_4096, 'mask_1x1xSxS2_ff0': mask_1x1xSxS2_ff0, 'L0_attn_wq_w': _L0_attn_in['wq_w'], 'L0_attn_wq_b': _L0_attn_in['wq_b'], 'L0_attn_wk_w': _L0_attn_in['wk_w'], 'L0_attn_wk_b': _L0_attn_in['wk_b'], 'L0_attn_wv_w': _L0_attn_in['wv_w'], 'L0_attn_wv_b': _L0_attn_in['wv_b'], 'L0_attn_wo_w': _L0_attn_in['wo_w'], 'L0_attn_wo_b': _L0_attn_in['wo_b'], 'L0_xattn_Wq': _L0_xattn_in['Wq'], 'L0_xattn_Wk': _L0_xattn_in['Wk'], 'L0_xattn_Wv': _L0_xattn_in['Wv'], 'L0_xattn_Wo': _L0_xattn_in['Wo'], 'L0_xattn_q_norm_w': _L0_xattn_in['q_norm_w'], 'L0_xattn_k_norm_w': _L0_xattn_in['k_norm_w'], 'L0_ffn_W_base': _L0_ffn_in['W_base'], 'L0_ffn_b_base': _L0_ffn_in['b_base'], 'L0_ffn_W_gate': _L0_ffn_in['W_gate'], 'L0_ffn_A': _L0_ffn_in['A'], 'L0_ffn_B': _L0_ffn_in['B'], 'L1_attn_Wq': _L1_attn_in['Wq'], 'L1_attn_Wk': _L1_attn_in['Wk'], 'L1_attn_Wv': _L1_attn_in['Wv'], 'L1_attn_Wo': _L1_attn_in['Wo'], 'L1_xattn_Wq': _L1_xattn_in['Wq'], 'L1_xattn_Wk': _L1_xattn_in['Wk'], 'L1_xattn_Wv': _L1_xattn_in['Wv'], 'L1_xattn_Wo': _L1_xattn_in['Wo'], 'L1_ffn_W_base': _L1_ffn_in['W_base'], 'L1_ffn_b_base': _L1_ffn_in['b_base'], 'L1_ffn_W_gate': _L1_ffn_in['W_gate'], 'L1_ffn_W_thr': _L1_ffn_in['W_thr'], 'L1_ffn_b_thr': _L1_ffn_in['b_thr'], 'L1_ffn_A_w': _L1_ffn_in['A_w'], 'L1_ffn_B_w': _L1_ffn_in['B_w']}

def reference(x, ctx_4096, mask_1x1xSxS2_ff0, L0_attn_wq_w, L0_attn_wq_b, L0_attn_wk_w, L0_attn_wk_b, L0_attn_wv_w, L0_attn_wv_b, L0_attn_wo_w, L0_attn_wo_b, L0_xattn_Wq, L0_xattn_Wk, L0_xattn_Wv, L0_xattn_Wo, L0_xattn_q_norm_w, L0_xattn_k_norm_w, L0_ffn_W_base, L0_ffn_b_base, L0_ffn_W_gate, L0_ffn_A, L0_ffn_B, L1_attn_Wq, L1_attn_Wk, L1_attn_Wv, L1_attn_Wo, L1_xattn_Wq, L1_xattn_Wk, L1_xattn_Wv, L1_xattn_Wo, L1_ffn_W_base, L1_ffn_b_base, L1_ffn_W_gate, L1_ffn_W_thr, L1_ffn_b_thr, L1_ffn_A_w, L1_ffn_B_w):
    import jax
    import jax.numpy as jnp

    def _L0_attn_ref(x, wq_w, wq_b, wk_w, wk_b, wv_w, wv_b, wo_w, wo_b):
        import jax, jax.numpy as jnp
        import numpy as np
        B, T, D = (2, 256, 512)
        H = 32
        HKV = 1
        HD = D // H
        b, t, d = x.shape
        q = (x @ wq_w.T + wq_b).reshape(b, t, H, HD)
        k = (x @ wk_w.T + wk_b).reshape(b, t, HKV, HD)
        v = (x @ wv_w.T + wv_b).reshape(b, t, HKV, HD)
        k1 = k[:, :, 0, :]
        v1 = v[:, :, 0, :]
        scores = jnp.einsum('bqhd,bkd->bhqk', q, k1) / jnp.sqrt(jnp.float32(HD))
        causal = jnp.tril(jnp.ones((t, t), dtype=bool))
        scores = jnp.where(causal, scores, -jnp.inf)
        weights = jax.nn.softmax(scores, axis=-1)
        attn = jnp.einsum('bhqk,bkd->bqhd', weights, v1)
        attn = attn.reshape(b, t, H * HD)
        return attn @ wo_w.T + wo_b

    def _L0_xattn_ref(hidden_states, cross_attention_states, attention_mask, Wq, Wk, Wv, Wo, q_norm_w, k_norm_w):
        import jax, jax.numpy as jnp
        import numpy as np
        B, Q, K, D = (1, 128, 6404, 512)
        H, KVH, HD = (32, 8, 128)
        GROUPS = H // KVH
        EPS = 1e-05

        def _rmsnorm(x, w):
            xf = x.astype(jnp.float32)
            var = jnp.mean(xf * xf, axis=-1, keepdims=True)
            return (xf * jax.lax.rsqrt(var + EPS)).astype(x.dtype) * w
        bsz, q_len, _ = hidden_states.shape
        kv_len = cross_attention_states.shape[1]
        q = (hidden_states @ Wq.T).reshape(bsz, q_len, H, HD).transpose(0, 2, 1, 3)
        k = (cross_attention_states @ Wk.T).reshape(bsz, kv_len, KVH, HD).transpose(0, 2, 1, 3)
        v = (cross_attention_states @ Wv.T).reshape(bsz, kv_len, KVH, HD).transpose(0, 2, 1, 3)
        q = _rmsnorm(q, q_norm_w)
        k = jnp.repeat(k, GROUPS, axis=1)
        v = jnp.repeat(v, GROUPS, axis=1)
        k = _rmsnorm(k, k_norm_w)
        scale = 1.0 / np.sqrt(HD)
        scores = jnp.einsum('bhqd,bhkd->bhqk', q, k) * scale
        scores = scores + attention_mask[:, :, :, :kv_len]
        probs = jax.nn.softmax(scores.astype(jnp.float32), axis=-1).astype(q.dtype)
        out = jnp.einsum('bhqk,bhkd->bhqd', probs, v)
        out = out.transpose(0, 2, 1, 3).reshape(bsz, q_len, H * HD)
        return out @ Wo.T

    def _L0_ffn_ref(x, W_base, b_base, W_gate, A, B):
        import jax, jax.numpy as jnp
        import numpy as np
        BATCH, TOK, DIM, OUT = (4, 256, 512, 512)
        E, R, TOP_K = (8, 16, 2)
        SCALING = 16.0 / R
        result = jnp.einsum('bnd,od->bno', x, W_base) + b_base
        logits = jnp.einsum('bnd,ed->bne', x, W_gate)
        probs = jax.nn.softmax(logits.astype(jnp.float32), axis=-1)
        top_p, top_i = jax.lax.top_k(probs, TOP_K)
        top_p = top_p / jnp.sum(top_p, axis=-1, keepdims=True)
        top_p = top_p.astype(x.dtype)
        route_w = jnp.sum(jax.nn.one_hot(top_i, E, dtype=x.dtype) * top_p[..., None], axis=-2)
        h = jnp.einsum('bnd,erd->bner', x, A)
        hw = h * route_w[..., None]
        delta = jnp.einsum('bner,eor->bno', hw, B)
        return result + delta * SCALING

    def _L1_attn_ref(x, Wq, Wk, Wv, Wo):
        import jax, jax.numpy as jnp
        import numpy as np
        B, S, D = (2, 256, 512)
        NQ, NKV, DK = (32, 4, 128)
        GROUPS = NQ // NKV
        NEG = -1000000000.0
        b, s, _ = x.shape
        Q = (x @ Wq).reshape(b, s, NQ, DK).transpose(0, 2, 1, 3)
        K = (x @ Wk).reshape(b, s, NKV, DK).transpose(0, 2, 1, 3)
        V = (x @ Wv).reshape(b, s, NKV, DK).transpose(0, 2, 1, 3)
        K = jnp.repeat(K, GROUPS, axis=1)
        V = jnp.repeat(V, GROUPS, axis=1)
        scores = jnp.einsum('bhqd,bhkd->bhqk', Q, K) / np.sqrt(DK).astype(np.float32)
        mask = jnp.triu(jnp.ones((s, s), jnp.float32), k=1)
        scores = jnp.where(mask == 0, NEG, scores)
        attn = jax.nn.softmax(scores, axis=-1)
        out = jnp.einsum('bhqk,bhkd->bhqd', attn, V)
        out = out.transpose(0, 2, 1, 3).reshape(b, s, NQ * DK)
        return out @ Wo

    def _L1_xattn_ref(latents, context, Wq, Wk, Wv, Wo):
        import jax, jax.numpy as jnp
        import numpy as np
        import math
        HIDDEN = 512
        N_HEADS = 32
        HEAD_DIM = 128
        N_KV_HEADS = 4
        N_GROUPS = N_HEADS // N_KV_HEADS
        b, q_len, _ = latents.shape
        kv_len = q_len + context.shape[1]
        hidden_states = jnp.concatenate([context, latents], axis=1)
        q = (latents @ Wq).reshape(b, q_len, N_KV_HEADS, N_GROUPS, HEAD_DIM)
        k = (hidden_states @ Wk).reshape(b, kv_len, N_KV_HEADS, HEAD_DIM)
        v = (hidden_states @ Wv).reshape(b, kv_len, N_KV_HEADS, HEAD_DIM)
        scale = 1.0 / math.sqrt(HEAD_DIM)
        scores = jnp.einsum('bqhgd,bkhd->bhgqk', q, k) * scale
        attn = jax.nn.softmax(scores.astype(jnp.float32), axis=-1).astype(q.dtype)
        out = jnp.einsum('bhgqk,bkhd->bqhgd', attn, v)
        out = out.reshape(b, q_len, N_HEADS * HEAD_DIM)
        return out @ Wo

    def _L1_ffn_ref(x, W_base, b_base, W_gate, W_thr, b_thr, A_w, B_w):
        import jax, jax.numpy as jnp
        import numpy as np
        B, S, D, O, E, R = (4, 256, 512, 512, 8, 16)
        SCALING = 32.0 / 16.0
        MAX_THRESHOLD = 0.125
        base = jnp.einsum('bsd,od->bso', x, W_base) + b_base
        xf = x.reshape(-1, D)
        gate = jax.nn.softmax(xf @ W_gate.T, axis=-1)
        thr = jax.nn.sigmoid(xf @ W_thr + b_thr[0]) * MAX_THRESHOLD
        adapted = gate - thr[:, None]
        selected = (adapted >= 0).astype(x.dtype)
        w = adapted * selected
        wsum = jnp.sum(w, axis=-1, keepdims=True)
        wsum = jnp.where(wsum == 0, jnp.ones_like(wsum), wsum)
        w = w / wsum
        h = jnp.einsum('nd,erd->ner', xf, A_w)
        moe = jnp.einsum('ner,ne,eor->no', h, w, B_w) * SCALING
        return base + moe.reshape(base.shape)
    x = _layernorm(x + _L0_attn_ref(x, L0_attn_wq_w, L0_attn_wq_b, L0_attn_wk_w, L0_attn_wk_b, L0_attn_wv_w, L0_attn_wv_b, L0_attn_wo_w, L0_attn_wo_b), axis=-1)
    x = _layernorm(x + _L0_xattn_ref(x, ctx_4096, mask_1x1xSxS2_ff0, L0_xattn_Wq, L0_xattn_Wk, L0_xattn_Wv, L0_xattn_Wo, L0_xattn_q_norm_w, L0_xattn_k_norm_w), axis=-1)
    x = _layernorm(x + _L0_ffn_ref(x, L0_ffn_W_base, L0_ffn_b_base, L0_ffn_W_gate, L0_ffn_A, L0_ffn_B), axis=-1)
    x = _layernorm(x + _L1_attn_ref(x, L1_attn_Wq, L1_attn_Wk, L1_attn_Wv, L1_attn_Wo), axis=-1)
    x = _layernorm(x + _L1_xattn_ref(x, ctx_4096, L1_xattn_Wq, L1_xattn_Wk, L1_xattn_Wv, L1_xattn_Wo), axis=-1)
    x = _layernorm(x + _L1_ffn_ref(x, L1_ffn_W_base, L1_ffn_b_base, L1_ffn_W_gate, L1_ffn_W_thr, L1_ffn_b_thr, L1_ffn_A_w, L1_ffn_B_w), axis=-1)
    return x

_drawn_inputs = setup_inputs


def setup_inputs(seed=0):
    import zlib

    import numpy as np

    out = dict(_drawn_inputs(seed))
    spreads = {'L0_xattn_q_norm_w': (1.0, 0.6), 'L0_xattn_k_norm_w': (1.0, 0.6)}
    factors = {'L0_attn_wq_b': 8.0,
     'L0_attn_wk_b': 8.0,
     'L0_ffn_b_base': 4.096,
     'L1_attn_Wq': 3.519,
     'L1_attn_Wk': 3.585,
     'L1_ffn_b_base': 5.69}
    for name, (base, spread) in spreads.items():
        noise = np.random.default_rng([zlib.crc32(name.encode()), seed]).standard_normal(out[name].shape)
        drawn = base * np.exp(spread * noise) if base else spread * noise
        out[name] = jnp.asarray(drawn.astype(out[name].dtype))
    for name, factor in factors.items():
        out[name] = (out[name] * factor).astype(out[name].dtype)
    return out
```

```python
from collections import namedtuple
from contextlib import ExitStack

import concourse.bass as bass
from concourse import mybir

F = mybir.dt.float32
R = mybir.dt.float32r
ALU = mybir.AluOpType
ACT = mybir.ActivationFunctionType
AX = mybir.AxisListType

P = 128
B, S, D = 4, 256, 512
TOK = B * S
NT = TOK // P
KT = D // P
CTX = 64
HD = 128
NH = 32
NE, RANK = 8, 16
ER = NE * RANK
GATE = NE + 2
EPS = 1e-5
MASKED = -1e30


def f32(ap):
    return ap.bitcast(F)


def products(nc, out, terms, start=True, stop=True, cover=False):
    passes = []
    for lh, ll, rh, rl in terms:
        passes += [(lh, rh)] + ([(lh, rl)] if rl is not None else []) + ([(ll, rh)] if ll is not None else [])
    for i, (lhsT, rhs) in enumerate(passes):
        last = nc.tensor.matmul(out, lhsT, rhs, start=start and i == 0, stop=stop and i == len(passes) - 1,
                                skip_group_check=cover)
    return last


class Core:
    pass


def high_part(k, out, raw):
    one = k.one[:]
    while len(one.shape) < len(raw.shape):
        one = one.unsqueeze(1)
    return k.nc.gpsimd.tensor_tensor(out, raw, one.to_broadcast(list(raw.shape)), ALU.mult)


def clear(nc, sems):
    with nc.Block() as block:
        @block.sync
        def _(sp):
            for s in sems:
                nc.sync.sem_clear(s)


HD0 = D // NH
NCH = D // P
HPC = NH // NCH
HALF = D // 2


def l0_self_attention(k, x_nat, xT, wq, bq, wk, bk, wv, bv, wo, bo, headmask, causal4):
    nc = k.nc
    UN = 6
    UB = UN * NCH
    units = [(c, v) for c in range(NCH) for v in range(UN)]

    with ExitStack() as ctx:
        def sb(name, shape, dt=F):
            return ctx.enter_context(nc.sbuf_tensor("a0_" + name, shape, dt))

        def sem(name):
            return ctx.enter_context(nc.semaphore("a0_" + name))

        wraw = sb("wraw", [P, KT, D])
        wqh, wql = sb("wqh", [P, KT, D], R), sb("wql", [P, KT, D], R)
        woh, wol = sb("woh", [P, KT, D], R), sb("wol", [P, KT, D], R)
        kvraw = sb("kvraw", [P, 2, KT, P])
        kvh, kvl = sb("kvh", [P, 2, KT, P], R), sb("kvl", [P, 2, KT, P], R)
        bias = sb("bias", [P, NCH + 2])
        bo_b = sb("bo_b", [P, D])
        hm = sb("hm", [P, HPC])
        caus_f, caus = sb("caus_f", [P, 4, P]), sb("caus", [P, 4, P], R)
        xraw = sb("xraw", [P, KT, S])
        xh, xl = sb("xh", [P, KT, S], R), sb("xl", [P, KT, S], R)
        kf, kfh, kfl = sb("kf", [P, S]), sb("kfh", [P, S], R), sb("kfl", [P, S], R)
        kdh, kdl = sb("kdh", [P, HPC, S], R), sb("kdl", [P, HPC, S], R)
        vf = sb("vf", [P, S])
        DIAG = P + HD0
        vdh, vdl = sb("vdh", [P, 2, HPC * DIAG], R), sb("vdl", [P, 2, HPC * DIAG], R)
        qh, ql = sb("qh", [P, 2, S], R), sb("ql", [P, 2, S], R)
        nmax, rsum, rinv = sb("nmax", [P, 4, 4]), sb("rsum", [P, 4, 4]), sb("rinv", [P, 4, 4])
        pb = sb("pb", [P, 4, 4, P])
        pth, ptl = sb("pth", [P, 2, 4, P], R), sb("ptl", [P, 2, 4, P], R)
        oh, ol = sb("oh", [P, NCH, S], R), sb("ol", [P, NCH, S], R)
        SB, TB, OB, XB = k.ps[0:3], k.ps[3:5], k.ps[5:7], k.ps[7]

        def head_view(t, kt):
            return t[:, kt, :].rearrange("p (j r) -> p j r", r=DIAG)[:, :, 0:HD0]

        names = ("cst wq_in wo_in kv_in xin w_split wraw_free kv_split xh_done xl_done zeroed x_ready kv_done kh_done kd_done "
                 "v_done vt_done vd_done q_ready q_hi q_lo s_ready max_done exp_done inv_done p_done t_ready "
                 "t_hi t_lo o_ready o_hi o_lo y_ready y_done s_link")
        m = namedtuple("Sems", names)(*map(sem, names.split()))

        def shape_of(v):
            return (4 * v, 4, 0, P) if v < 2 else (2 * (v - 2), 2, 1, S)

        ctx.callback(clear, nc, m)
        block = ctx.enter_context(nc.Block())

        @block.sync
        def _(sp):
            sp.dma_start(kvraw[:, 0], wk).then_inc(m.kv_in, 16)
            sp.dma_start(kvraw[:, 1], wv).then_inc(m.kv_in, 16)
            sp.dma_start(xraw[:], xT[:, :, 0:S]).then_inc(m.xin, 16)
            sp.dma_start(wraw[:], wq).then_inc(m.wq_in, 16)
            for dst, src in ((bias[:, 0:NCH], bq), (bias[:, NCH:NCH + 1], bk), (bias[:, NCH + 1:NCH + 2], bv),
                             (hm[:], headmask), (caus_f[:], causal4), (k.ident[:], k.ident_in),
                             (bo_b[:], bo.partition_broadcast(P)),
                             (k.x[:], x_nat.rearrange("(t p) d -> p t d", p=P))):
                sp.dma_start(dst, src).then_inc(m.cst, 16)
            sp.wait_ge(m.wraw_free, 1)
            sp.dma_start(wraw[:], wo).then_inc(m.wo_in, 16)
            with nc.sync.Fori(1, B) as b:
                sp.wait_ge(m.xl_done, b)
                sp.dma_start(xraw[:], xT[:, :, bass.ds(b * S, S)]).then_inc(m.xin, 16)

        @block.gpsimd
        def _(pool):
            nc.gpsimd.memset(f32(vdh[:]), 0.0).then_inc(m.zeroed, 1)
            nc.gpsimd.memset(f32(vdl[:]), 0.0).then_inc(m.zeroed, 1)
            pool.wait_ge(m.kv_in, 32)
            high_part(k, kvh[:], kvraw[:]).then_inc(m.s_link, 1)
            pool.wait_ge(m.s_link, 1)
            nc.gpsimd.tensor_tensor(kvl[:], kvraw[:], f32(kvh[:]), ALU.subtract).then_inc(m.kv_split, 1)
            with nc.gpsimd.Fori(0, B) as b:
                for u, (c, v) in enumerate(units):
                    j, n, qt, w = shape_of(v)
                    pool.wait_ge(m.inv_done, b * UB + u + 1)
                    pv = pb[:, u % 4].rearrange("p (n a) q -> p n (a q)", n=n)
                    nc.gpsimd.tensor_tensor(
                        pv, pv, rinv[:, u % 4, 0:n].unsqueeze(2).to_broadcast([P, n, w]), ALU.mult
                    ).then_inc(m.p_done, 1)

        @block.scalar
        def _(act):
            act.wait_ge(m.wq_in, 16)
            nc.scalar.activation(wqh[:], wraw[:], ACT.Copy).then_inc(m.w_split, 1)
            act.wait_ge(m.cst, 128)
            nc.scalar.activation(caus[:], caus_f[:], ACT.Copy).then_inc(m.w_split, 1)
            nc.scalar.activation(k.ident_r[:], k.ident[:], ACT.Copy).then_inc(m.w_split, 1)
            act.wait_ge(m.wo_in, 16)
            nc.scalar.activation(woh[:], wraw[:], ACT.Copy).then_inc(m.w_split, 1)
            with nc.scalar.Fori(0, B) as b:
                act.wait_ge(m.xin, (b + 1) * 16)
                act.wait_ge(m.y_done, b * 2 + 1)
                nc.scalar.activation(xh[:], xraw[:], ACT.Copy).then_inc(m.xh_done, 1)
                act.wait_ge(m.kd_done, b * 3 + 1)
                nc.scalar.activation(kfh[:], kf[:], ACT.Copy).then_inc(m.kh_done, 1)
                act.wait_ge(m.vt_done, b + 1)
                act.wait_ge(m.zeroed, 2)
                for kt in range(2):
                    nc.scalar.activation(head_view(vdh, kt), XB[:, kt * P:(kt + 1) * P].rearrange(
                        "p (j r) -> p j r", r=HD0), ACT.Copy).then_inc(m.v_done, 1)

                def query(c):
                    act.wait_ge(m.q_ready, b * NCH + c + 1)
                    nc.scalar.activation(qh[:, c % 2], XB[:, 0:S], ACT.Identity, bias=bias[:, c:c + 1]).then_inc(
                        m.q_hi, 1)

                def transposed(u):
                    act.wait_ge(m.t_ready, b * UB + u + 1)
                    if u >= 2:
                        act.wait_ge(m.o_ready, b * UB + u - 1)
                    nc.scalar.activation(pth[:, u % 2], TB[u % 2][:].rearrange("p (n q) -> p n q", q=P),
                                         ACT.Copy).then_inc(m.t_hi, 1)

                def attended(c):
                    act.wait_ge(m.o_ready, b * UB + UN * (c + 1))
                    nc.scalar.activation(oh[:, c], OB[c % 2][:, 0:S], ACT.Copy).then_inc(m.o_hi, 1)

                query(0)
                for u in range(UB + 3):
                    if u < UB:
                        c, v = units[u]
                        j, n, qt, w = shape_of(v)
                        if v == 0 and c + 1 < NCH:
                            query(c + 1)
                        act.wait_ge(m.max_done, b * UB + u + 1)
                        if u >= 4:
                            act.wait_ge(m.t_ready, b * UB + u - 3)
                        for i in range(n):
                            pv = pb[:, u % 4].rearrange("p (n a) q -> p n (a q)", n=n)
                            last = nc.scalar.activation(
                                pv[:, i], SB[u % 3][:, i * w:(i + 1) * w], ACT.Exp, bias=nmax[:, u % 4, i:i + 1],
                                accum_out=rsum[:, u % 4, i:i + 1])
                        last.then_inc(m.exp_done, 1)
                    if 2 <= u < UB + 2:
                        transposed(u - 2)
                    if u >= 3 and (u - 3) % UN == UN - 1:
                        attended((u - 3) // UN)

        @block.vector
        def _(dve):
            nc.vector.memset(rsum[:], 1.0).then_inc(m.y_done, 1)
            dve.wait_ge(m.w_split, 1)
            nc.vector.tensor_tensor(wql[:], wraw[:], f32(wqh[:]), ALU.subtract).then_inc(m.wraw_free, 1)
            dve.wait_ge(m.cst, 128)
            dve.wait_ge(m.w_split, 4)
            nc.vector.tensor_tensor(wol[:], wraw[:], f32(woh[:]), ALU.subtract).then_inc(m.wraw_free, 1)
            with nc.vector.Fori(0, B) as b:
                dve.wait_ge(m.xh_done, b + 1)
                nc.vector.tensor_tensor(xl[:], xraw[:], f32(xh[:]), ALU.subtract).then_inc(m.xl_done, 1)
                dve.wait_ge(m.kv_done, b + 1)
                nc.vector.tensor_scalar(kf[:], XB[:, 0:S], bias[:, NCH:NCH + 1], HD0 ** -0.5, ALU.add,
                                        ALU.mult).then_inc(m.kd_done, 1)
                nc.vector.tensor_scalar(vf[:], XB[:, S:2 * S], bias[:, NCH + 1:NCH + 2], None,
                                        ALU.add).then_inc(m.x_ready, 1)
                dve.wait_ge(m.kh_done, b + 1)
                nc.vector.tensor_tensor(kfl[:], kf[:], f32(kfh[:]), ALU.subtract).then_inc(m.kd_done, 1)
                dve.wait_ge(m.kd_done, b * 3 + 2)
                for j in range(HPC):
                    nc.vector.tensor_scalar(kdh[:, j], f32(kfh[:]), hm[:, j:j + 1], None, ALU.mult)
                    last = nc.vector.tensor_scalar(kdl[:, j], f32(kfl[:]), hm[:, j:j + 1], None, ALU.mult)
                last.then_inc(m.kd_done, 1)
                dve.wait_ge(m.v_done, b * 2 + 2)
                for kt in range(2):
                    last = nc.vector.tensor_tensor(head_view(vdl, kt), XB[:, kt * P:(kt + 1) * P].rearrange(
                        "p (j r) -> p j r", r=HD0), f32(head_view(vdh, kt)), ALU.subtract)
                last.then_inc(m.vd_done, 1)

                def query(c):
                    dve.wait_ge(m.q_hi, b * NCH + c + 1)
                    nc.vector.scalar_tensor_tensor(ql[:, c % 2], XB[:, 0:S], bias[:, c:c + 1], f32(qh[:, c % 2]),
                                                   ALU.add, ALU.subtract).then_inc(m.q_lo, 1)

                def inverse(u):
                    n = shape_of(units[u][1])[1]
                    dve.wait_ge(m.exp_done, b * UB + u + 1)
                    nc.vector.reciprocal(rinv[:, u % 4, 0:n], rsum[:, u % 4, 0:n]).then_inc(m.inv_done, 1)

                query(0)
                for u in range(UB + 3):
                    if u < UB:
                        c, v = units[u]
                        j, n, qt, w = shape_of(v)
                        if v == 0 and c + 1 < NCH:
                            query(c + 1)
                        dve.wait_ge(m.s_ready, b * UB + u + 1)
                        nc.vector.tensor_reduce(nmax[:, u % 4, 0:n], SB[u % 3][:].rearrange("p (n w) -> p n w", n=n),
                                                AX.X, ALU.max, negate=True).then_inc(m.max_done, 1)
                    if 1 <= u < UB + 1:
                        inverse(u - 1)
                    if 2 <= u < UB + 2:
                        dve.wait_ge(m.t_hi, b * UB + u - 1)
                        nc.vector.tensor_tensor(ptl[:, u % 2], TB[u % 2][:].rearrange("p (n q) -> p n q", q=P),
                                                f32(pth[:, u % 2]), ALU.subtract).then_inc(m.t_lo, 1)
                    if u >= 3 and (u - 3) % UN == UN - 1:
                        c = (u - 3) // UN
                        dve.wait_ge(m.o_hi, b * NCH + c + 1)
                        nc.vector.tensor_tensor(ol[:, c], OB[c % 2][:, 0:S], f32(oh[:, c]),
                                                ALU.subtract).then_inc(m.o_lo, 1)
                for t in range(2):
                    dve.wait_ge(m.y_ready, b * 2 + t + 1)
                    nc.vector.tensor_tensor(k.acc[:, bass.ds(b * 2 + t, 1), :], (SB[0], SB[1])[t][:].unsqueeze(1),
                                            bo_b[:].unsqueeze(1), ALU.add).then_inc(m.y_done, 1)

        @block.tensor
        def _(pe):
            pe.wait_ge(m.kv_split, 1)
            pe.wait_ge(m.w_split, 4)
            pe.wait_ge(m.wraw_free, 2)
            pe.wait_ge(m.zeroed, 2)
            with nc.tensor.Fori(0, B) as b:
                pe.wait_ge(m.xl_done, b + 1)
                for i in range(2):
                    last = products(nc, XB[:, i * S:(i + 1) * S],
                                    [(kvh[:, i, kt], kvl[:, i, kt], xh[:, kt], xl[:, kt]) for kt in range(KT)])
                last.then_inc(m.kv_done, 1)
                pe.wait_ge(m.x_ready, b + 1)
                for kt in range(2):
                    last = nc.tensor.transpose(XB[:, kt * P:(kt + 1) * P], vf[:, kt * P:(kt + 1) * P], k.ident[:])
                last.then_inc(m.vt_done, 1)
                pe.wait_ge(m.vd_done, b + 1)

                def query(c):
                    if c:
                        pe.wait_ge(m.q_lo, b * NCH + c)
                    products(nc, XB[:, 0:S], [(wqh[:, kt, c * P:(c + 1) * P], wql[:, kt, c * P:(c + 1) * P],
                                               xh[:, kt], xl[:, kt]) for kt in range(KT)]).then_inc(m.q_ready, 1)

                def scores(u):
                    c, v = units[u]
                    j, n, qt, w = shape_of(v)
                    if v == 0:
                        pe.wait_ge(m.q_lo, b * NCH + c + 1)
                    if u >= 3:
                        pe.wait_ge(m.exp_done, b * UB + u - 2)
                    ql_, qh_ = ql[:, c % 2, qt * P:(qt + 1) * P], qh[:, c % 2, qt * P:(qt + 1) * P]
                    out = SB[u % 3][:].rearrange("p (n w) -> p n w", n=n)
                    products(nc, out, [(qh_, ql_, kdh[:, j:j + n, 0:w], kdl[:, j:j + n, 0:w])])
                    nc.tensor.matmul(out[:, :, w - P:w], k.ident_r[:], caus[:, 0:n], start=False,
                                     stop=True, skip_group_check=True).then_inc(m.s_ready, 1)

                def transpose(u):
                    pe.wait_ge(m.p_done, b * UB + u + 1)
                    if u >= 2:
                        pe.wait_ge(m.t_lo, b * UB + u - 1)
                    for i in range(4):
                        last = nc.tensor.transpose(TB[u % 2][:, i * P:(i + 1) * P], pb[:, u % 4, i], k.ident[:])
                    last.then_inc(m.t_ready, 1)

                def attend(u):
                    c, v = units[u]
                    j, n, qt, w = shape_of(v)
                    pe.wait_ge(m.t_lo, b * UB + u + 1)
                    if v == 0 and c >= 2:
                        pe.wait_ge(m.o_lo, b * NCH + c - 1)
                    out = OB[c % 2][:, qt * P:(qt + 1) * P]
                    for i in range(n):
                        for kt in range(w // P):
                            at = i * (w // P) + kt
                            vj = slice((j + i) * P, (j + i + 1) * P)
                            last = products(nc, out, [(vdh[:, kt, vj], vdl[:, kt, vj], pth[:, u % 2, at],
                                                       ptl[:, u % 2, at])], start=v == 0 and i == 0,
                                            stop=v in (1, UN - 1) and i == n - 1 and kt == w // P - 1, cover=True)
                    last.then_inc(m.o_ready, 1)

                query(0)
                pe.wait_ge(m.kd_done, b * 3 + 3)
                for u in range(UB + 3):
                    if u < UB:
                        scores(u)
                        if units[u][1] == 0 and units[u][0] + 1 < NCH:
                            query(units[u][0] + 1)
                    if 2 <= u < UB + 2:
                        transpose(u - 2)
                    if u >= 3:
                        attend(u - 3)
                pe.wait_ge(m.o_lo, b * NCH + NCH)
                for t in range(2):
                    pe.wait_ge(m.exp_done, b * UB + UB)
                    products(nc, (SB[0], SB[1])[t][:], [(oh[:, c, t * P:(t + 1) * P], ol[:, c, t * P:(t + 1) * P],
                                                         woh[:, c], wol[:, c]) for c in range(NCH)]).then_inc(
                        m.y_ready, 1)
                pe.wait_ge(m.y_done, b * 2 + 3)


def norm_stage(k, tag, keep_T=True, out=None):
    nc = k.nc
    TB = k.ps[0:4]
    with ExitStack() as ctx:
        def sb(name, shape, dt=F):
            return ctx.enter_context(nc.sbuf_tensor(f"{tag}_{name}", shape, dt))

        def sem(name):
            return ctx.enter_context(nc.semaphore(f"{tag}_{name}"))

        r_sum, stats, mv = sb("r_sum", [P, 2, D]), sb("stats", [P, 2, 6]), sb("mv", [P, 2, 2])
        ve, rs = sb("ve", [P, 2]), sb("rs", [P, 2])
        names = "link var rstd r_used tr hi lo stored"
        m = namedtuple("Sems", names)(*map(sem, names.split()))
        ctx.callback(clear, nc, m)
        block = ctx.enter_context(nc.Block())

        def low(dve, t):
            dve.wait_ge(m.hi, t + 1)
            nc.vector.tensor_tensor(k.xl[:, :, t * P:(t + 1) * P], TB[t % 4][:].rearrange("p (c q) -> p c q", c=KT),
                                    f32(k.xh[:, :, t * P:(t + 1) * P]), ALU.subtract).then_inc(m.lo, 1)

        @block.vector
        def _(dve):
            for t in range(NT):
                if t >= 2:
                    dve.wait_ge(m.r_used, t - 1)
                nc.vector.tensor_tensor(r_sum[:, t % 2], k.x[:, t], k.acc[:, t], ALU.add).then_inc(m.link, 1)
                dve.wait_ge(m.link, 3 * t + 1)
                nc.vector.bn_stats(stats[:, t % 2], r_sum[:, t % 2]).then_inc(m.link, 1)
                dve.wait_ge(m.link, 3 * t + 2)
                nc.vector.bn_aggr(mv[:, t % 2], stats[:, t % 2]).then_inc(m.link, 1)
                dve.wait_ge(m.link, 3 * t + 3)
                nc.vector.tensor_scalar(ve[:, t % 2:t % 2 + 1], mv[:, t % 2, 1:2], EPS, None,
                                        ALU.add).then_inc(m.var, 1)
                dve.wait_ge(m.rstd, t + 1)
                nc.vector.tensor_scalar(k.x[:, t], r_sum[:, t % 2], mv[:, t % 2, 0:1], rs[:, t % 2:t % 2 + 1],
                                        ALU.subtract, ALU.mult).then_inc(m.r_used, 1)
                if keep_T and t >= 1:
                    low(dve, t - 1)
            if keep_T:
                low(dve, NT - 1)

        @block.gpsimd
        def _(pool):
            for t in range(NT):
                pool.wait_ge(m.var, t + 1)
                nc.gpsimd.tensor_tensor(rs[:, t % 2:t % 2 + 1], ve[:, t % 2:t % 2 + 1], k.half[:],
                                        ALU.pow).then_inc(m.rstd, 1)

        if keep_T:
            @block.tensor
            def _(pe):
                for t in range(NT):
                    pe.wait_ge(m.r_used, t + 1)
                    if t >= 4:
                        pe.wait_ge(m.lo, t - 3)
                    for c in range(KT):
                        last = nc.tensor.transpose(TB[t % 4][:, c * P:(c + 1) * P], k.x[:, t, c * P:(c + 1) * P],
                                                   k.ident[:])
                    last.then_inc(m.tr, 1)

            @block.scalar
            def _(act):
                for t in range(NT):
                    act.wait_ge(m.tr, t + 1)
                    nc.scalar.activation(k.xh[:, :, t * P:(t + 1) * P], TB[t % 4][:].rearrange(
                        "p (c q) -> p c q", c=KT), ACT.Copy).then_inc(m.hi, 1)
        else:
            @block.sync
            def _(sp):
                for t in range(NT):
                    sp.wait_ge(m.r_used, t + 1)
                    sp.dma_start(out[t * P:(t + 1) * P, :], k.x[:, t]).then_inc(m.stored, 16)
                sp.wait_ge(m.stored, 16 * NT)


X0_GROUPS = 8
X0_PER = NH // X0_GROUPS


def l0_cross_keys(k, st, ctx_dup, ctxT, wk, q_norm, k_norm):
    nc = k.nc
    with ExitStack() as ctx:
        def sb(name, shape, dt=F):
            return ctx.enter_context(nc.sbuf_tensor("xk_" + name, shape, dt))

        def sem(name):
            return ctx.enter_context(nc.semaphore("xk_" + name))

        W = X0_GROUPS * HD
        craw = sb("craw", [P, KT, B, P])
        oraw, och, ocl = sb("oraw", [P, KT, B * CTX]), sb("och", [P, KT, B * CTX], R), sb("ocl", [P, KT, B * CTX], R)
        wraw = sb("wraw", [P, KT, W])
        wh, wl = sb("wh", [P, KT, W], R), sb("wl", [P, KT, W], R)
        sq, kn = sb("sq", [P, 4, 4, HD]), sb("kn", [P, 4, 4, HD])
        ss, rk = sb("ss", [P, 4, 4]), sb("rk", [P, 4, 4])
        norms, w = sb("norms", [P, 2]), sb("w", [P, 1])
        names = "w_in c_in wh_done split sq_done ss_done rk_done w_done k_ready kn_done t_ready hi lo link"
        m = namedtuple("Sems", names)(*map(sem, names.split()))
        ctx.callback(clear, nc, m)
        block = ctx.enter_context(nc.Block())

        @block.sync
        def _(sp):
            sp.dma_start(craw[:], ctx_dup).then_inc(m.c_in, 16)
            sp.dma_start(oraw[:], ctxT).then_inc(m.c_in, 16)
            sp.dma_start(norms[:, 0:1], q_norm).then_inc(m.c_in, 16)
            sp.dma_start(norms[:, 1:2], k_norm).then_inc(m.c_in, 16)
            sp.dma_start(wraw[:], wk).then_inc(m.w_in, 16)

        @block.scalar
        def _(act):
            act.wait_ge(m.c_in, 64)
            nc.scalar.activation(st.ch[:], craw[:], ACT.Copy)
            nc.scalar.activation(och[:], oraw[:], ACT.Copy).then_inc(m.wh_done, 1)
            act.wait_ge(m.w_in, 16)
            nc.scalar.activation(wh[:], wraw[:], ACT.Copy).then_inc(m.wh_done, 1)
            for i in range(4):
                act.wait_ge(m.k_ready, i + 1)
                nc.scalar.activation(sq[:, i], k.ps[i][:].rearrange("p (g d) -> p g d", d=HD),
                                     ACT.Square).then_inc(m.sq_done, 1)
            act.wait_ge(m.w_done, 1)
            for i in range(4):
                act.wait_ge(m.t_ready, i + 1)
                nc.scalar.activation(st.kh[:, 2 * i:2 * i + 2], k.ps[4 + i][:].rearrange("p (g n) -> p g n", g=2),
                                     ACT.Copy, scale=w[:]).then_inc(m.hi, 1)

        @block.gpsimd
        def _(pool):
            pool.wait_ge(m.ss_done, 1)
            nc.gpsimd.tensor_tensor(rk[:], ss[:], k.half[:].unsqueeze(2).to_broadcast([P, 4, 4]), ALU.pow).then_inc(
                m.rk_done, 1)

        @block.vector
        def _(dve):
            dve.wait_ge(m.c_in, 64)
            nc.vector.tensor_scalar(w[:], norms[:, 0:1], norms[:, 1:2], HD ** -0.5, ALU.mult, ALU.mult).then_inc(
                m.w_done, 1)
            dve.wait_ge(m.wh_done, 1)
            nc.vector.tensor_tensor(st.cl[:], craw[:], f32(st.ch[:]), ALU.subtract)
            nc.vector.tensor_tensor(ocl[:], oraw[:], f32(och[:]), ALU.subtract)
            dve.wait_ge(m.wh_done, 2)
            nc.vector.tensor_tensor(wl[:], wraw[:], f32(wh[:]), ALU.subtract).then_inc(m.split, 1)
            for i in range(4):
                dve.wait_ge(m.sq_done, i + 1)
                last = nc.vector.tensor_reduce(ss[:, i], sq[:, i], AX.X, ALU.add)
            last.then_inc(m.link, 1)
            dve.wait_ge(m.link, 1)
            nc.vector.tensor_scalar(ss[:], ss[:], 1.0 / HD, EPS, ALU.mult, ALU.add).then_inc(m.ss_done, 1)
            dve.wait_ge(m.rk_done, 1)
            for i in range(4):
                nc.vector.tensor_tensor(kn[:, i], k.ps[i][:].rearrange("p (g d) -> p g d", d=HD),
                                        rk[:, i].unsqueeze(2).to_broadcast([P, 4, HD]), ALU.mult).then_inc(
                    m.kn_done, 1)
            for i in range(4):
                dve.wait_ge(m.hi, i + 1)
                last = nc.vector.scalar_tensor_tensor(st.kl[:, 2 * i:2 * i + 2],
                                               k.ps[4 + i][:].rearrange("p (g n) -> p g n", g=2), w[:],
                                               f32(st.kh[:, 2 * i:2 * i + 2]), ALU.mult, ALU.subtract)
            last.then_inc(m.lo, 1)

        @block.tensor
        def _(pe):
            pe.wait_ge(m.split, 1)
            for i in range(4):
                pair, half = divmod(i, 2)
                rows = slice(pair * P, (pair + 1) * P)
                cols = slice(half * 512, (half + 1) * 512)
                products(nc, k.ps[i][:], [(och[:, kt, rows], ocl[:, kt, rows], wh[:, kt, cols], wl[:, kt, cols]) for kt in range(KT)]).then_inc(m.k_ready, 1)
            pe.wait_ge(m.kn_done, 4)
            for i in range(4):
                for j in range(2):
                    g = 2 * i + j
                    for pair in range(2):
                        last = nc.tensor.transpose(k.ps[4 + i][:, (2 * j + pair) * P:(2 * j + pair + 1) * P],
                                                   kn[:, 2 * pair + g // 4, g % 4], k.ident[:])
                last.then_inc(m.t_ready, 1)


def l0_cross_attention(k, ctx_dup, ctxT, wk, wq, wv, wo, q_norm, k_norm, mask):
    nc = k.nc
    with ExitStack() as ctx:
        def sb(name, shape, dt=F):
            return ctx.enter_context(nc.sbuf_tensor("x0_" + name, shape, dt))

        def sem(name):
            return ctx.enter_context(nc.semaphore("x0_" + name))

        st = namedtuple("Context", "ch cl kh kl")(ch=sb("ch", [P, KT, B, P], R), cl=sb("cl", [P, KT, B, P], R),
                             kh=sb("kh", [P, X0_GROUPS, B * CTX], R), kl=sb("kl", [P, X0_GROUPS, B * CTX], R))
        l0_cross_keys(k, st, ctx_dup, ctxT, wk, q_norm, k_norm)

        wqraw, woraw, wvraw = sb("wqraw", [P, KT, HD]), sb("woraw", [P, D]), sb("wvraw", [P, KT, HD])
        wqh, wql = sb("wqh", [P, 2, KT, HD], R), sb("wql", [P, 2, KT, HD], R)
        wvh, wvl = sb("wvh", [P, KT, HD], R), sb("wvl", [P, KT, HD], R)
        woh, wol = sb("woh", [P, X0_PER, D], R), sb("wol", [P, X0_PER, D], R)
        vh, vl = sb("vh", [P, B, HD], R), sb("vl", [P, B, HD], R)
        qh, ql = sb("qh", [P, 2, TOK], R), sb("ql", [P, 2, TOK], R)
        q2 = sb("q2", [P, TOK])
        ones = sb("ones", [P, 1])
        qv, rq = sb("qv", [P, NT]), sb("rq", [P, NT])
        mask_sb = sb("mask", [P, 2, CTX])
        pb = sb("pb", [P, NT, 2, CTX])
        mx, sm, rs = sb("mx", [P, NT]), sb("sm", [P, NT]), sb("rs", [P, NT])
        pth, ptl = sb("pth", [P, 2, 512], R), sb("ptl", [P, 2, 512], R)
        oh, ol = sb("oh", [P, X0_PER, TOK], R), sb("ol", [P, X0_PER, TOK], R)
        QB, SB, OB, XB, TB = k.ps[0:2], k.ps[2:4], k.ps[4:6], k.ps[6], k.ps[7]

        names = ("wq_in wo_in wv_in cst wq_hi wv_split wq_split wo_split q_ready q_hi sq q_lo n_ready n_out rq_done "
                 "s_ready scaled masked shifted exp_done sums inv_done p_done v_ready v_hi v_lo t_ready t_hi t_lo "
                 "o_ready o_hi o_lo y_ready y_done link reduced")
        m = namedtuple("Sems", names)(*map(sem, names.split()))
        TBK = (TB, XB)
        ctx.callback(clear, nc, m)
        block = ctx.enter_context(nc.Block())

        def wide(ap):
            return ap.unsqueeze(2).to_broadcast([P, NT, CTX])

        @block.sync
        def _(sp):
            sp.dma_start(wqraw[:], wq[0]).then_inc(m.wq_in, 16)
            sp.dma_start(wvraw[:], wv[0]).then_inc(m.wv_in, 16)
            sp.dma_start(mask_sb[:], mask.rearrange("(t p) n -> p t n", p=P)).then_inc(m.cst, 16)
            sp.wait_ge(m.wq_split, 1)
            sp.dma_start(wqraw[:], wq[1]).then_inc(m.wq_in, 16)
            with nc.sync.Fori(0, X0_GROUPS) as g:
                sp.wait_ge(m.wv_split, g + 1)
                sp.dma_start(wvraw[:], wv[bass.ds(g + 1, 1)].rearrange("a p k n -> (a p) k n")).then_inc(
                    m.wv_in, 16)
                for i in range(X0_PER):
                    h = g * X0_PER + i
                    sp.wait_ge(m.wo_split, h + 1)
                    sp.dma_start(woraw[:], wo[bass.ds(h, 1)].rearrange("a p n -> (a p) n")).then_inc(
                        m.wo_in, 16)
                    sp.wait_ge(m.wq_split, h + 2)
                    sp.dma_start(wqraw[:], wq[bass.ds(h + 2, 1)].rearrange("a p k n -> (a p) k n")).then_inc(
                        m.wq_in, 16)

        @block.gpsimd
        def _(pool):
            nc.gpsimd.memset(k.acc[:], 0.0).then_inc(m.wo_split, 1)
            pool.wait_ge(m.wv_in, 16)
            high_part(k, wvh[:], wvraw[:]).then_inc(m.link, 1)
            pool.wait_ge(m.link, 1)
            nc.gpsimd.tensor_tensor(wvl[:], wvraw[:], f32(wvh[:]), ALU.subtract).then_inc(m.wv_split, 1)
            pool.wait_ge(m.cst, 16)

            def inverse_root(H):
                pool.wait_ge(m.n_out, H + 1)
                nc.gpsimd.tensor_tensor(rq[:], qv[:], k.half[:].to_broadcast([P, NT]), ALU.pow).then_inc(
                    m.rq_done, 1)

            inverse_root(0)
            with nc.gpsimd.Fori(0, X0_GROUPS) as g:
                for h in range(X0_PER):
                    H = g * X0_PER + h
                    pool.wait_ge(m.scaled, H + 1)
                    pv = pb[:, :, h % 2].rearrange("p (b q) n -> p q b n", q=2)
                    for q in range(2):
                        last = nc.gpsimd.tensor_tensor(pv[:, q], pv[:, q], mask_sb[:, q:q + 1].to_broadcast(
                            [P, B, CTX]), ALU.add)
                    last.then_inc(m.masked, 1)
                    pool.wait_ge(m.wq_in, 16 * H + 48)
                    pool.wait_ge(m.q_ready, 2 * H + 2)
                    high_part(k, wqh[:, h % 2], wqraw[:]).then_inc(m.link, 1)
                    pool.wait_ge(m.inv_done, H + 1)
                    nc.gpsimd.tensor_tensor(pb[:, :, h % 2], pb[:, :, h % 2], wide(rs[:]), ALU.mult).then_inc(
                        m.p_done, 1)
                    inverse_root(H + 1)
                    pool.wait_ge(m.link, 2 * H + g + 2)
                    nc.gpsimd.tensor_tensor(wql[:, h % 2], wqraw[:], f32(wqh[:, h % 2]), ALU.subtract).then_inc(
                        m.wq_split, 1)
                    pool.wait_ge(m.wo_in, 16 * H + 16)
                    high_part(k, woh[:, h], woraw[:]).then_inc(m.link, 1)
                    pool.wait_ge(m.link, 2 * H + g + 3)
                    nc.gpsimd.tensor_tensor(wol[:, h], woraw[:], f32(woh[:, h]), ALU.subtract).then_inc(
                        m.wo_split, 1)
                pool.wait_ge(m.wv_in, 16 * g + 32)
                pool.wait_ge(m.v_ready, g + 1)
                high_part(k, wvh[:], wvraw[:]).then_inc(m.link, 1)
                pool.wait_ge(m.link, 2 * X0_PER * (g + 1) + g + 2)
                nc.gpsimd.tensor_tensor(wvl[:], wvraw[:], f32(wvh[:]), ALU.subtract).then_inc(
                    m.wv_split, 1)

        @block.scalar
        def _(act):
            for i in range(2):
                act.wait_ge(m.wq_in, 16 * (i + 1))
                nc.scalar.activation(wqh[:, i], wqraw[:], ACT.Copy).then_inc(m.wq_hi, 1)

            def query(H, par):
                for i in range(2):
                    cols = slice(i * 512, (i + 1) * 512)
                    act.wait_ge(m.q_ready, 2 * H + i + 1)
                    nc.scalar.activation(qh[:, par, cols], QB[i][:], ACT.Copy).then_inc(m.q_hi, 1)
                    nc.scalar.activation(q2[:, cols], QB[i][:], ACT.Square).then_inc(m.sq, 1)

            query(0, 0)
            with nc.scalar.Fori(0, X0_GROUPS) as g:
                for h in range(X0_PER):
                    H = g * X0_PER + h
                    query(H + 1, (h + 1) % 2)
                    act.wait_ge(m.shifted, H + 1)
                    nc.scalar.activation(pb[:, :, h % 2], pb[:, :, h % 2], ACT.Exp).then_inc(m.exp_done, 1)
                    if h == 1:
                        act.wait_ge(m.v_ready, g + 1)
                        nc.scalar.activation(vh[:], XB[:].rearrange("p (b d) -> p b d", b=B), ACT.Copy).then_inc(
                            m.v_hi, 1)
                    if h % 2:
                        A = g * 2 + h // 2
                        for i in range(2):
                            act.wait_ge(m.t_ready, 2 * A + i + 1)
                            nc.scalar.activation(pth[:, i], TBK[i][:], ACT.Copy).then_inc(m.t_hi, 1)
                        for i in range(2):
                            for par in range(2):
                                act.wait_ge(m.o_ready, 4 * A + 2 * i + par + 1)
                                nc.scalar.activation(oh[:, h - 1 + par, i * 512:(i + 1) * 512], OB[par][:],
                                                     ACT.Copy).then_inc(m.o_hi, 1)

        @block.vector
        def _(dve):
            nc.vector.memset(ones[:], 1.0).then_inc(m.y_done, 1)
            for i in range(2):
                dve.wait_ge(m.wq_hi, i + 1)
                nc.vector.tensor_tensor(wql[:, i], wqraw[:], f32(wqh[:, i]), ALU.subtract).then_inc(
                    m.wq_split, 1)

            def query(H, i, par):
                cols = slice(i * 512, (i + 1) * 512)
                dve.wait_ge(m.sq, 2 * H + i + 1)
                nc.vector.tensor_tensor(ql[:, par, cols], QB[i][:], f32(qh[:, par, cols]), ALU.subtract).then_inc(
                    m.q_lo, 1)

            def variance(H):
                dve.wait_ge(m.n_ready, H + 1)
                nc.vector.tensor_scalar(qv[:], XB[:, 0:NT], 1.0 / HD, EPS, ALU.mult, ALU.add).then_inc(
                    m.n_out, 1)

            def project(g, pair):
                for t in range(NT):
                    dve.wait_ge(m.y_ready, (g * 2 + pair) * NT + t + 1)
                    nc.vector.tensor_tensor(k.acc[:, t], OB[t % 2][:], k.acc[:, t], ALU.add).then_inc(
                        m.y_done, 1)

            query(0, 0, 0)
            query(0, 1, 0)
            variance(0)
            with nc.vector.Fori(0, X0_GROUPS) as g:
                for h in range(X0_PER):
                    H = g * X0_PER + h
                    pv = pb[:, :, h % 2]
                    dve.wait_ge(m.s_ready, H + 1)
                    dve.wait_ge(m.rq_done, H + 1)
                    nc.vector.tensor_tensor(pv, SB[h % 2][:].rearrange("p (t n) -> p t n", t=NT), wide(rq[:]),
                                            ALU.mult).then_inc(m.scaled, 1)
                    query(H + 1, 0, (h + 1) % 2)
                    dve.wait_ge(m.masked, H + 1)
                    nc.vector.tensor_reduce(mx[:], pv, AX.X, ALU.max).then_inc(m.reduced, 1)
                    dve.wait_ge(m.reduced, 2 * H + 1)
                    nc.vector.tensor_tensor(pv, pv, wide(mx[:]), ALU.subtract).then_inc(m.shifted, 1)
                    query(H + 1, 1, (h + 1) % 2)
                    dve.wait_ge(m.exp_done, H + 1)
                    nc.vector.tensor_reduce(sm[:], pv, AX.X, ALU.add).then_inc(m.reduced, 1)
                    dve.wait_ge(m.reduced, 2 * H + 2)
                    nc.vector.reciprocal(rs[:], sm[:]).then_inc(m.inv_done, 1)
                    variance(H + 1)
                    if h == 1:
                        dve.wait_ge(m.v_hi, g + 1)
                        nc.vector.tensor_tensor(vl[:], XB[:].rearrange("p (b d) -> p b d", b=B), f32(vh[:]),
                                                ALU.subtract).then_inc(m.v_lo, 1)
                    if h == 3:
                        project(g, 0)
                    if h % 2:
                        A = g * 2 + h // 2
                        for i in range(2):
                            dve.wait_ge(m.t_hi, 2 * A + i + 1)
                            nc.vector.tensor_tensor(ptl[:, i], TBK[i][:], f32(pth[:, i]), ALU.subtract).then_inc(
                                m.t_lo, 1)
                        for i in range(2):
                            for par in range(2):
                                dve.wait_ge(m.o_hi, 4 * A + 2 * i + par + 1)
                                cols = slice(i * 512, (i + 1) * 512)
                                nc.vector.tensor_tensor(ol[:, h - 1 + par, cols], OB[par][:],
                                                        f32(oh[:, h - 1 + par, cols]), ALU.subtract).then_inc(
                                    m.o_lo, 1)
                project(g, 1)

        @block.tensor
        def _(pe):
            def query(H, i, par):
                cols = slice(i * 512, (i + 1) * 512)
                pe.wait_ge(m.wq_split, H + 1)
                products(nc, QB[i][:], [(wqh[:, par, kt], wql[:, par, kt], k.xh[:, kt, cols], k.xl[:, kt, cols])
                                        for kt in range(KT)]).then_inc(m.q_ready, 1)

            def project(g, pair):
                A = g * 2 + pair
                pe.wait_ge(m.wo_split, g * X0_PER + 2 * pair + 3)
                pe.wait_ge(m.o_lo, 4 * A + 4)
                for t in range(NT):
                    if t >= 2:
                        pe.wait_ge(m.y_done, NT * A + t)
                    tok = slice(t * P, (t + 1) * P)
                    products(nc, OB[t % 2][:], [(oh[:, h, tok], ol[:, h, tok], woh[:, h], wol[:, h])
                                                for h in range(2 * pair, 2 * pair + 2)]).then_inc(m.y_ready, 1)

            def squares(H):
                pe.wait_ge(m.sq, 2 * H + 2)
                for t in range(NT):
                    last = nc.tensor.matmul(XB[:, t:t + 1], q2[:, t * P:(t + 1) * P], ones[:], start=True, stop=True)
                last.then_inc(m.n_ready, 1)

            query(0, 0, 0)
            query(0, 1, 0)
            pe.wait_ge(m.y_done, 1)
            squares(0)
            with nc.tensor.Fori(0, X0_GROUPS) as g:
                for h in range(X0_PER):
                    H = g * X0_PER + h
                    pair = h // 2
                    A = g * 2 + pair
                    pe.wait_ge(m.q_lo, 2 * H + 2)
                    if h >= 2:
                        pe.wait_ge(m.scaled, H - 1)
                    for t in range(NT):
                        tok = slice(t * P, (t + 1) * P)
                        keys = slice(t // 2 * CTX, (t // 2 + 1) * CTX)
                        last = products(nc, SB[h % 2][:, t * CTX:(t + 1) * CTX],
                                        [(qh[:, h % 2, tok], ql[:, h % 2, tok], st.kh[:, bass.ds(g, 1), keys].rearrange(
                                            "p a n -> p (a n)"), st.kl[:, bass.ds(g, 1), keys].rearrange(
                                            "p a n -> p (a n)"))])
                    last.then_inc(m.s_ready, 1)
                    query(H + 1, 0, (h + 1) % 2)
                    query(H + 1, 1, (h + 1) % 2)
                    if h % 2 == 0:
                        pe.wait_ge(m.n_out, H + 1)
                        squares(H + 1)
                        continue
                    pe.wait_ge(m.n_out, H + 1)
                    squares(H + 1)
                    if pair == 0:
                        pe.wait_ge(m.wv_split, g + 1)
                        pe.wait_ge(m.n_out, H + 2)
                        for b in range(B):
                            last = products(nc, XB[:, b * HD:(b + 1) * HD],
                                            [(st.ch[:, kt, b], st.cl[:, kt, b], wvh[:, kt], wvl[:, kt])
                                             for kt in range(KT)])
                        last.then_inc(m.v_ready, 1)
                        pe.wait_ge(m.v_lo, g + 1)
                    else:
                        project(g, 0)
                    pe.wait_ge(m.p_done, H + 1)
                    pe.wait_ge(m.n_out, H + 2)
                    for i in range(2):
                        for t in range(4):
                            last = nc.tensor.transpose(TBK[i][:, t * P:(t + 1) * P], pb[:, 4 * i + t].rearrange(
                                "p h n -> p (h n)"), k.ident[:])
                        last.then_inc(m.t_ready, 1)
                    for i in range(2):
                        pe.wait_ge(m.t_lo, 2 * A + i + 1)
                        for par in range(2):
                            if i == 0 and par == 0:
                                pe.wait_ge(m.y_done, NT * A + 1)
                            if i:
                                pe.wait_ge(m.o_lo, 4 * A + par + 1)
                            rows = slice(par * CTX, (par + 1) * CTX)
                            for b in range(2 * i, 2 * i + 2):
                                last = products(nc, OB[par][:, (b % 2) * S:(b % 2 + 1) * S],
                                                [(vh[rows, b], vl[rows, b], pth[rows, i, (b % 2) * S:(b % 2 + 1) * S],
                                                  ptl[rows, i, (b % 2) * S:(b % 2 + 1) * S])])
                            last.then_inc(m.o_ready, 1)
                project(g, 1)


def mixture(k, tag, w_base, b_base, w_small, w_up, b_thr=None, before=None):
    nc = k.nc
    thresholded = b_thr is not None
    SMALL = ER + GATE
    LINKS = 9 if not thresholded else 9

    with ExitStack() as ctx:
        def sb(name, shape, dt=F):
            return ctx.enter_context(nc.sbuf_tensor(f"{tag}_{name}", shape, dt))

        def sem(name):
            return ctx.enter_context(nc.semaphore(f"{tag}_{name}"))

        braw, bh, bl = sb("braw", [P, KT, D]), sb("bh", [P, KT, D], R), sb("bl", [P, KT, D], R)
        sraw, sh, sl = sb("sraw", [P, KT, SMALL]), sb("sh", [P, KT, SMALL], R), sb("sl", [P, KT, SMALL], R)
        uraw, uh, ul = sb("uraw", [P, D]), sb("uh", [P, D], R), sb("ul", [P, D], R)
        bias = sb("bias", [P, D])
        first = sb("first", [P, NE, NE])
        thr = sb("thr", [P, 1])
        small = sb("small", [P, 2, 12, NE])
        pair = sb("pair", [P, 2, 2, NE, NE])
        one = sb("one", [P, 2, 6])
        hw = sb("hw", [P, 2, ER])
        hth, htl = sb("hth", [P, 2, P], R), sb("htl", [P, 2, P], R)
        YB, GB, TB = k.ps[0:3], k.ps[3:5], k.ps[5:7]
        names = "w_in cst hi_done lo_done g_ready nmax exp_done thr_done link hw_done t_ready t_hi t_lo y_ready"
        m = namedtuple("Sems", names)(*map(sem, names.split()))

        ctx.callback(clear, nc, m)
        with nc.Block() as block:
            @block.sync
            def _(sp):
                for dst, src in ((braw, w_base), (sraw, w_small), (uraw, w_up)):
                    sp.dma_start(dst[:], src).then_inc(m.w_in, 16)
                sp.dma_start(bias[:], b_base.partition_broadcast(P)).then_inc(m.cst, 16)
                sp.dma_start(thr[:] if thresholded else first[:],
                             b_thr.partition_broadcast(P) if thresholded else before).then_inc(m.cst, 16)

            @block.scalar
            def _(act):
                act.wait_ge(m.w_in, 48)
                for h, raw in ((bh, braw), (sh, sraw), (uh, uraw)):
                    nc.scalar.activation(h[:], raw[:], ACT.Copy).then_inc(m.hi_done, 1)
                if thresholded:
                    act.wait_ge(m.cst, 32)
                for t in range(NT + 1):
                    if t < NT:
                        gate = GB[t % 2][:, ER:ER + NE]
                        if thresholded:
                            act.wait_ge(m.nmax, 2 * t + 1)
                            nc.scalar.activation(one[:, t % 2, 2:3], one[:, t % 2, 1:2], ACT.Exp,
                                                 scale=-1.0).then_inc(m.thr_done, 1)
                        act.wait_ge(m.nmax, (2 if thresholded else 1) * (t + 1))
                        nc.scalar.activation(small[:, t % 2, 0], gate, ACT.Exp, bias=one[:, t % 2, 0:1],
                                             accum_out=one[:, t % 2, 3:4]).then_inc(m.exp_done, 1)
                    if t >= 1:
                        act.wait_ge(m.t_ready, t)
                        nc.scalar.activation(hth[:, (t - 1) % 2], TB[(t - 1) % 2][:, 0:P], ACT.Copy).then_inc(
                            m.t_hi, 1)

            @block.vector
            def _(dve):
                for i, (lo, raw, h) in enumerate(((bl, braw, bh), (sl, sraw, sh), (ul, uraw, uh))):
                    dve.wait_ge(m.hi_done, i + 1)
                    nc.vector.tensor_tensor(lo[:], raw[:], f32(h[:]), ALU.subtract).then_inc(m.lo_done, 1)
                dve.wait_ge(m.cst, 32)
                links = 0
                for t in range(NT + 2):
                    if t < NT:
                        s_, o_, p_ = small[:, t % 2], one[:, t % 2], pair[:, t % 2]
                        gb = GB[t % 2]
                        dve.wait_ge(m.g_ready, t + 1)
                        if thresholded:
                            nc.vector.tensor_scalar(o_[:, 1:2], gb[:, ER + NE:ER + NE + 1], thr[:], None,
                                                    ALU.add).then_inc(m.nmax, 1)
                        nc.vector.tensor_reduce(o_[:, 0:1], gb[:, ER:ER + NE], AX.X, ALU.max, negate=True).then_inc(
                            m.nmax, 1)
                        dve.wait_ge(m.exp_done, t + 1)
                        e = s_[:, 0]
                        if thresholded:
                            dve.wait_ge(m.thr_done, t + 1)
                            nc.vector.tensor_scalar(o_[:, 2:3], o_[:, 2:3], 1.0, 8.0, ALU.add, ALU.mult).then_inc(
                                m.link, 1)
                            dve.wait_ge(m.link, links + 1)
                            nc.vector.reciprocal(o_[:, 2:4], o_[:, 2:4]).then_inc(m.link, 1)
                            dve.wait_ge(m.link, links + 2)
                            nc.vector.tensor_scalar(s_[:, 1], e, o_[:, 3:4], o_[:, 2:3], ALU.mult,
                                                    ALU.subtract).then_inc(m.link, 1)
                            dve.wait_ge(m.link, links + 3)
                            nc.vector.tensor_scalar(s_[:, 2], s_[:, 1], 0.0, None, ALU.max).then_inc(
                                m.link, 1)
                            dve.wait_ge(m.link, links + 4)
                            nc.vector.tensor_reduce(o_[:, 4:5], s_[:, 2], AX.X, ALU.add).then_inc(m.link, 1)
                            dve.wait_ge(m.link, links + 5)
                            nc.vector.tensor_scalar(o_[:, 5:6], o_[:, 4:5], 0.0, None, ALU.is_equal).then_inc(
                                m.link, 1)
                            dve.wait_ge(m.link, links + 6)
                            nc.vector.tensor_scalar(o_[:, 4:5], o_[:, 4:5], o_[:, 5:6], 0.5, ALU.add,
                                                    ALU.mult).then_inc(m.link, 1)
                            dve.wait_ge(m.link, links + 7)
                            nc.vector.reciprocal(o_[:, 5:6], o_[:, 4:5]).then_inc(m.link, 1)
                            dve.wait_ge(m.link, links + 8)
                            nc.vector.tensor_scalar(s_[:, 3], s_[:, 2], o_[:, 5:6], None, ALU.mult).then_inc(
                                m.link, 1)
                            links += 9
                        else:
                            own = e.unsqueeze(2).to_broadcast([P, NE, NE])
                            other = e.unsqueeze(1).to_broadcast([P, NE, NE])
                            nc.vector.tensor_tensor(p_[:, 0], other, own, ALU.is_gt).then_inc(m.link, 1)
                            nc.vector.tensor_tensor(p_[:, 1], other, own, ALU.is_equal).then_inc(m.link, 1)
                            dve.wait_ge(m.link, links + 2)
                            nc.vector.tensor_tensor(p_[:, 1], p_[:, 1], first[:], ALU.mult).then_inc(
                                m.link, 1)
                            dve.wait_ge(m.link, links + 3)
                            nc.vector.tensor_tensor(p_[:, 0], p_[:, 0], p_[:, 1], ALU.add).then_inc(
                                m.link, 1)
                            dve.wait_ge(m.link, links + 4)
                            nc.vector.tensor_reduce(s_[:, 1], p_[:, 0], AX.X, ALU.add).then_inc(m.link, 1)
                            dve.wait_ge(m.link, links + 5)
                            nc.vector.scalar_tensor_tensor(s_[:, 2], s_[:, 1], 1.5, e, ALU.is_lt,
                                                           ALU.mult).then_inc(m.link, 1)
                            dve.wait_ge(m.link, links + 6)
                            nc.vector.tensor_reduce(o_[:, 4:5], s_[:, 2], AX.X, ALU.add).then_inc(m.link, 1)
                            dve.wait_ge(m.link, links + 7)
                            nc.vector.reciprocal(o_[:, 5:6], o_[:, 4:5]).then_inc(m.link, 1)
                            dve.wait_ge(m.link, links + 8)
                            nc.vector.tensor_scalar(s_[:, 3], s_[:, 2], o_[:, 5:6], None, ALU.mult).then_inc(
                                m.link, 1)
                            links += 9
                        dve.wait_ge(m.link, links)
                        if t >= 2:
                            dve.wait_ge(m.t_ready, t - 1)
                        nc.vector.tensor_tensor(hw[:, t % 2].rearrange("p (e r) -> p e r", e=NE),
                                                gb[:, 0:ER].rearrange("p (e r) -> p e r", e=NE),
                                                s_[:, 3].unsqueeze(2).to_broadcast([P, NE, RANK]),
                                                ALU.mult).then_inc(m.hw_done, 1)
                    if 1 <= t < NT + 1:
                        dve.wait_ge(m.t_hi, t)
                        nc.vector.tensor_tensor(htl[:, (t - 1) % 2], TB[(t - 1) % 2][:, 0:P],
                                                f32(hth[:, (t - 1) % 2]), ALU.subtract).then_inc(m.t_lo, 1)
                    if t >= 2:
                        dve.wait_ge(m.y_ready, t - 1)
                        nc.vector.tensor_tensor(k.acc[:, t - 2], YB[(t - 2) % 3][:], bias[:], ALU.add).then_inc(
                            m.link, 1)
                        links += 1

            @block.tensor
            def _(pe):
                def lift(t):
                    pe.wait_ge(m.t_lo, t + 1)
                    products(nc, YB[t % 3][:], [(hth[:, t % 2], htl[:, t % 2], uh[:], ul[:])], start=False).then_inc(
                        m.y_ready, 1)

                pe.wait_ge(m.lo_done, 3)
                for t in range(NT + 2):
                    if t < NT:
                        tok = slice(t * P, (t + 1) * P)
                        if t >= 2:
                            pe.wait_ge(m.hw_done, t - 1)
                        products(nc, GB[t % 2][:, 0:SMALL], [(k.xh[:, kt, tok], k.xl[:, kt, tok], sh[:, kt], sl[:, kt])
                                                             for kt in range(KT)]).then_inc(m.g_ready, 1)
                        if t >= 3:
                            pe.wait_ge(m.link, LINKS * t + (t - 2))
                        products(nc, YB[t % 3][:], [(k.xh[:, kt, tok], k.xl[:, kt, tok], bh[:, kt], bl[:, kt])
                                                    for kt in range(KT)], stop=False)
                    if 1 <= t < NT + 1:
                        pe.wait_ge(m.hw_done, t)
                        if t >= 3:
                            pe.wait_ge(m.t_lo, t - 2)
                        nc.tensor.transpose(TB[(t - 1) % 2][:, 0:P], hw[:, (t - 1) % 2], k.ident[:]).then_inc(
                            m.t_ready, 1)
                    if t >= 2:
                        lift(t - 2)


L1_GROUPS = 4
QUAD = 4
ROUNDS = NH // L1_GROUPS // QUAD
WQ_AHEAD = 2


def l1_attention(k, tag, wq, wk, wv, wo, scale, anticausal=None, uniform=None, last_row=None, ctxT=None):
    nc = k.nc
    cross = ctxT is not None
    KEYS = S + CTX if cross else S
    NKV = 6 if cross else 4
    NVT = NT + B if cross else NT
    NG = 2 if cross else 1
    UR = QUAD * B
    PTW = 3 * S if cross else S + P

    with ExitStack() as ctx:
        def sb(name, shape, dt=F):
            return ctx.enter_context(nc.sbuf_tensor(f"{tag}_{name}", shape, dt))

        def sem(name):
            return ctx.enter_context(nc.semaphore(f"{tag}_{name}"))

        wqraw, woraw = sb("wqraw", [P, KT, HD]), sb("woraw", [P, D])
        kvraw = sb("kvraw", [P, 2, KT, HD])
        wqh, wql = sb("wqh", [P, 2, KT, HD], R), sb("wql", [P, 2, KT, HD], R)
        woh, wol = sb("woh", [P, QUAD, D], R), sb("wol", [P, QUAD, D], R)
        wkvh, wkvl = sb("wkvh", [P, 2, KT, HD], R), sb("wkvl", [P, 2, KT, HD], R)
        kh, kl = sb("kh", [P, B, KEYS], R), sb("kl", [P, B, KEYS], R)
        vh, vl = sb("vh", [P, NVT, HD], R), sb("vl", [P, NVT, HD], R)
        qh, ql = sb("qh", [P, 2, TOK], R), sb("ql", [P, 2, TOK], R)
        pb = sb("pb", [P, 2, 2, KEYS])
        pth, ptl = sb("pth", [P, 2, PTW], R), sb("ptl", [P, 2, PTW], R)
        oh, ol = sb("oh", [P, QUAD, TOK], R), sb("ol", [P, QUAD, TOK], R)
        nmax, rsum, rinv = sb("nmax", [P, 2, 2]), sb("rsum", [P, 2, 2]), sb("rinv", [P, 2, 2])
        if cross:
            ctx_raw = sb("ctx_raw", [P, KT, B * CTX])
            ch, cl = sb("ch", [P, KT, B * CTX], R), sb("cl", [P, KT, B * CTX], R)
        else:
            mask_f, mask = sb("mask_f", [P, P]), sb("mask", [P, P], R)
            uni_f, uni = sb("uni_f", [P, 2]), sb("uni", [P, 2], R)
            fix, rfirst = sb("fix", [P, 2]), sb("rfirst", [P, 2, 2])
        SB, TB, QB, OB = k.ps[0:2], k.ps[2:4], k.ps[4:6], k.ps[6:8]

        names = ("wq_in wo_in kv_in cst acc_zero cst_split kvw_split wq_split wo_split kv_ready kv_hi kv_lo q_ready "
                 "q_hi q_lo s_ready max_done exp_done inv_first inv_done p_done t_ready t_hi t_lo o_ready o_hi o_lo "
                 "y_ready y_done link")
        m = namedtuple("Sems", names)(*map(sem, names.split()))

        if cross:
            blocks = [(P, 4 * P, [(q, t * P, t * S + q * P) for t in range(2) for q in range(2)]),
                      (CTX, S, [(q, S, q * P) for q in range(2)])]
        else:
            blocks = [(P, 3 * P, [(0, P, 0), (1, P, P), (0, 0, 2 * P)])]

        def pt_part(t, u, g):
            rows, width, _ = blocks[g]
            return t[0:rows, u % 2, g * 4 * P:g * 4 * P + width]

        def t_bank(u, g):
            rows, width, _ = blocks[g]
            return TB[g if cross else u % 2][0:rows, 0:width]

        def kv_parts():
            for i in range(2):
                yield (TB[i][:].rearrange("p (b s) -> p b s", b=2), kh[:, 2 * i:2 * i + 2, 0:S],
                       kl[:, 2 * i:2 * i + 2, 0:S])
            for i in range(2):
                yield (SB[i][:].rearrange("p (t d) -> p t d", t=4), vh[:, 4 * i:4 * i + 4], vl[:, 4 * i:4 * i + 4])
            if cross:
                yield (OB[0][:, 0:B * CTX].rearrange("p (b s) -> p b s", b=B), kh[:, :, S:], kl[:, :, S:])
                yield (OB[1][0:CTX, :].rearrange("p (t d) -> p t d", t=B), vh[0:CTX, NT:], vl[0:CTX, NT:])

        ctx.callback(clear, nc, m)
        block = ctx.enter_context(nc.Block())

        @block.sync
        def _(sp):
            sp.dma_start(wqraw[:], wq[0]).then_inc(m.wq_in, 16)
            for i, w in enumerate((wk, wv)):
                sp.dma_start(kvraw[:, i], w[0]).then_inc(m.kv_in, 16)
            pairs = ((ctx_raw, ctxT),) if cross else ((mask_f, anticausal), (uni_f, uniform), (fix, last_row))
            for dst, src in pairs:
                sp.dma_start(dst[:], src).then_inc(m.cst, 16)
            sp.wait_ge(m.wq_split, 1)
            sp.dma_start(wqraw[:], wq[1]).then_inc(m.wq_in, 16)
            with nc.sync.Fori(0, L1_GROUPS) as g:
                sp.wait_ge(m.kvw_split, g + 1)
                for i, w in enumerate((wk, wv)):
                    sp.dma_start(kvraw[:, i], w[bass.ds(g + 1, 1)].rearrange("a p k n -> (a p) k n")).then_inc(
                        m.kv_in, 16)
                with nc.sync.Fori(0, NH // L1_GROUPS) as i:
                    h = g * (NH // L1_GROUPS) + i
                    sp.wait_ge(m.wo_split, h + 1)
                    sp.dma_start(woraw[:], wo[bass.ds(h, 1)].rearrange("a p n -> (a p) n")).then_inc(
                        m.wo_in, 16)
                    sp.wait_ge(m.wq_split, h + 2)
                    sp.dma_start(wqraw[:], wq[bass.ds(h + 2, 1)].rearrange("a p k n -> (a p) k n")).then_inc(
                        m.wq_in, 16)

        @block.gpsimd
        def _(pool):
            nc.gpsimd.memset(k.acc[:], 0.0).then_inc(m.wo_split, 1)

            def split_kv(link):
                high_part(k, wkvh[:], kvraw[:]).then_inc(m.link, 1)
                pool.wait_ge(m.link, link)
                nc.gpsimd.tensor_tensor(wkvl[:], kvraw[:], f32(wkvh[:]), ALU.subtract).then_inc(
                    m.kvw_split, 1)

            pool.wait_ge(m.kv_in, 32)
            split_kv(1)
            with nc.gpsimd.Fori(0, L1_GROUPS) as g:
                with nc.gpsimd.Fori(0, ROUNDS) as s:
                    r = g * ROUNDS + s
                    for u in range(UR):
                        h, b = divmod(u, B)
                        pool.wait_ge(m.inv_done, r * UR + u + 1)
                        for q, lo in (((0, 0), (1, P)) if not cross else ((None, 0),)):
                            pv = pb[:, u % 2] if cross else pb[:, u % 2, q, lo:]
                            rv = rinv[:, u % 2] if cross else rinv[:, u % 2, q:q + 1]
                            if cross:
                                last = nc.gpsimd.tensor_tensor(pv, pv, rv.unsqueeze(2).to_broadcast([P, 2, KEYS]),
                                                               ALU.mult)
                            else:
                                last = nc.gpsimd.tensor_tensor(pv, pv, rv.to_broadcast([P, S - lo]), ALU.mult)
                        last.then_inc(m.p_done, 1)
                        H = r * QUAD + h
                        if b == 0:
                            pool.wait_ge(m.wo_in, 16 * H + 16)
                            pool.wait_ge(m.wq_in, 16 * H + 48)
                            pool.wait_ge(m.q_ready, 2 * H + 2)
                        cols = slice(b * P, (b + 1) * P)
                        high_part(k, woh[:, h, cols], woraw[:, cols])
                        high_part(k, wqh[:, h % 2, b], wqraw[:, b]).then_inc(m.link, 1)
                        pool.wait_ge(m.link, r * UR + u + g + 2)
                        o = nc.gpsimd.tensor_tensor(wol[:, h, cols], woraw[:, cols], f32(woh[:, h, cols]),
                                                    ALU.subtract)
                        q = nc.gpsimd.tensor_tensor(wql[:, h % 2, b], wqraw[:, b], f32(wqh[:, h % 2, b]),
                                                    ALU.subtract)
                        if b == B - 1:
                            o.then_inc(m.wo_split, 1)
                            q.then_inc(m.wq_split, 1)
                pool.wait_ge(m.kv_in, 32 * g + 64)
                pool.wait_ge(m.kv_ready, NKV * (g + 1))
                high_part(k, wkvh[:], kvraw[:]).then_inc(m.link, 1)
                pool.wait_ge(m.link, (g + 1) * ROUNDS * UR + g + 2)
                nc.gpsimd.tensor_tensor(wkvl[:], kvraw[:], f32(wkvh[:]), ALU.subtract).then_inc(
                    m.kvw_split, 1)

        @block.scalar
        def _(act):
            for i in range(2):
                act.wait_ge(m.wq_in, 16 * (i + 1))
                nc.scalar.activation(wqh[:, i], wqraw[:], ACT.Copy).then_inc(m.cst_split, 1)
            act.wait_ge(m.cst, 16 if cross else 48)
            for dst, src in (((ch, ctx_raw),) if cross else ((mask, mask_f), (uni, uni_f))):
                nc.scalar.activation(dst[:], src[:], ACT.Copy).then_inc(m.cst_split, 1)

            def query(H, i, par):
                act.wait_ge(m.q_ready, 2 * H + i + 1)
                nc.scalar.activation(qh[:, par, i * 512:(i + 1) * 512], QB[i][:], ACT.Copy).then_inc(
                    m.q_hi, 1)

            for i in range(2):
                query(0, i, 0)
            with nc.scalar.Fori(0, L1_GROUPS) as g:
                for i, (bank, high, low) in enumerate(kv_parts()):
                    act.wait_ge(m.kv_ready, NKV * g + i + 1)
                    nc.scalar.activation(high, bank, ACT.Copy, scale=scale if i in (0, 1, 4) else 1.0).then_inc(
                        m.kv_hi, 1)
                with nc.scalar.Fori(0, ROUNDS) as s:
                    r = g * ROUNDS + s

                    def transposed(u):
                        for j in range(NG):
                            act.wait_ge(m.t_ready, (r * UR + u) * NG + j + 1)
                            if u >= 2 and j == 0:
                                act.wait_ge(m.o_ready, r * UR + u - 1)
                            nc.scalar.activation(pt_part(pth, u, j), t_bank(u, j), ACT.Copy).then_inc(
                                m.t_hi, 1)

                    def attended(u):
                        h, b = divmod(u, B)
                        act.wait_ge(m.o_ready, r * UR + u + 1)
                        nc.scalar.activation(oh[:, h, b * S:(b + 1) * S], OB[u % 2][:, 0:S], ACT.Copy).then_inc(
                            m.o_hi, 1)

                    for u in range(UR):
                        h, b = divmod(u, B)
                        for q in range(2):
                            lo = P if q and not cross else 0
                            act.wait_ge(m.max_done, (r * UR + u) * 2 + q + 1)
                            if u >= 2 and q == 0:
                                act.wait_ge(m.t_ready, (r * UR + u - 1) * NG)
                            nc.scalar.activation(pb[:, u % 2, q, lo:], SB[q][:, lo:KEYS], ACT.Exp,
                                                 bias=nmax[:, u % 2, q:q + 1],
                                                 accum_out=rsum[:, u % 2, q:q + 1]).then_inc(m.exp_done, 1)
                        if b % 2:
                            query(r * QUAD + h + 1, b // 2, (h + 1) % 2)
                        if u >= 1:
                            transposed(u - 1)
                        if u >= 2:
                            attended(u - 2)
                    attended(UR - 2)
                    transposed(UR - 1)
                    attended(UR - 1)

        @block.vector
        def _(dve):
            nc.vector.memset(rsum[:], 1.0).then_inc(m.y_done, 1)
            for i in range(2):
                dve.wait_ge(m.cst_split, i + 1)
                nc.vector.tensor_tensor(wql[:, i], wqraw[:], f32(wqh[:, i]), ALU.subtract).then_inc(
                    m.wq_split, 1)
            if cross:
                dve.wait_ge(m.cst_split, 3)
                nc.vector.tensor_tensor(cl[:], ctx_raw[:], f32(ch[:]), ALU.subtract).then_inc(m.acc_zero, 1)

            def query(H, i, par):
                dve.wait_ge(m.q_hi, 2 * H + i + 1)
                cols = slice(i * 512, (i + 1) * 512)
                nc.vector.tensor_tensor(ql[:, par, cols], QB[i][:], f32(qh[:, par, cols]), ALU.subtract).then_inc(
                    m.q_lo, 1)

            for i in range(2):
                query(0, i, 0)
            with nc.vector.Fori(0, L1_GROUPS) as g:
                for i, (bank, high, low) in enumerate(kv_parts()):
                    dve.wait_ge(m.kv_hi, NKV * g + i + 1)
                    if i in (0, 1, 4):
                        for b in range(high.shape[1]):
                            last = nc.vector.scalar_tensor_tensor(low[:, b], bank[:, b], scale, f32(high[:, b]),
                                                                  ALU.mult, ALU.subtract)
                        last.then_inc(m.kv_lo, 1)
                    else:
                        nc.vector.tensor_tensor(low, bank, f32(high), ALU.subtract).then_inc(m.kv_lo, 1)
                with nc.vector.Fori(0, ROUNDS) as s:
                    r = g * ROUNDS + s

                    def transposed(u):
                        for j in range(NG):
                            dve.wait_ge(m.t_hi, (r * UR + u) * NG + j + 1)
                            nc.vector.tensor_tensor(pt_part(ptl, u, j), t_bank(u, j), f32(pt_part(pth, u, j)),
                                                    ALU.subtract).then_inc(m.t_lo, 1)

                    def attended(u):
                        h, b = divmod(u, B)
                        dve.wait_ge(m.o_hi, r * UR + u + 1)
                        cols = slice(b * S, (b + 1) * S)
                        nc.vector.tensor_tensor(ol[:, h, cols], OB[u % 2][:, 0:S], f32(oh[:, h, cols]),
                                                ALU.subtract).then_inc(m.o_lo, 1)

                    def projected(t):
                        dve.wait_ge(m.y_ready, r * NT + t + 1)
                        nc.vector.tensor_tensor(k.acc[:, t], SB[t % 2][:], k.acc[:, t], ALU.add).then_inc(
                            m.y_done, 1)

                    for u in range(UR):
                        h, b = divmod(u, B)
                        for q in range(2):
                            lo = P if q and not cross else 0
                            dve.wait_ge(m.s_ready, (r * UR + u) * 2 + q + 1)
                            nc.vector.tensor_reduce(nmax[:, u % 2, q:q + 1], SB[q][:, lo:KEYS], AX.X, ALU.max,
                                                    negate=True).then_inc(m.max_done, 1)
                        if b % 2:
                            query(r * QUAD + h + 1, b // 2, (h + 1) % 2)
                        if u >= 1:
                            transposed(u - 1)
                        dve.wait_ge(m.exp_done, (r * UR + u) * 2 + 2)
                        if cross:
                            nc.vector.reciprocal(rinv[:, u % 2], rsum[:, u % 2]).then_inc(m.inv_done, 1)
                        else:
                            nc.vector.reciprocal(rfirst[:, u % 2], rsum[:, u % 2]).then_inc(m.inv_first, 1)
                            dve.wait_ge(m.inv_first, r * UR + u + 1)
                            nc.vector.tensor_tensor(rinv[:, u % 2], rfirst[:, u % 2], fix[:], ALU.mult).then_inc(
                                m.inv_done, 1)
                        if u >= 2:
                            attended(u - 2)
                    attended(UR - 2)
                    projected(0)
                    projected(1)
                    transposed(UR - 1)
                    projected(2)
                    projected(3)
                    attended(UR - 1)
                    for t in range(4, NT):
                        projected(t)

        @block.tensor
        def _(pe):
            def query(H, i, par, kts=range(KT)):
                if kts[0] == 0:
                    pe.wait_ge(m.wq_split, H + 1)
                cols = slice(i * 512, (i + 1) * 512)
                last = products(nc, QB[i][:], [(wqh[:, par, kt], wql[:, par, kt], k.xh[:, kt, cols], k.xl[:, kt, cols])
                                               for kt in kts], start=kts[0] == 0, stop=kts[-1] == KT - 1)
                if kts[-1] == KT - 1:
                    last.then_inc(m.q_ready, 1)

            for i in range(2):
                query(0, i, 0)
            if cross:
                pe.wait_ge(m.acc_zero, 1)
            pe.wait_ge(m.cst_split, 3 if cross else 4)
            with nc.tensor.Fori(0, L1_GROUPS) as g:
                pe.wait_ge(m.kvw_split, g + 1)
                pe.wait_ge(m.y_done, g * ROUNDS * NT + 1)
                for i in range(2):
                    cols = slice(i * 512, (i + 1) * 512)
                    products(nc, TB[i][:], [(wkvh[:, 0, kt], wkvl[:, 0, kt], k.xh[:, kt, cols], k.xl[:, kt, cols])
                                            for kt in range(KT)]).then_inc(m.kv_ready, 1)
                for i in range(2):
                    for t in range(4):
                        tok = slice((4 * i + t) * P, (4 * i + t + 1) * P)
                        last = products(nc, SB[i][:, t * HD:(t + 1) * HD],
                                        [(k.xh[:, kt, tok], k.xl[:, kt, tok], wkvh[:, 1, kt], wkvl[:, 1, kt])
                                         for kt in range(KT)])
                    last.then_inc(m.kv_ready, 1)
                if cross:
                    products(nc, OB[0][:, 0:B * CTX], [(wkvh[:, 0, kt], wkvl[:, 0, kt], ch[:, kt], cl[:, kt])
                                                       for kt in range(KT)]).then_inc(m.kv_ready, 1)
                    for b in range(B):
                        own = slice(b * CTX, (b + 1) * CTX)
                        last = products(nc, OB[1][0:CTX, b * HD:(b + 1) * HD],
                                        [(ch[:, kt, own], cl[:, kt, own], wkvh[:, 1, kt], wkvl[:, 1, kt])
                                         for kt in range(KT)])
                    last.then_inc(m.kv_ready, 1)
                with nc.tensor.Fori(0, ROUNDS) as s:
                    r = g * ROUNDS + s

                    def scores(u):
                        h, b = divmod(u, B)
                        if b % 2 == 0:
                            pe.wait_ge(m.q_lo, (r * QUAD + h) * 2 + b // 2 + 1)
                        for q in range(2):
                            if u == 0 and q == 0:
                                pe.wait_ge(m.y_done, r * NT + 1)
                            elif u:
                                pe.wait_ge(m.exp_done, (r * UR + u - 1) * 2 + q + 1)
                            tok = slice(b * S + q * P, b * S + (q + 1) * P)
                            lo = P if q and not cross else 0
                            last = products(nc, SB[q][:, lo:KEYS], [(qh[:, h % 2, tok], ql[:, h % 2, tok],
                                                                     kh[:, b, lo:], kl[:, b, lo:])])
                            if not cross:
                                last = nc.tensor.matmul(SB[q][:, q * P:(q + 1) * P], k.ident_r[:], mask[:],
                                                        start=False, stop=True, skip_group_check=True)
                            last.then_inc(m.s_ready, 1)

                    def transpose(u):
                        pe.wait_ge(m.p_done, r * UR + u + 1)
                        if cross and u >= 1:
                            pe.wait_ge(m.t_lo, (r * UR + u) * NG)
                        elif not cross and u >= 2:
                            pe.wait_ge(m.t_lo, r * UR + u - 1)
                        for j, (rows, width, parts) in enumerate(blocks):
                            for q, key, at in parts:
                                last = nc.tensor.transpose(t_bank(u, j)[:, at:at + P],
                                                           pb[:, u % 2, q, key:key + rows], k.ident[:])
                            last.then_inc(m.t_ready, 1)

                    def attend(u):
                        h, b = divmod(u, B)
                        pe.wait_ge(m.t_lo, (r * UR + u + 1) * NG)
                        if u >= 2:
                            pe.wait_ge(m.o_lo, r * UR + u - 1)
                        out = OB[u % 2][:, 0:S]
                        ph, pl = pth[:, u % 2], ptl[:, u % 2]
                        if cross:
                            v, o = vh, vl
                            last = products(nc, out, [
                                (vh[:, 2 * b], vl[:, 2 * b], ph[:, 0:S], pl[:, 0:S]),
                                (vh[:, 2 * b + 1], vl[:, 2 * b + 1], ph[:, S:2 * S], pl[:, S:2 * S]),
                                (vh[0:CTX, NT + b], vl[0:CTX, NT + b], ph[0:CTX, 2 * S:], pl[0:CTX, 2 * S:])])
                        else:
                            products(nc, out, [(vh[:, 2 * b + 1], vl[:, 2 * b + 1], ph[:, 0:S], pl[:, 0:S])])
                            products(nc, out[:, 0:P], [(vh[:, 2 * b], vl[:, 2 * b], ph[:, S:], pl[:, S:])],
                                     start=False, cover=True)
                            last = products(nc, out[:, S - 2:S], [(vh[:, 2 * b], vl[:, 2 * b], uni[:], None)],
                                            start=False, cover=True)
                        last.then_inc(m.o_ready, 1)

                    def project(t):
                        pe.wait_ge(m.o_lo, r * UR + UR - B + t // 2 + 1)
                        pe.wait_ge(m.exp_done, (r * UR + UR) * 2)
                        if t >= 2:
                            pe.wait_ge(m.y_done, r * NT + t)
                        products(nc, SB[t % 2][:], [(oh[:, h, t * P:(t + 1) * P], ol[:, h, t * P:(t + 1) * P],
                                                     woh[:, h], wol[:, h]) for h in range(QUAD)]).then_inc(
                            m.y_ready, 1)

                    pe.wait_ge(m.kv_lo, NKV * (g + 1))
                    for u in range(UR):
                        h, b = divmod(u, B)
                        scores(u)
                        if b % 2 == 0:
                            pe.wait_ge(m.q_lo, (r * QUAD + h) * 2 + b // 2 + 1)
                        query(r * QUAD + h + 1, b // 2, (h + 1) % 2, range(0, 2) if b % 2 == 0 else range(2, KT))
                        if u >= 1:
                            transpose(u - 1)
                        if u >= 2:
                            attend(u - 2)
                    attend(UR - 2)
                    pe.wait_ge(m.wo_split, (r + 1) * QUAD + 1)
                    project(0)
                    project(1)
                    transpose(UR - 1)
                    project(2)
                    project(3)
                    attend(UR - 1)
                    for t in range(4, NT):
                        project(t)


def build(nc, a, out, stages=6):
    with ExitStack() as ctx:
        def sb(name, shape, dt=F):
            return ctx.enter_context(nc.sbuf_tensor(name, shape, dt))

        k = Core()
        k.nc = nc
        k.x, k.acc = sb("x", [P, NT, D]), sb("acc", [P, NT, D])
        k.xh, k.xl = sb("xT_high", [P, KT, TOK], R), sb("xT_low", [P, KT, TOK], R)
        k.ident, k.ident_r, k.half = sb("ident", [P, P]), sb("ident_r", [P, P], R), sb("minus_half", [P, 1])
        k.one = sb("one", [P, 1])
        k.ps = [ctx.enter_context(nc.psum_tensor(f"bank{i}", [P, 512], F)) for i in range(8)]
        k.ident_in = a["identity"]
        with nc.Block() as block:
            @block.vector
            def _(dve):
                nc.vector.memset(k.half[:], -0.5)
                nc.vector.memset(k.one[:], 1.0)
        l0_self_attention(k, a["x"], a["xT"], a["a0_wq"], a["a0_bq"], a["a0_wk"], a["a0_bk"], a["a0_wv"], a["a0_bv"],
                          a["a0_wo"], a["a0_bo"], a["headmask"], a["causal4"])
        if stages == 1:
            return norm_stage(k, "n1", keep_T=False, out=out)
        norm_stage(k, "n2")
        l0_cross_attention(k, a["ctx_dup"], a["ctxT"], a["x0_wk"], a["x0_wq"], a["x0_wv"], a["x0_wo"], a["x0_q_norm"],
                           a["x0_k_norm"], a["x0_mask"])
        if stages == 2:
            return norm_stage(k, "n3", keep_T=False, out=out)
        norm_stage(k, "n4")
        mixture(k, "f0", a["f0_base"], a["f0_bias"], a["f0_small"], a["f0_up"], before=a["before"])
        if stages == 3:
            return norm_stage(k, "n5", keep_T=False, out=out)
        norm_stage(k, "n6")
        l1_attention(k, "a1", a["a1_wq"], a["a1_wk"], a["a1_wv"], a["a1_wo"], HD ** -0.5,
                     anticausal=a["anticausal"], uniform=a["uniform"], last_row=a["last_row"])
        if stages == 4:
            return norm_stage(k, "n7", keep_T=False, out=out)
        norm_stage(k, "n8")
        l1_attention(k, "x1", a["x1_wq"], a["x1_wk"], a["x1_wv"], a["x1_wo"], HD ** -0.5, ctxT=a["ctxT"])
        if stages == 5:
            return norm_stage(k, "n9", keep_T=False, out=out)
        norm_stage(k, "n10")
        mixture(k, "f1", a["f1_base"], a["f1_bias"], a["f1_small"], a["f1_up"], b_thr=a["f1_thr"])
        norm_stage(k, "n11", keep_T=False, out=out)


def kernel(**inputs):
    import numpy as np
    import concourse.bacc as bacc
    from concourse.bass_utils import run_bass_kernel_spmd

    arrays = layouts(np, inputs)
    nc = bacc.Bacc("TRN2", target_bir_lowering=False, num_devices=1)
    args = {n: nc.dram_tensor("in_" + n, v.shape, mybir.dt.from_np(v.dtype), kind="ExternalInput").ap()
            for n, v in arrays.items()}
    out = nc.dram_tensor("out", (TOK, D), F, kind="ExternalOutput").ap()
    build(nc, args, out)
    r = run_bass_kernel_spmd(nc, [{"in_" + n: v for n, v in arrays.items()}], core_ids=[0])
    return r.results[0]["out"].reshape(B, S, D)


def layouts(np, i):
    def parts(w):
        return np.ascontiguousarray(w.reshape(KT, P, -1).transpose(1, 0, 2))

    i = {n: np.asarray(v) for n, v in i.items()}
    x = i["x"].reshape(TOK, D)
    a = {"x": x, "xT": parts(x.T), "identity": np.eye(P, dtype=np.float32)}
    a["a0_wq"] = parts(i["L0_attn_wq_w"].T)
    a["a0_bq"] = np.ascontiguousarray(i["L0_attn_wq_b"].reshape(NCH, P).T)
    for n in "kv":
        a[f"a0_w{n}"] = parts(np.tile(i[f"L0_attn_w{n}_w"], (HPC, 1)).T)
        a[f"a0_b{n}"] = np.tile(i[f"L0_attn_w{n}_b"], HPC).reshape(P, 1)
    a["a0_wo"] = parts(i["L0_attn_wo_w"].T)
    a["a0_bo"] = i["L0_attn_wo_b"]
    a["headmask"] = np.kron(np.eye(HPC), np.ones((HD0, 1))).astype(np.float32)
    later = np.triu(np.ones((P, P)), 1)
    a["causal4"] = np.ascontiguousarray(np.repeat((later * MASKED).astype(np.float32)[:, None], 4, 1))
    c = i["ctx_4096"].reshape(B * CTX, D)
    a["ctxT"] = parts(c.T)
    dup = c.reshape(B, 1, CTX, D).repeat(2, 1).reshape(B * P, D)
    a["ctx_dup"] = parts(dup.T).reshape(P, KT, B, P)

    def heads(w, n, spare):
        h = w.reshape(KT, P, n, HD).transpose(2, 1, 0, 3)
        return np.ascontiguousarray(np.concatenate([h, h[:spare]]))

    a["x0_wk"] = parts(i["L0_xattn_Wk"].T)
    a["x0_wq"] = heads(i["L0_xattn_Wq"].T, NH, WQ_AHEAD)
    a["x0_wv"] = heads(i["L0_xattn_Wv"].T, X0_GROUPS, 1)
    a["x0_wo"] = np.ascontiguousarray(i["L0_xattn_Wo"].T).reshape(NH, HD, D)
    a["x0_q_norm"] = i["L0_xattn_q_norm_w"].reshape(HD, 1)
    a["x0_k_norm"] = i["L0_xattn_k_norm_w"].reshape(HD, 1)
    a["x0_mask"] = i["mask_1x1xSxS2_ff0"].reshape(S, CTX)
    for t, n in (("a1", "L1_attn"), ("x1", "L1_xattn")):
        a[t + "_wq"] = heads(i[n + "_Wq"], NH, WQ_AHEAD)
        a[t + "_wk"] = heads(i[n + "_Wk"], L1_GROUPS, 1)
        a[t + "_wv"] = heads(i[n + "_Wv"], L1_GROUPS, 1)
        a[t + "_wo"] = i[n + "_Wo"].reshape(NH, HD, D)
    a["anticausal"] = (np.tril(np.ones((P, P))) * MASKED).astype(np.float32)
    a["uniform"] = np.repeat(np.array([[0, 1 / S]], np.float32), P, 0)
    a["last_row"] = np.ones((P, 2), np.float32)
    a["last_row"][P - 1, 1] = P / S
    a["before"] = np.repeat(np.tril(np.ones((NE, NE), np.float32), -1)[None], P, 0)

    def small(A, gate, *thr):
        cols = [A.reshape(ER, D).T, gate.T] + [t.reshape(D, 1) for t in thr]
        have = sum(c.shape[1] for c in cols)
        return parts(np.concatenate(cols + [np.zeros((D, ER + GATE - have), np.float32)], 1))

    def up(w):
        return np.ascontiguousarray(w.transpose(0, 2, 1)).reshape(ER, D)

    a["f0_base"], a["f0_bias"] = parts(i["L0_ffn_W_base"].T), i["L0_ffn_b_base"]
    a["f0_small"], a["f0_up"] = small(i["L0_ffn_A"], i["L0_ffn_W_gate"]), up(i["L0_ffn_B"])
    a["f1_base"], a["f1_bias"] = parts(i["L1_ffn_W_base"].T), i["L1_ffn_b_base"]
    a["f1_small"] = small(i["L1_ffn_A_w"], i["L1_ffn_W_gate"], i["L1_ffn_W_thr"])
    a["f1_up"], a["f1_thr"] = up(i["L1_ffn_B_w"]), i["L1_ffn_b_thr"]
    return a
```

```python
from collections import namedtuple
from contextlib import ExitStack

import concourse.bass as bass
from concourse import mybir

F = mybir.dt.float32
R = mybir.dt.float32r
ALU = mybir.AluOpType
ACT = mybir.ActivationFunctionType
AX = mybir.AxisListType

P = 128
B, S, D = 4, 256, 512
TOK = B * S
NT = TOK // P
KT = D // P
CTX = 64
HD = 128
NH = 32
NE, RANK = 8, 16
ER = NE * RANK
GATE = NE + 2
EPS = 1e-5
MASKED = -1e30


def f32(ap):
    return ap.bitcast(F)


def products(nc, out, terms, start=True, stop=True, cover=False):
    passes = []
    for lh, ll, rh, rl in terms:
        passes += [(lh, rh)] + ([(lh, rl)] if rl is not None else []) + ([(ll, rh)] if ll is not None else [])
    for i, (lhsT, rhs) in enumerate(passes):
        last = nc.tensor.matmul(out, lhsT, rhs, start=start and i == 0, stop=stop and i == len(passes) - 1,
                                skip_group_check=cover)
    return last


class Core:
    pass


def high_part(k, out, raw):
    one = k.one[:]
    while len(one.shape) < len(raw.shape):
        one = one.unsqueeze(1)
    return k.nc.gpsimd.tensor_tensor(out, raw, one.to_broadcast(list(raw.shape)), ALU.mult)


def clear(nc, sems):
    with nc.Block() as block:
        @block.sync
        def _(sp):
            for s in sems:
                nc.sync.sem_clear(s)


HD0 = D // NH
NCH = D // P
HPC = NH // NCH
HALF = D // 2


def l0_self_attention(k, x_nat, xT, wq, bq, wk, bk, wv, bv, wo, bo, headmask, causal4):
    nc = k.nc
    UN = 6
    UB = UN * NCH
    units = [(c, v) for c in range(NCH) for v in range(UN)]

    with ExitStack() as ctx:
        def sb(name, shape, dt=F):
            return ctx.enter_context(nc.sbuf_tensor("a0_" + name, shape, dt))

        def sem(name):
            return ctx.enter_context(nc.semaphore("a0_" + name))

        wraw = sb("wraw", [P, KT, D])
        wqh, wql = sb("wqh", [P, KT, D], R), sb("wql", [P, KT, D], R)
        woh, wol = sb("woh", [P, KT, D], R), sb("wol", [P, KT, D], R)
        kvraw = sb("kvraw", [P, 2, KT, P])
        kvh, kvl = sb("kvh", [P, 2, KT, P], R), sb("kvl", [P, 2, KT, P], R)
        bias = sb("bias", [P, NCH + 2])
        bo_b = sb("bo_b", [P, D])
        hm = sb("hm", [P, HPC])
        caus_f, caus = sb("caus_f", [P, 4, P]), sb("caus", [P, 4, P], R)
        xraw = sb("xraw", [P, KT, S])
        xh, xl = sb("xh", [P, KT, S], R), sb("xl", [P, KT, S], R)
        kf, kfh, kfl = sb("kf", [P, S]), sb("kfh", [P, S], R), sb("kfl", [P, S], R)
        kdh, kdl = sb("kdh", [P, HPC, S], R), sb("kdl", [P, HPC, S], R)
        vf = sb("vf", [P, S])
        DIAG = P + HD0
        vdh, vdl = sb("vdh", [P, 2, HPC * DIAG], R), sb("vdl", [P, 2, HPC * DIAG], R)
        qh, ql = sb("qh", [P, 2, S], R), sb("ql", [P, 2, S], R)
        nmax, rsum, rinv = sb("nmax", [P, 4, 4]), sb("rsum", [P, 4, 4]), sb("rinv", [P, 4, 4])
        pb = sb("pb", [P, 4, 4, P])
        pth, ptl = sb("pth", [P, 2, 4, P], R), sb("ptl", [P, 2, 4, P], R)
        oh, ol = sb("oh", [P, NCH, S], R), sb("ol", [P, NCH, S], R)
        SB, TB, OB, XB = k.ps[0:3], k.ps[3:5], k.ps[5:7], k.ps[7]

        def head_view(t, kt):
            return t[:, kt, :].rearrange("p (j r) -> p j r", r=DIAG)[:, :, 0:HD0]

        names = ("cst wq_in wo_in kv_in xin w_split wraw_free kv_split xh_done xl_done zeroed x_ready kv_done kh_done kd_done "
                 "v_done vt_done vd_done q_ready q_hi q_lo s_ready max_done exp_done inv_done p_done t_ready "
                 "t_hi t_lo o_ready o_hi o_lo y_ready y_done s_link")
        m = namedtuple("Sems", names)(*map(sem, names.split()))

        def shape_of(v):
            return (4 * v, 4, 0, P) if v < 2 else (2 * (v - 2), 2, 1, S)

        ctx.callback(clear, nc, m)
        block = ctx.enter_context(nc.Block())

        @block.sync
        def _(sp):
            sp.dma_start(kvraw[:, 0], wk).then_inc(m.kv_in, 16)
            sp.dma_start(kvraw[:, 1], wv).then_inc(m.kv_in, 16)
            sp.dma_start(xraw[:], xT[:, :, 0:S]).then_inc(m.xin, 16)
            sp.dma_start(wraw[:], wq).then_inc(m.wq_in, 16)
            for dst, src in ((bias[:, 0:NCH], bq), (bias[:, NCH:NCH + 1], bk), (bias[:, NCH + 1:NCH + 2], bv),
                             (hm[:], headmask), (caus_f[:], causal4), (k.ident[:], k.ident_in),
                             (bo_b[:], bo.partition_broadcast(P)),
                             (k.x[:], x_nat.rearrange("(t p) d -> p t d", p=P))):
                sp.dma_start(dst, src).then_inc(m.cst, 16)
            sp.wait_ge(m.wraw_free, 1)
            sp.dma_start(wraw[:], wo).then_inc(m.wo_in, 16)
            with nc.sync.Fori(1, B) as b:
                sp.wait_ge(m.xl_done, b)
                sp.dma_start(xraw[:], xT[:, :, bass.ds(b * S, S)]).then_inc(m.xin, 16)

        @block.gpsimd
        def _(pool):
            nc.gpsimd.memset(f32(vdh[:]), 0.0).then_inc(m.zeroed, 1)
            nc.gpsimd.memset(f32(vdl[:]), 0.0).then_inc(m.zeroed, 1)
            pool.wait_ge(m.kv_in, 32)
            high_part(k, kvh[:], kvraw[:]).then_inc(m.s_link, 1)
            pool.wait_ge(m.s_link, 1)
            nc.gpsimd.tensor_tensor(kvl[:], kvraw[:], f32(kvh[:]), ALU.subtract).then_inc(m.kv_split, 1)
            with nc.gpsimd.Fori(0, B) as b:
                for u, (c, v) in enumerate(units):
                    j, n, qt, w = shape_of(v)
                    pool.wait_ge(m.inv_done, b * UB + u + 1)
                    pv = pb[:, u % 4].rearrange("p (n a) q -> p n (a q)", n=n)
                    nc.gpsimd.tensor_tensor(
                        pv, pv, rinv[:, u % 4, 0:n].unsqueeze(2).to_broadcast([P, n, w]), ALU.mult
                    ).then_inc(m.p_done, 1)

        @block.scalar
        def _(act):
            act.wait_ge(m.wq_in, 16)
            nc.scalar.activation(wqh[:], wraw[:], ACT.Copy).then_inc(m.w_split, 1)
            act.wait_ge(m.cst, 128)
            nc.scalar.activation(caus[:], caus_f[:], ACT.Copy).then_inc(m.w_split, 1)
            nc.scalar.activation(k.ident_r[:], k.ident[:], ACT.Copy).then_inc(m.w_split, 1)
            act.wait_ge(m.wo_in, 16)
            nc.scalar.activation(woh[:], wraw[:], ACT.Copy).then_inc(m.w_split, 1)
            with nc.scalar.Fori(0, B) as b:
                act.wait_ge(m.xin, (b + 1) * 16)
                act.wait_ge(m.y_done, b * 2 + 1)
                nc.scalar.activation(xh[:], xraw[:], ACT.Copy).then_inc(m.xh_done, 1)
                act.wait_ge(m.kd_done, b * 3 + 1)
                nc.scalar.activation(kfh[:], kf[:], ACT.Copy).then_inc(m.kh_done, 1)
                act.wait_ge(m.vt_done, b + 1)
                act.wait_ge(m.zeroed, 2)
                for kt in range(2):
                    nc.scalar.activation(head_view(vdh, kt), XB[:, kt * P:(kt + 1) * P].rearrange(
                        "p (j r) -> p j r", r=HD0), ACT.Copy).then_inc(m.v_done, 1)

                def query(c):
                    act.wait_ge(m.q_ready, b * NCH + c + 1)
                    nc.scalar.activation(qh[:, c % 2], XB[:, 0:S], ACT.Identity, bias=bias[:, c:c + 1]).then_inc(
                        m.q_hi, 1)

                def transposed(u):
                    act.wait_ge(m.t_ready, b * UB + u + 1)
                    if u >= 2:
                        act.wait_ge(m.o_ready, b * UB + u - 1)
                    nc.scalar.activation(pth[:, u % 2], TB[u % 2][:].rearrange("p (n q) -> p n q", q=P),
                                         ACT.Copy).then_inc(m.t_hi, 1)

                def attended(c):
                    act.wait_ge(m.o_ready, b * UB + UN * (c + 1))
                    nc.scalar.activation(oh[:, c], OB[c % 2][:, 0:S], ACT.Copy).then_inc(m.o_hi, 1)

                query(0)
                for u in range(UB + 3):
                    if u < UB:
                        c, v = units[u]
                        j, n, qt, w = shape_of(v)
                        if v == 0 and c + 1 < NCH:
                            query(c + 1)
                        act.wait_ge(m.max_done, b * UB + u + 1)
                        if u >= 4:
                            act.wait_ge(m.t_ready, b * UB + u - 3)
                        for i in range(n):
                            pv = pb[:, u % 4].rearrange("p (n a) q -> p n (a q)", n=n)
                            last = nc.scalar.activation(
                                pv[:, i], SB[u % 3][:, i * w:(i + 1) * w], ACT.Exp, bias=nmax[:, u % 4, i:i + 1],
                                accum_out=rsum[:, u % 4, i:i + 1])
                        last.then_inc(m.exp_done, 1)
                    if 2 <= u < UB + 2:
                        transposed(u - 2)
                    if u >= 3 and (u - 3) % UN == UN - 1:
                        attended((u - 3) // UN)

        @block.vector
        def _(dve):
            nc.vector.memset(rsum[:], 1.0).then_inc(m.y_done, 1)
            dve.wait_ge(m.w_split, 1)
            nc.vector.tensor_tensor(wql[:], wraw[:], f32(wqh[:]), ALU.subtract).then_inc(m.wraw_free, 1)
            dve.wait_ge(m.cst, 128)
            dve.wait_ge(m.w_split, 4)
            nc.vector.tensor_tensor(wol[:], wraw[:], f32(woh[:]), ALU.subtract).then_inc(m.wraw_free, 1)
            with nc.vector.Fori(0, B) as b:
                dve.wait_ge(m.xh_done, b + 1)
                nc.vector.tensor_tensor(xl[:], xraw[:], f32(xh[:]), ALU.subtract).then_inc(m.xl_done, 1)
                dve.wait_ge(m.kv_done, b + 1)
                nc.vector.tensor_scalar(kf[:], XB[:, 0:S], bias[:, NCH:NCH + 1], HD0 ** -0.5, ALU.add,
                                        ALU.mult).then_inc(m.kd_done, 1)
                nc.vector.tensor_scalar(vf[:], XB[:, S:2 * S], bias[:, NCH + 1:NCH + 2], None,
                                        ALU.add).then_inc(m.x_ready, 1)
                dve.wait_ge(m.kh_done, b + 1)
                nc.vector.tensor_tensor(kfl[:], kf[:], f32(kfh[:]), ALU.subtract).then_inc(m.kd_done, 1)
                dve.wait_ge(m.kd_done, b * 3 + 2)
                for j in range(HPC):
                    nc.vector.tensor_scalar(kdh[:, j], f32(kfh[:]), hm[:, j:j + 1], None, ALU.mult)
                    last = nc.vector.tensor_scalar(kdl[:, j], f32(kfl[:]), hm[:, j:j + 1], None, ALU.mult)
                last.then_inc(m.kd_done, 1)
                dve.wait_ge(m.v_done, b * 2 + 2)
                for kt in range(2):
                    last = nc.vector.tensor_tensor(head_view(vdl, kt), XB[:, kt * P:(kt + 1) * P].rearrange(
                        "p (j r) -> p j r", r=HD0), f32(head_view(vdh, kt)), ALU.subtract)
                last.then_inc(m.vd_done, 1)

                def query(c):
                    dve.wait_ge(m.q_hi, b * NCH + c + 1)
                    nc.vector.scalar_tensor_tensor(ql[:, c % 2], XB[:, 0:S], bias[:, c:c + 1], f32(qh[:, c % 2]),
                                                   ALU.add, ALU.subtract).then_inc(m.q_lo, 1)

                def inverse(u):
                    n = shape_of(units[u][1])[1]
                    dve.wait_ge(m.exp_done, b * UB + u + 1)
                    nc.vector.reciprocal(rinv[:, u % 4, 0:n], rsum[:, u % 4, 0:n]).then_inc(m.inv_done, 1)

                query(0)
                for u in range(UB + 3):
                    if u < UB:
                        c, v = units[u]
                        j, n, qt, w = shape_of(v)
                        if v == 0 and c + 1 < NCH:
                            query(c + 1)
                        dve.wait_ge(m.s_ready, b * UB + u + 1)
                        nc.vector.tensor_reduce(nmax[:, u % 4, 0:n], SB[u % 3][:].rearrange("p (n w) -> p n w", n=n),
                                                AX.X, ALU.max, negate=True).then_inc(m.max_done, 1)
                    if 1 <= u < UB + 1:
                        inverse(u - 1)
                    if 2 <= u < UB + 2:
                        dve.wait_ge(m.t_hi, b * UB + u - 1)
                        nc.vector.tensor_tensor(ptl[:, u % 2], TB[u % 2][:].rearrange("p (n q) -> p n q", q=P),
                                                f32(pth[:, u % 2]), ALU.subtract).then_inc(m.t_lo, 1)
                    if u >= 3 and (u - 3) % UN == UN - 1:
                        c = (u - 3) // UN
                        dve.wait_ge(m.o_hi, b * NCH + c + 1)
                        nc.vector.tensor_tensor(ol[:, c], OB[c % 2][:, 0:S], f32(oh[:, c]),
                                                ALU.subtract).then_inc(m.o_lo, 1)
                for t in range(2):
                    dve.wait_ge(m.y_ready, b * 2 + t + 1)
                    nc.vector.tensor_tensor(k.acc[:, bass.ds(b * 2 + t, 1), :], (SB[0], SB[1])[t][:].unsqueeze(1),
                                            bo_b[:].unsqueeze(1), ALU.add).then_inc(m.y_done, 1)

        @block.tensor
        def _(pe):
            pe.wait_ge(m.kv_split, 1)
            pe.wait_ge(m.w_split, 4)
            pe.wait_ge(m.wraw_free, 2)
            pe.wait_ge(m.zeroed, 2)
            with nc.tensor.Fori(0, B) as b:
                pe.wait_ge(m.xl_done, b + 1)
                for i in range(2):
                    last = products(nc, XB[:, i * S:(i + 1) * S],
                                    [(kvh[:, i, kt], kvl[:, i, kt], xh[:, kt], xl[:, kt]) for kt in range(KT)])
                last.then_inc(m.kv_done, 1)
                pe.wait_ge(m.x_ready, b + 1)
                for kt in range(2):
                    last = nc.tensor.transpose(XB[:, kt * P:(kt + 1) * P], vf[:, kt * P:(kt + 1) * P], k.ident[:])
                last.then_inc(m.vt_done, 1)
                pe.wait_ge(m.vd_done, b + 1)

                def query(c):
                    if c:
                        pe.wait_ge(m.q_lo, b * NCH + c)
                    products(nc, XB[:, 0:S], [(wqh[:, kt, c * P:(c + 1) * P], wql[:, kt, c * P:(c + 1) * P],
                                               xh[:, kt], xl[:, kt]) for kt in range(KT)]).then_inc(m.q_ready, 1)

                def scores(u):
                    c, v = units[u]
                    j, n, qt, w = shape_of(v)
                    if v == 0:
                        pe.wait_ge(m.q_lo, b * NCH + c + 1)
                    if u >= 3:
                        pe.wait_ge(m.exp_done, b * UB + u - 2)
                    ql_, qh_ = ql[:, c % 2, qt * P:(qt + 1) * P], qh[:, c % 2, qt * P:(qt + 1) * P]
                    out = SB[u % 3][:].rearrange("p (n w) -> p n w", n=n)
                    products(nc, out, [(qh_, ql_, kdh[:, j:j + n, 0:w], kdl[:, j:j + n, 0:w])])
                    nc.tensor.matmul(out[:, :, w - P:w], k.ident_r[:], caus[:, 0:n], start=False,
                                     stop=True, skip_group_check=True).then_inc(m.s_ready, 1)

                def transpose(u):
                    pe.wait_ge(m.p_done, b * UB + u + 1)
                    if u >= 2:
                        pe.wait_ge(m.t_lo, b * UB + u - 1)
                    for i in range(4):
                        last = nc.tensor.transpose(TB[u % 2][:, i * P:(i + 1) * P], pb[:, u % 4, i], k.ident[:])
                    last.then_inc(m.t_ready, 1)

                def attend(u):
                    c, v = units[u]
                    j, n, qt, w = shape_of(v)
                    pe.wait_ge(m.t_lo, b * UB + u + 1)
                    if v == 0 and c >= 2:
                        pe.wait_ge(m.o_lo, b * NCH + c - 1)
                    out = OB[c % 2][:, qt * P:(qt + 1) * P]
                    for i in range(n):
                        for kt in range(w // P):
                            at = i * (w // P) + kt
                            vj = slice((j + i) * P, (j + i + 1) * P)
                            last = products(nc, out, [(vdh[:, kt, vj], vdl[:, kt, vj], pth[:, u % 2, at],
                                                       ptl[:, u % 2, at])], start=v == 0 and i == 0,
                                            stop=v in (1, UN - 1) and i == n - 1 and kt == w // P - 1, cover=True)
                    last.then_inc(m.o_ready, 1)

                query(0)
                pe.wait_ge(m.kd_done, b * 3 + 3)
                for u in range(UB + 3):
                    if u < UB:
                        scores(u)
                        if units[u][1] == 0 and units[u][0] + 1 < NCH:
                            query(units[u][0] + 1)
                    if 2 <= u < UB + 2:
                        transpose(u - 2)
                    if u >= 3:
                        attend(u - 3)
                pe.wait_ge(m.o_lo, b * NCH + NCH)
                for t in range(2):
                    pe.wait_ge(m.exp_done, b * UB + UB)
                    products(nc, (SB[0], SB[1])[t][:], [(oh[:, c, t * P:(t + 1) * P], ol[:, c, t * P:(t + 1) * P],
                                                         woh[:, c], wol[:, c]) for c in range(NCH)]).then_inc(
                        m.y_ready, 1)
                pe.wait_ge(m.y_done, b * 2 + 3)


def norm_stage(k, tag, keep_T=True, out=None):
    nc = k.nc
    TB = k.ps[0:4]
    with ExitStack() as ctx:
        def sb(name, shape, dt=F):
            return ctx.enter_context(nc.sbuf_tensor(f"{tag}_{name}", shape, dt))

        def sem(name):
            return ctx.enter_context(nc.semaphore(f"{tag}_{name}"))

        r_sum, stats, mv = sb("r_sum", [P, 2, D]), sb("stats", [P, 2, 6]), sb("mv", [P, 2, 2])
        ve, rs = sb("ve", [P, 2]), sb("rs", [P, 2])
        names = "link var rstd r_used tr hi lo stored"
        m = namedtuple("Sems", names)(*map(sem, names.split()))
        ctx.callback(clear, nc, m)
        block = ctx.enter_context(nc.Block())

        def low(dve, t):
            dve.wait_ge(m.hi, t + 1)
            nc.vector.tensor_tensor(k.xl[:, :, t * P:(t + 1) * P], TB[t % 4][:].rearrange("p (c q) -> p c q", c=KT),
                                    f32(k.xh[:, :, t * P:(t + 1) * P]), ALU.subtract).then_inc(m.lo, 1)

        @block.vector
        def _(dve):
            for t in range(NT):
                if t >= 2:
                    dve.wait_ge(m.r_used, t - 1)
                nc.vector.tensor_tensor(r_sum[:, t % 2], k.x[:, t], k.acc[:, t], ALU.add).then_inc(m.link, 1)
                dve.wait_ge(m.link, 3 * t + 1)
                nc.vector.bn_stats(stats[:, t % 2], r_sum[:, t % 2]).then_inc(m.link, 1)
                dve.wait_ge(m.link, 3 * t + 2)
                nc.vector.bn_aggr(mv[:, t % 2], stats[:, t % 2]).then_inc(m.link, 1)
                dve.wait_ge(m.link, 3 * t + 3)
                nc.vector.tensor_scalar(ve[:, t % 2:t % 2 + 1], mv[:, t % 2, 1:2], EPS, None,
                                        ALU.add).then_inc(m.var, 1)
                dve.wait_ge(m.rstd, t + 1)
                nc.vector.tensor_scalar(k.x[:, t], r_sum[:, t % 2], mv[:, t % 2, 0:1], rs[:, t % 2:t % 2 + 1],
                                        ALU.subtract, ALU.mult).then_inc(m.r_used, 1)
                if keep_T and t >= 1:
                    low(dve, t - 1)
            if keep_T:
                low(dve, NT - 1)

        @block.gpsimd
        def _(pool):
            for t in range(NT):
                pool.wait_ge(m.var, t + 1)
                nc.gpsimd.tensor_tensor(rs[:, t % 2:t % 2 + 1], ve[:, t % 2:t % 2 + 1], k.half[:],
                                        ALU.pow).then_inc(m.rstd, 1)

        if keep_T:
            @block.tensor
            def _(pe):
                for t in range(NT):
                    pe.wait_ge(m.r_used, t + 1)
                    if t >= 4:
                        pe.wait_ge(m.lo, t - 3)
                    for c in range(KT):
                        last = nc.tensor.transpose(TB[t % 4][:, c * P:(c + 1) * P], k.x[:, t, c * P:(c + 1) * P],
                                                   k.ident[:])
                    last.then_inc(m.tr, 1)

            @block.scalar
            def _(act):
                for t in range(NT):
                    act.wait_ge(m.tr, t + 1)
                    nc.scalar.activation(k.xh[:, :, t * P:(t + 1) * P], TB[t % 4][:].rearrange(
                        "p (c q) -> p c q", c=KT), ACT.Copy).then_inc(m.hi, 1)
        else:
            @block.sync
            def _(sp):
                for t in range(NT):
                    sp.wait_ge(m.r_used, t + 1)
                    sp.dma_start(out[t * P:(t + 1) * P, :], k.x[:, t]).then_inc(m.stored, 16)
                sp.wait_ge(m.stored, 16 * NT)


X0_GROUPS = 8
X0_PAIRS = NH // X0_GROUPS // 2
X0_AHEAD = 4


def l0_cross_keys(k, st, ctxT, wk, wv, q_norm, k_norm):
    nc = k.nc
    with ExitStack() as ctx:
        def sb(name, shape, dt=F):
            return ctx.enter_context(nc.sbuf_tensor("xk_" + name, shape, dt))

        def sem(name):
            return ctx.enter_context(nc.semaphore("xk_" + name))

        W = X0_GROUPS * HD
        craw, ch, cl = sb("craw", [P, KT, B * CTX]), sb("ch", [P, KT, B * CTX], R), sb("cl", [P, KT, B * CTX], R)
        wraw = sb("wraw", [P, KT, W])
        wkh, wkl = sb("wkh", [P, KT, W], R), sb("wkl", [P, KT, W], R)
        wvh, wvl = sb("wvh", [P, KT, W], R), sb("wvl", [P, KT, W], R)
        sq = sb("sq", [P, 4, 4, HD])
        kn = sq
        ss, rk = sb("ss", [P, 4, 4]), sb("rk", [P, 4, 4])
        norms, w = sb("norms", [P, 2]), sb("w", [P, 1])
        names = ("wk_in wv_in c_in c_hi c_lo w_hi w_lo sq_done ss_done rk_done w_done k_ready v_ready v_hi v_lo "
                 "kn_done t_ready hi lo link")
        m = namedtuple("Sems", names)(*map(sem, names.split()))
        KB, VB = k.ps[0:4], k.ps[4:8]
        ctx.callback(clear, nc, m)
        block = ctx.enter_context(nc.Block())

        @block.sync
        def _(sp):
            sp.dma_start(craw[:], ctxT).then_inc(m.c_in, 16)
            sp.dma_start(norms[:, 0:1], q_norm).then_inc(m.c_in, 16)
            sp.dma_start(norms[:, 1:2], k_norm).then_inc(m.c_in, 16)
            sp.dma_start(wraw[:], wk).then_inc(m.wk_in, 16)
            sp.wait_ge(m.w_lo, KT)
            sp.dma_start(wraw[:], wv).then_inc(m.wv_in, 16)

        @block.scalar
        def _(act):
            act.wait_ge(m.c_in, 48)
            nc.scalar.activation(ch[:], craw[:], ACT.Copy).then_inc(m.c_hi, 1)
            act.wait_ge(m.wk_in, 16)
            for kt in range(KT):
                nc.scalar.activation(wkh[:, kt], wraw[:, kt], ACT.Copy).then_inc(m.w_hi, 1)
            act.wait_ge(m.wv_in, 16)
            for kt in range(KT):
                nc.scalar.activation(wvh[:, kt], wraw[:, kt], ACT.Copy).then_inc(m.w_hi, 1)
            for i in range(4):
                act.wait_ge(m.k_ready, i + 1)
                nc.scalar.activation(sq[:, i], KB[i][:].rearrange("p (g d) -> p g d", d=HD),
                                     ACT.Square).then_inc(m.sq_done, 1)
            for i in range(4):
                act.wait_ge(m.v_ready, i + 1)
                nc.scalar.activation(st.vh[:, 2 * i:2 * i + 2], VB[i][:].rearrange("p (g n) -> p g n", g=2),
                                     ACT.Copy).then_inc(m.v_hi, 1)
            act.wait_ge(m.w_done, 1)
            for i in range(4):
                act.wait_ge(m.t_ready, i + 1)
                nc.scalar.activation(st.kh[:, 2 * i:2 * i + 2], VB[i][:].rearrange("p (g n) -> p g n", g=2),
                                     ACT.Copy, scale=w[:]).then_inc(m.hi, 1)

        @block.gpsimd
        def _(pool):
            pool.wait_ge(m.ss_done, 1)
            nc.gpsimd.tensor_tensor(rk[:], ss[:], k.half[:].unsqueeze(2).to_broadcast([P, 4, 4]), ALU.pow).then_inc(
                m.rk_done, 1)

        @block.vector
        def _(dve):
            dve.wait_ge(m.c_in, 48)
            nc.vector.tensor_scalar(w[:], norms[:, 0:1], norms[:, 1:2], HD ** -0.5, ALU.mult, ALU.mult).then_inc(
                m.w_done, 1)
            dve.wait_ge(m.c_hi, 1)
            nc.vector.tensor_tensor(cl[:], craw[:], f32(ch[:]), ALU.subtract).then_inc(m.c_lo, 1)
            for i, (high, low) in enumerate(((wkh, wkl), (wvh, wvl))):
                for kt in range(KT):
                    dve.wait_ge(m.w_hi, i * KT + kt + 1)
                    nc.vector.tensor_tensor(low[:, kt], wraw[:, kt], f32(high[:, kt]), ALU.subtract).then_inc(
                        m.w_lo, 1)
            for i in range(4):
                dve.wait_ge(m.sq_done, i + 1)
                last = nc.vector.tensor_reduce(ss[:, i], sq[:, i], AX.X, ALU.add)
            last.then_inc(m.link, 1)
            dve.wait_ge(m.link, 1)
            nc.vector.tensor_scalar(ss[:], ss[:], 1.0 / HD, EPS, ALU.mult, ALU.add).then_inc(m.ss_done, 1)
            dve.wait_ge(m.rk_done, 1)
            for i in range(4):
                nc.vector.tensor_tensor(kn[:, i], KB[i][:].rearrange("p (g d) -> p g d", d=HD),
                                        rk[:, i].unsqueeze(2).to_broadcast([P, 4, HD]), ALU.mult).then_inc(
                    m.kn_done, 1)
            for i in range(4):
                dve.wait_ge(m.v_hi, i + 1)
                nc.vector.tensor_tensor(st.vl[:, 2 * i:2 * i + 2], VB[i][:].rearrange("p (g n) -> p g n", g=2),
                                        f32(st.vh[:, 2 * i:2 * i + 2]), ALU.subtract).then_inc(m.v_lo, 1)
            for i in range(4):
                dve.wait_ge(m.hi, i + 1)
                nc.vector.scalar_tensor_tensor(st.kl[:, 2 * i:2 * i + 2], VB[i][:].rearrange(
                    "p (g n) -> p g n", g=2), w[:], f32(st.kh[:, 2 * i:2 * i + 2]), ALU.mult,
                    ALU.subtract).then_inc(m.lo, 1)

        @block.tensor
        def _(pe):
            pe.wait_ge(m.c_lo, 1)
            for kt in range(KT):
                pe.wait_ge(m.w_lo, kt + 1)
                for i in range(4):
                    pair, half = divmod(i, 2)
                    rows, cols = slice(pair * P, (pair + 1) * P), slice(half * 512, (half + 1) * 512)
                    last = products(nc, KB[i][:], [(ch[:, kt, rows], cl[:, kt, rows], wkh[:, kt, cols],
                                                    wkl[:, kt, cols])], start=kt == 0, stop=kt == KT - 1)
                    if kt == KT - 1:
                        last.then_inc(m.k_ready, 1)
            pe.wait_ge(m.w_lo, 2 * KT)
            for g in range(X0_GROUPS):
                own = slice(g * HD, (g + 1) * HD)
                last = products(nc, VB[g // 2][:, g % 2 * 256:(g % 2 + 1) * 256],
                                [(wvh[:, kt, own], wvl[:, kt, own], ch[:, kt], cl[:, kt]) for kt in range(KT)])
                if g % 2:
                    last.then_inc(m.v_ready, 1)
            pe.wait_ge(m.kn_done, 4)
            for i in range(4):
                pe.wait_ge(m.v_lo, i + 1)
                for j in range(2):
                    g = 2 * i + j
                    for pair in range(2):
                        last = nc.tensor.transpose(VB[i][:, (2 * j + pair) * P:(2 * j + pair + 1) * P],
                                                   kn[:, 2 * pair + g // 4, g % 4], k.ident[:])
                last.then_inc(m.t_ready, 1)


def l0_cross_attention(k, ctxT, wk, wq, wv, wo, q_norm, k_norm, mask):
    nc = k.nc
    with ExitStack() as ctx:
        def sb(name, shape, dt=F):
            return ctx.enter_context(nc.sbuf_tensor("x0_" + name, shape, dt))

        def sem(name):
            return ctx.enter_context(nc.semaphore("x0_" + name))

        st = namedtuple("Context", "kh kl vh vl")(*(sb(n, [P, X0_GROUPS, B * CTX], R) for n in ("kh", "kl", "vh", "vl")))
        l0_cross_keys(k, st, ctxT, wk, wv, q_norm, k_norm)

        wqraw, woraw = sb("wqraw", [P, 2, KT, HD]), sb("woraw", [P, 2, D])
        wqh, wql = sb("wqh", [P, 2, KT, HD], R), sb("wql", [P, 2, KT, HD], R)
        woh, wol = sb("woh", [P, 2, D], R), sb("wol", [P, 2, D], R)
        PAD = 3 * CTX
        kph, kpl = sb("kph", [P, B, PAD], R), sb("kpl", [P, B, PAD], R)
        vph, vpl = sb("vph", [P, B, PAD], R), sb("vpl", [P, B, PAD], R)
        qh, ql, q2 = sb("qh", [P, 2, TOK], R), sb("ql", [P, 2, TOK], R), sb("q2", [P, 2, TOK])
        ones = sb("ones", [P, 1])
        NS = 2 * NT
        qv, rq, mx, sm, rs = (sb(n, [P, NS]) for n in ("qv", "rq", "mx", "sm", "rs"))
        mask_sb = sb("mask", [P, 2, CTX])
        sT = sb("sT", [P, TOK])
        pb = sb("pb", [P, NT, P])
        pth, ptl = sb("pth", [P, TOK], R), sb("ptl", [P, TOK], R)
        uh, ul = sb("uh", [P, B, D], R), sb("ul", [P, B, D], R)
        QB, TB, SB, UB = k.ps[0:2], k.ps[2:4], k.ps[4:6], k.ps[6:8]

        names = ("wq_a_in wq_b_in wo_in cst zeroed wq_hi wq_a_split wq_b_split wo_split k_placed v_placed q_ready q_used q_lo "
                 "n_ready n_out rq_done st_ready st_out s_ready scaled masked maxed shifted exp_done summed inv_done "
                 "p_done t_ready t_hi t_lo u_ready u_hi u_lo y_ready y_done link")
        m = namedtuple("Sems", names)(*map(sem, names.split()))
        wq_in, wq_split = (m.wq_a_in, m.wq_b_in), (m.wq_a_split, m.wq_b_split)
        ctx.callback(clear, nc, m)
        block = ctx.enter_context(nc.Block())

        def half(ap, h):
            return ap[:, h * 4:h * 4 + 4].rearrange("p t (a n) -> p (t a) n", n=CTX)

        def wide(ap, h):
            return ap[:, h * NT:(h + 1) * NT].unsqueeze(2).to_broadcast([P, NT, CTX])

        def group_rows(t, g):
            return f32(t[:, bass.ds(g, 1), :].rearrange("p a (b n) -> p (a b) n", b=B))

        @block.sync
        def _(sp):
            for par in range(2):
                sp.dma_start(wqraw[:, par], wq[par]).then_inc(wq_in[par], 16)
            sp.dma_start(mask_sb[:], mask.rearrange("(t p) n -> p t n", p=P)).then_inc(m.cst, 16)
            sp.dma_start(woraw[:], wo[0:2].rearrange("a p n -> p a n")).then_inc(m.wo_in, 16)
            for par in range(2):
                sp.wait_ge(wq_split[par], 1)
                sp.dma_start(wqraw[:, par], wq[2 + par]).then_inc(wq_in[par], 16)
            with nc.sync.Fori(0, NH // 2) as p:
                for par in range(2):
                    sp.wait_ge(wq_split[par], p + 2)
                    sp.dma_start(wqraw[:, par], wq[bass.ds(2 * p + par + 4, 1)].rearrange(
                        "a p k n -> (a p) k n")).then_inc(wq_in[par], 16)
                sp.wait_ge(m.wo_split, p + 1)
                sp.dma_start(woraw[:], wo[bass.ds(2 * p + 2, 2)].rearrange("a p n -> p a n")).then_inc(m.wo_in, 16)

        @block.gpsimd
        def _(pool):
            for t in (kph, kpl, vph, vpl):
                last = nc.gpsimd.memset(f32(t[:]), 0.0)
            last.then_inc(m.zeroed, 1)

            def split_wo(link):
                high_part(k, woh[:], woraw[:]).then_inc(m.link, 1)
                pool.wait_ge(m.link, link)
                nc.gpsimd.tensor_tensor(wol[:], woraw[:], f32(woh[:]), ALU.subtract).then_inc(m.wo_split, 1)

            def split_wq(par, link):
                high_part(k, wqh[:, par], wqraw[:, par]).then_inc(m.link, 1)
                pool.wait_ge(m.link, link)
                nc.gpsimd.tensor_tensor(wql[:, par], wqraw[:, par], f32(wqh[:, par]), ALU.subtract).then_inc(
                    wq_split[par], 1)

            def inverse_root(p):
                pool.wait_ge(m.n_out, p + 1)
                nc.gpsimd.tensor_tensor(rq[:], qv[:], k.half[:].to_broadcast([P, NS]), ALU.pow).then_inc(
                    m.rq_done, 1)

            for par in range(2):
                pool.wait_ge(wq_in[par], 32)
                pool.wait_ge(m.q_ready, 2 * par + 2)
                split_wq(par, par + 1)
            pool.wait_ge(m.wo_in, 16)
            split_wo(3)
            inverse_root(0)
            pool.wait_ge(m.cst, 16)
            pool.wait_ge(m.zeroed, 1)
            with nc.gpsimd.Fori(0, X0_GROUPS) as g:
                for i in range(X0_PAIRS):
                    p = g * X0_PAIRS + i
                    if i == 0:
                        one = k.one[:].unsqueeze(1).to_broadcast([P, B, CTX])
                        nc.gpsimd.tensor_tensor(vph[:, :, CTX:2 * CTX], group_rows(st.vh, g), one, ALU.mult)
                        nc.gpsimd.tensor_tensor(vpl[:, :, CTX:2 * CTX], group_rows(st.vl, g), one,
                                                ALU.mult).then_inc(m.v_placed, 1)
                    for h in range(2):
                        pool.wait_ge(m.scaled, 2 * p + h + 1)
                        pv = pb[:, 4 * h:4 * h + 4].rearrange("p (b q) (a n) -> p q b a n", q=2, n=CTX)
                        for q in range(2):
                            last = nc.gpsimd.tensor_tensor(pv[:, q], pv[:, q], mask_sb[:, q:q + 1].unsqueeze(
                                1).to_broadcast([P, 2, 2, CTX]), ALU.add)
                        last.then_inc(m.masked, 1)
                    pool.wait_ge(m.wq_a_in, 16 * p + 48)
                    pool.wait_ge(m.q_ready, 4 * p + 6)
                    split_wq(0, 3 * p + 4)
                    for h in range(2):
                        pool.wait_ge(m.inv_done, 2 * p + h + 1)
                        nc.gpsimd.tensor_tensor(half(pb, h), half(pb, h), wide(rs, h), ALU.mult).then_inc(
                            m.p_done, 1)
                    pool.wait_ge(m.wq_b_in, 16 * p + 48)
                    pool.wait_ge(m.q_ready, 4 * p + 8)
                    split_wq(1, 3 * p + 5)
                    pool.wait_ge(m.wo_in, 16 * p + 32)
                    pool.wait_ge(m.u_ready, 4 * p + 4)
                    split_wo(3 * p + 6)
                    inverse_root(p + 1)

        @block.scalar
        def _(act):
            for par in range(2):
                act.wait_ge(wq_in[par], 16)
                nc.scalar.activation(wqh[:, par], wqraw[:, par], ACT.Copy).then_inc(m.wq_hi, 1)

            def query(H, i, par):
                cols = slice(i * 512, (i + 1) * 512)
                act.wait_ge(m.q_ready, 2 * H + i + 1)
                nc.scalar.activation(qh[:, par, cols], QB[i][:], ACT.Copy)
                nc.scalar.activation(q2[:, par, cols], QB[i][:], ACT.Square).then_inc(m.q_used, 1)

            for par in range(2):
                for i in range(2):
                    query(par, i, par)
            act.wait_ge(m.zeroed, 1)
            with nc.scalar.Fori(0, X0_GROUPS) as g:
                for j in range(X0_PAIRS):
                    p = g * X0_PAIRS + j
                    if j == 0:
                        nc.scalar.activation(kph[:, :, CTX:2 * CTX], group_rows(st.kh, g), ACT.Copy)
                        nc.scalar.activation(kpl[:, :, CTX:2 * CTX], group_rows(st.kl, g), ACT.Copy).then_inc(
                            m.k_placed, 1)
                    for i in range(2):
                        act.wait_ge(m.st_ready, 2 * p + i + 1)
                        nc.scalar.activation(sT[:, i * 512:(i + 1) * 512], TB[i][:], ACT.Copy).then_inc(
                            m.st_out, 1)
                    for h in range(2):
                        query(2 * p + 2, h, 0)
                        act.wait_ge(m.shifted, 2 * p + h + 1)
                        nc.scalar.activation(half(pb, h), half(pb, h), ACT.Exp).then_inc(m.exp_done, 1)
                    for i in range(2):
                        query(2 * p + 3, i, 1)
                    for b in range(B):
                        act.wait_ge(m.u_ready, 4 * p + b + 1)
                        nc.scalar.activation(uh[:, b], UB[b % 2][:], ACT.Copy).then_inc(m.u_hi, 1)
                    for i in range(2):
                        act.wait_ge(m.t_ready, 2 * p + i + 1)
                        nc.scalar.activation(pth[:, i * 512:(i + 1) * 512], TB[i][:], ACT.Copy).then_inc(
                            m.t_hi, 1)

        @block.vector
        def _(dve):
            nc.vector.memset(ones[:], 1.0)
            nc.vector.memset(f32(pth[:]), 0.0)
            nc.vector.memset(f32(ptl[:]), 0.0).then_inc(m.t_lo, 2)
            nc.vector.memset(f32(uh[:]), 0.0)
            nc.vector.memset(f32(ul[:]), 0.0).then_inc(m.u_lo, B)
            nc.vector.memset(k.acc[:], 0.0)
            for par in range(2):
                dve.wait_ge(m.wq_hi, par + 1)
                nc.vector.tensor_tensor(wql[:, par], wqraw[:, par], f32(wqh[:, par]), ALU.subtract).then_inc(
                    wq_split[par], 1)

            def query(H, i, par):
                cols = slice(i * 512, (i + 1) * 512)
                dve.wait_ge(m.q_used, 2 * H + i + 1)
                nc.vector.tensor_tensor(ql[:, par, cols], QB[i][:], f32(qh[:, par, cols]), ALU.subtract).then_inc(
                    m.q_lo, 1)

            def variance(p):
                dve.wait_ge(m.n_ready, p + 1)
                nc.vector.tensor_scalar(qv[:], QB[0][:, 0:NS], 1.0 / HD, EPS, ALU.mult, ALU.add).then_inc(m.n_out, 1)

            def project(p):
                for t in range(NT):
                    dve.wait_ge(m.y_ready, p * NT + t + 1)
                    nc.vector.tensor_tensor(k.acc[:, t], UB[t % 2][:], k.acc[:, t], ALU.add).then_inc(
                        m.y_done, 1)

            for par in range(2):
                for i in range(2):
                    query(par, i, par)
            variance(0)
            with nc.vector.Fori(0, X0_GROUPS) as g:
                for j in range(X0_PAIRS):
                    p = g * X0_PAIRS + j
                    project(p)
                    dve.wait_ge(m.rq_done, p + 1)
                    for h in range(2):
                        dve.wait_ge(m.s_ready, 2 * p + h + 1)
                        nc.vector.tensor_tensor(half(pb, h), SB[h][:].rearrange("p (t n) -> p t n", n=CTX),
                                                wide(rq, h), ALU.mult).then_inc(m.scaled, 1)
                    for h in range(2):
                        dve.wait_ge(m.masked, 2 * p + h + 1)
                        nc.vector.tensor_reduce(mx[:, h * NT:(h + 1) * NT], half(pb, h), AX.X, ALU.max).then_inc(
                            m.maxed, 1)
                        dve.wait_ge(m.maxed, 2 * p + h + 1)
                        nc.vector.tensor_tensor(half(pb, h), half(pb, h), wide(mx, h), ALU.subtract).then_inc(
                            m.shifted, 1)
                    for i in range(2):
                        query(2 * p + 2, i, 0)
                    for h in range(2):
                        dve.wait_ge(m.exp_done, 2 * p + h + 1)
                        own = slice(h * NT, (h + 1) * NT)
                        nc.vector.tensor_reduce(sm[:, own], half(pb, h), AX.X, ALU.add).then_inc(m.summed, 1)
                        dve.wait_ge(m.summed, 2 * p + h + 1)
                        nc.vector.reciprocal(rs[:, own], sm[:, own]).then_inc(m.inv_done, 1)
                    for i in range(2):
                        query(2 * p + 3, i, 1)
                    for b in range(B):
                        dve.wait_ge(m.u_hi, 4 * p + b + 1)
                        nc.vector.tensor_tensor(ul[:, b], UB[b % 2][:], f32(uh[:, b]), ALU.subtract).then_inc(
                            m.u_lo, 1)
                    for i in range(2):
                        cols = slice(i * 512, (i + 1) * 512)
                        dve.wait_ge(m.t_hi, 2 * p + i + 1)
                        nc.vector.tensor_tensor(ptl[:, cols], TB[i][:], f32(pth[:, cols]), ALU.subtract).then_inc(
                            m.t_lo, 1)
                    variance(p + 1)
            project(NH // 2)

        @block.tensor
        def _(pe):
            def query(H, i, par):
                cols = slice(i * 512, (i + 1) * 512)
                products(nc, QB[i][:], [(wqh[:, par, kt], wql[:, par, kt], k.xh[:, kt, cols], k.xl[:, kt, cols])
                                        for kt in range(KT)]).then_inc(m.q_ready, 1)

            def squares(p):
                pe.wait_ge(m.q_lo, 4 * p + 4)
                for t in range(NT):
                    for par in range(2):
                        last = nc.tensor.matmul(QB[0][:, 2 * t + par:2 * t + par + 1],
                                                q2[:, par, t * P:(t + 1) * P], ones[:], start=True, stop=True)
                last.then_inc(m.n_ready, 1)

            def project(p):
                pe.wait_ge(m.t_lo, 2 * p + 2)
                pe.wait_ge(m.u_lo, B * p + B)
                for t in range(NT):
                    if t >= 2:
                        pe.wait_ge(m.y_done, NT * p + t - 1)
                    tok, b = slice(t * P, (t + 1) * P), t // 2
                    products(nc, UB[t % 2][:], [(pth[:, tok], ptl[:, tok], uh[:, b], ul[:, b])]).then_inc(
                        m.y_ready, 1)

            for par in range(2):
                pe.wait_ge(wq_split[par], 1)
                for i in range(2):
                    if par:
                        pe.wait_ge(m.q_lo, i + 1)
                    query(par, i, par)
            squares(0)
            with nc.tensor.Fori(0, X0_GROUPS) as g:
                for j in range(X0_PAIRS):
                    p = g * X0_PAIRS + j
                    if j == 0:
                        pe.wait_ge(m.k_placed, g + 1)
                    pe.wait_ge(m.t_lo, 2 * p + 2)
                    for i in range(2):
                        for b in (2 * i, 2 * i + 1):
                            tok = slice(b * S, (b + 1) * S)
                            last = products(nc, TB[i][:, b % 2 * S:(b % 2 + 1) * S], [
                                (kph[:, b, at:at + P], kpl[:, b, at:at + P], qh[:, par, tok], ql[:, par, tok])
                                for par, at in ((0, CTX), (1, 0))])
                        last.then_inc(m.st_ready, 1)
                    project(p)
                    for i in range(2):
                        pe.wait_ge(m.st_out, 2 * p + i + 1)
                        for t in range(4 * i, 4 * i + 4):
                            last = nc.tensor.transpose(SB[i][:, t % 4 * P:(t % 4 + 1) * P], sT[:, t * P:(t + 1) * P],
                                                       k.ident[:])
                        last.then_inc(m.s_ready, 1)
                    pe.wait_ge(m.wq_a_split, p + 2)
                    pe.wait_ge(m.n_out, p + 1)
                    for i in range(2):
                        query(2 * p + 2, i, 0)
                    pe.wait_ge(m.wq_b_split, p + 2)
                    for i in range(2):
                        pe.wait_ge(m.q_lo, 4 * p + 5 + i)
                        query(2 * p + 3, i, 1)
                    pe.wait_ge(m.wo_split, p + 1)
                    if j == 0:
                        pe.wait_ge(m.v_placed, g + 1)
                    for b in range(B):
                        if b < 2:
                            pe.wait_ge(m.y_done, NT * p + NT - 1 + b)
                        else:
                            pe.wait_ge(m.u_lo, B * p + B + b - 1)
                        products(nc, UB[b % 2][:], [
                            (vph[:, b, at:at + P], vpl[:, b, at:at + P], woh[:, par], wol[:, par])
                            for par, at in ((0, CTX), (1, 0))]).then_inc(m.u_ready, 1)
                    for i in range(2):
                        pe.wait_ge(m.p_done, 2 * p + i + 1)
                        for t in range(4 * i, 4 * i + 4):
                            last = nc.tensor.transpose(TB[i][:, t % 4 * P:(t % 4 + 1) * P], pb[:, t], k.ident[:])
                        last.then_inc(m.t_ready, 1)
                    squares(p + 1)
            pe.wait_ge(m.y_done, NT * (NH // 2))
            project(NH // 2)


def mixture(k, tag, w_base, b_base, w_small, w_up, b_thr=None, before=None):
    nc = k.nc
    thresholded = b_thr is not None
    SMALL = ER + GATE
    LINKS = 9 if not thresholded else 9

    with ExitStack() as ctx:
        def sb(name, shape, dt=F):
            return ctx.enter_context(nc.sbuf_tensor(f"{tag}_{name}", shape, dt))

        def sem(name):
            return ctx.enter_context(nc.semaphore(f"{tag}_{name}"))

        braw, bh, bl = sb("braw", [P, KT, D]), sb("bh", [P, KT, D], R), sb("bl", [P, KT, D], R)
        sraw, sh, sl = sb("sraw", [P, KT, SMALL]), sb("sh", [P, KT, SMALL], R), sb("sl", [P, KT, SMALL], R)
        uraw, uh, ul = sb("uraw", [P, D]), sb("uh", [P, D], R), sb("ul", [P, D], R)
        bias = sb("bias", [P, D])
        first = sb("first", [P, NE, NE])
        thr = sb("thr", [P, 1])
        small = sb("small", [P, 2, 12, NE])
        pair = sb("pair", [P, 2, 2, NE, NE])
        one = sb("one", [P, 2, 6])
        hw = sb("hw", [P, 2, ER])
        hth, htl = sb("hth", [P, 2, P], R), sb("htl", [P, 2, P], R)
        YB, GB, TB = k.ps[0:3], k.ps[3:5], k.ps[5:7]
        names = "w_in cst hi_done lo_done g_ready nmax exp_done thr_done link hw_done t_ready t_hi t_lo y_ready"
        m = namedtuple("Sems", names)(*map(sem, names.split()))

        ctx.callback(clear, nc, m)
        with nc.Block() as block:
            @block.sync
            def _(sp):
                for dst, src in ((braw, w_base), (sraw, w_small), (uraw, w_up)):
                    sp.dma_start(dst[:], src).then_inc(m.w_in, 16)
                sp.dma_start(bias[:], b_base.partition_broadcast(P)).then_inc(m.cst, 16)
                sp.dma_start(thr[:] if thresholded else first[:],
                             b_thr.partition_broadcast(P) if thresholded else before).then_inc(m.cst, 16)

            @block.scalar
            def _(act):
                act.wait_ge(m.w_in, 48)
                for h, raw in ((bh, braw), (sh, sraw), (uh, uraw)):
                    nc.scalar.activation(h[:], raw[:], ACT.Copy).then_inc(m.hi_done, 1)
                if thresholded:
                    act.wait_ge(m.cst, 32)
                for t in range(NT + 1):
                    if t < NT:
                        gate = GB[t % 2][:, ER:ER + NE]
                        if thresholded:
                            act.wait_ge(m.nmax, 2 * t + 1)
                            nc.scalar.activation(one[:, t % 2, 2:3], one[:, t % 2, 1:2], ACT.Exp,
                                                 scale=-1.0).then_inc(m.thr_done, 1)
                        act.wait_ge(m.nmax, (2 if thresholded else 1) * (t + 1))
                        nc.scalar.activation(small[:, t % 2, 0], gate, ACT.Exp, bias=one[:, t % 2, 0:1],
                                             accum_out=one[:, t % 2, 3:4]).then_inc(m.exp_done, 1)
                    if t >= 1:
                        act.wait_ge(m.t_ready, t)
                        nc.scalar.activation(hth[:, (t - 1) % 2], TB[(t - 1) % 2][:, 0:P], ACT.Copy).then_inc(
                            m.t_hi, 1)

            @block.vector
            def _(dve):
                for i, (lo, raw, h) in enumerate(((bl, braw, bh), (sl, sraw, sh), (ul, uraw, uh))):
                    dve.wait_ge(m.hi_done, i + 1)
                    nc.vector.tensor_tensor(lo[:], raw[:], f32(h[:]), ALU.subtract).then_inc(m.lo_done, 1)
                dve.wait_ge(m.cst, 32)
                links = 0
                for t in range(NT + 2):
                    if t < NT:
                        s_, o_, p_ = small[:, t % 2], one[:, t % 2], pair[:, t % 2]
                        gb = GB[t % 2]
                        dve.wait_ge(m.g_ready, t + 1)
                        if thresholded:
                            nc.vector.tensor_scalar(o_[:, 1:2], gb[:, ER + NE:ER + NE + 1], thr[:], None,
                                                    ALU.add).then_inc(m.nmax, 1)
                        nc.vector.tensor_reduce(o_[:, 0:1], gb[:, ER:ER + NE], AX.X, ALU.max, negate=True).then_inc(
                            m.nmax, 1)
                        dve.wait_ge(m.exp_done, t + 1)
                        e = s_[:, 0]
                        if thresholded:
                            dve.wait_ge(m.thr_done, t + 1)
                            nc.vector.tensor_scalar(o_[:, 2:3], o_[:, 2:3], 1.0, 8.0, ALU.add, ALU.mult).then_inc(
                                m.link, 1)
                            dve.wait_ge(m.link, links + 1)
                            nc.vector.reciprocal(o_[:, 2:4], o_[:, 2:4]).then_inc(m.link, 1)
                            dve.wait_ge(m.link, links + 2)
                            nc.vector.tensor_scalar(s_[:, 1], e, o_[:, 3:4], o_[:, 2:3], ALU.mult,
                                                    ALU.subtract).then_inc(m.link, 1)
                            dve.wait_ge(m.link, links + 3)
                            nc.vector.tensor_scalar(s_[:, 2], s_[:, 1], 0.0, None, ALU.max).then_inc(
                                m.link, 1)
                            dve.wait_ge(m.link, links + 4)
                            nc.vector.tensor_reduce(o_[:, 4:5], s_[:, 2], AX.X, ALU.add).then_inc(m.link, 1)
                            dve.wait_ge(m.link, links + 5)
                            nc.vector.tensor_scalar(o_[:, 5:6], o_[:, 4:5], 0.0, None, ALU.is_equal).then_inc(
                                m.link, 1)
                            dve.wait_ge(m.link, links + 6)
                            nc.vector.tensor_scalar(o_[:, 4:5], o_[:, 4:5], o_[:, 5:6], 0.5, ALU.add,
                                                    ALU.mult).then_inc(m.link, 1)
                            dve.wait_ge(m.link, links + 7)
                            nc.vector.reciprocal(o_[:, 5:6], o_[:, 4:5]).then_inc(m.link, 1)
                            dve.wait_ge(m.link, links + 8)
                            nc.vector.tensor_scalar(s_[:, 3], s_[:, 2], o_[:, 5:6], None, ALU.mult).then_inc(
                                m.link, 1)
                            links += 9
                        else:
                            own = e.unsqueeze(2).to_broadcast([P, NE, NE])
                            other = e.unsqueeze(1).to_broadcast([P, NE, NE])
                            nc.vector.tensor_tensor(p_[:, 0], other, own, ALU.is_gt).then_inc(m.link, 1)
                            nc.vector.tensor_tensor(p_[:, 1], other, own, ALU.is_equal).then_inc(m.link, 1)
                            dve.wait_ge(m.link, links + 2)
                            nc.vector.tensor_tensor(p_[:, 1], p_[:, 1], first[:], ALU.mult).then_inc(
                                m.link, 1)
                            dve.wait_ge(m.link, links + 3)
                            nc.vector.tensor_tensor(p_[:, 0], p_[:, 0], p_[:, 1], ALU.add).then_inc(
                                m.link, 1)
                            dve.wait_ge(m.link, links + 4)
                            nc.vector.tensor_reduce(s_[:, 1], p_[:, 0], AX.X, ALU.add).then_inc(m.link, 1)
                            dve.wait_ge(m.link, links + 5)
                            nc.vector.scalar_tensor_tensor(s_[:, 2], s_[:, 1], 1.5, e, ALU.is_lt,
                                                           ALU.mult).then_inc(m.link, 1)
                            dve.wait_ge(m.link, links + 6)
                            nc.vector.tensor_reduce(o_[:, 4:5], s_[:, 2], AX.X, ALU.add).then_inc(m.link, 1)
                            dve.wait_ge(m.link, links + 7)
                            nc.vector.reciprocal(o_[:, 5:6], o_[:, 4:5]).then_inc(m.link, 1)
                            dve.wait_ge(m.link, links + 8)
                            nc.vector.tensor_scalar(s_[:, 3], s_[:, 2], o_[:, 5:6], None, ALU.mult).then_inc(
                                m.link, 1)
                            links += 9
                        dve.wait_ge(m.link, links)
                        if t >= 2:
                            dve.wait_ge(m.t_ready, t - 1)
                        nc.vector.tensor_tensor(hw[:, t % 2].rearrange("p (e r) -> p e r", e=NE),
                                                gb[:, 0:ER].rearrange("p (e r) -> p e r", e=NE),
                                                s_[:, 3].unsqueeze(2).to_broadcast([P, NE, RANK]),
                                                ALU.mult).then_inc(m.hw_done, 1)
                    if 1 <= t < NT + 1:
                        dve.wait_ge(m.t_hi, t)
                        nc.vector.tensor_tensor(htl[:, (t - 1) % 2], TB[(t - 1) % 2][:, 0:P],
                                                f32(hth[:, (t - 1) % 2]), ALU.subtract).then_inc(m.t_lo, 1)
                    if t >= 2:
                        dve.wait_ge(m.y_ready, t - 1)
                        nc.vector.tensor_tensor(k.acc[:, t - 2], YB[(t - 2) % 3][:], bias[:], ALU.add).then_inc(
                            m.link, 1)
                        links += 1

            @block.tensor
            def _(pe):
                def lift(t):
                    pe.wait_ge(m.t_lo, t + 1)
                    products(nc, YB[t % 3][:], [(hth[:, t % 2], htl[:, t % 2], uh[:], ul[:])], start=False).then_inc(
                        m.y_ready, 1)

                pe.wait_ge(m.lo_done, 3)
                for t in range(NT + 2):
                    if t < NT:
                        tok = slice(t * P, (t + 1) * P)
                        if t >= 2:
                            pe.wait_ge(m.hw_done, t - 1)
                        products(nc, GB[t % 2][:, 0:SMALL], [(k.xh[:, kt, tok], k.xl[:, kt, tok], sh[:, kt], sl[:, kt])
                                                             for kt in range(KT)]).then_inc(m.g_ready, 1)
                        if t >= 3:
                            pe.wait_ge(m.link, LINKS * t + (t - 2))
                        products(nc, YB[t % 3][:], [(k.xh[:, kt, tok], k.xl[:, kt, tok], bh[:, kt], bl[:, kt])
                                                    for kt in range(KT)], stop=False)
                    if 1 <= t < NT + 1:
                        pe.wait_ge(m.hw_done, t)
                        if t >= 3:
                            pe.wait_ge(m.t_lo, t - 2)
                        nc.tensor.transpose(TB[(t - 1) % 2][:, 0:P], hw[:, (t - 1) % 2], k.ident[:]).then_inc(
                            m.t_ready, 1)
                    if t >= 2:
                        lift(t - 2)


L1_GROUPS = 4
QUAD = 4
ROUNDS = NH // L1_GROUPS // QUAD
WQ_AHEAD = 2


def l1_attention(k, tag, wq, wk, wv, wo, scale, anticausal=None, uniform=None, last_row=None, ctxT=None):
    nc = k.nc
    cross = ctxT is not None
    KEYS = S + CTX if cross else S
    NKV = 6 if cross else 4
    NVT = NT + B if cross else NT
    NG = 2 if cross else 1
    UR = QUAD * B
    PTW = 3 * S if cross else 2 * S

    with ExitStack() as ctx:
        def sb(name, shape, dt=F):
            return ctx.enter_context(nc.sbuf_tensor(f"{tag}_{name}", shape, dt))

        def sem(name):
            return ctx.enter_context(nc.semaphore(f"{tag}_{name}"))

        wqraw, woraw = sb("wqraw", [P, KT, HD]), sb("woraw", [P, D])
        kvraw = sb("kvraw", [P, 2, KT, HD])
        wqh, wql = sb("wqh", [P, 2, KT, HD], R), sb("wql", [P, 2, KT, HD], R)
        woh, wol = sb("woh", [P, QUAD, D], R), sb("wol", [P, QUAD, D], R)
        wkvh, wkvl = sb("wkvh", [P, 2, KT, HD], R), sb("wkvl", [P, 2, KT, HD], R)
        kh, kl = sb("kh", [P, B, KEYS], R), sb("kl", [P, B, KEYS], R)
        vh, vl = sb("vh", [P, NVT, HD], R), sb("vl", [P, NVT, HD], R)
        qh, ql = sb("qh", [P, 2, TOK], R), sb("ql", [P, 2, TOK], R)
        pb = sb("pb", [P, 2, 2, KEYS])
        pth, ptl = sb("pth", [P, 2, PTW], R), sb("ptl", [P, 2, PTW], R)
        oh, ol = sb("oh", [P, QUAD, TOK], R), sb("ol", [P, QUAD, TOK], R)
        nmax, rsum, rinv = sb("nmax", [P, 2, 2]), sb("rsum", [P, 2, 2]), sb("rinv", [P, 2, 2])
        if cross:
            ctx_raw = sb("ctx_raw", [P, KT, B * CTX])
            ch, cl = sb("ch", [P, KT, B * CTX], R), sb("cl", [P, KT, B * CTX], R)
        else:
            mask_f, mask = sb("mask_f", [P, 2, P]), sb("mask", [P, 2, P], R)
            uni_f = sb("uni_f", [P, P])
            fix, rfirst = sb("fix", [P, 2]), sb("rfirst", [P, 2, 2])
        SB, TB, QB, OB = k.ps[0:2], k.ps[2:4], k.ps[4:6], k.ps[6:8]

        names = ("wq_in wo_in kv_in cst cst_low cst_split kvw_split wq_split wo_split kv_ready kv_hi kv_lo q_ready "
                 "q_hi q_lo s_ready max_done exp_done inv_first inv_done p_done t_ready t_hi t_lo o_ready o_hi o_lo "
                 "y_ready y_done link vt_ready vt_done")
        m = namedtuple("Sems", names)(*map(sem, names.split()))

        if cross:
            blocks = [(P, 4 * P, [(q, t * P, t * S + q * P) for t in range(2) for q in range(2)]),
                      (CTX, S, [(q, S, q * P) for q in range(2)])]
        else:
            blocks = [(P, 3 * P, [(0, P, 0), (1, P, P), (0, 0, 2 * P)])]

        def pt_part(t, u, g):
            rows, width, _ = blocks[g]
            return t[0:rows, u % 2, g * 4 * P:g * 4 * P + width]

        def t_bank(u, g):
            rows, width, _ = blocks[g]
            return TB[g if cross else u % 2][0:rows, 0:width]

        def kv_parts():
            for i in range(2):
                yield (TB[i][:].rearrange("p (b s) -> p b s", b=2), kh[:, 2 * i:2 * i + 2, 0:S],
                       kl[:, 2 * i:2 * i + 2, 0:S])
            if cross:
                yield (OB[0][:, 0:B * CTX].rearrange("p (b s) -> p b s", b=B), kh[:, :, S:], kl[:, :, S:])
            for i in range(2):
                yield (SB[i][:].rearrange("p (t d) -> p t d", t=4), vh[:, 4 * i:4 * i + 4], vl[:, 4 * i:4 * i + 4])
            if cross:
                yield (OB[1][0:CTX, :].rearrange("p (t d) -> p t d", t=B), vh[0:CTX, NT:], vl[0:CTX, NT:])

        v_rows = pb[:].rearrange("p a b n -> p (a b n)")
        v_parts = [(SB[0][:], 0, 512), (SB[1][:], 512, 1024)] + (
            [(OB[1][:, 0:B * CTX], TOK, TOK + B * CTX)] if cross else [])
        NVP = len(v_parts)

        def score_bank(u, q):
            return (SB[q][:, 0:KEYS], 0) if cross else (SB[u % 2][:, q * S:(q + 1) * S], q * P)

        ctx.callback(clear, nc, m)
        block = ctx.enter_context(nc.Block())

        @block.sync
        def _(sp):
            sp.dma_start(wqraw[:], wq[0]).then_inc(m.wq_in, 16)
            for i, w in enumerate((wk, wv)):
                sp.dma_start(kvraw[:, i], w[0]).then_inc(m.kv_in, 16)
            pairs = ((ctx_raw[:], ctxT),) if cross else ((mask_f[:, 0], anticausal), (mask_f[:, 1], anticausal),
                                                             (uni_f[:], uniform), (fix[:], last_row))
            for dst, src in pairs:
                sp.dma_start(dst, src).then_inc(m.cst, 16)
            sp.wait_ge(m.wq_split, 1)
            sp.dma_start(wqraw[:], wq[1]).then_inc(m.wq_in, 16)
            with nc.sync.Fori(0, L1_GROUPS) as g:
                sp.wait_ge(m.kvw_split, g + 1)
                for i, w in enumerate((wk, wv)):
                    sp.dma_start(kvraw[:, i], w[bass.ds(g + 1, 1)].rearrange("a p k n -> (a p) k n")).then_inc(
                        m.kv_in, 16)
                with nc.sync.Fori(0, NH // L1_GROUPS) as i:
                    h = g * (NH // L1_GROUPS) + i
                    sp.wait_ge(m.wo_split, h + 1)
                    sp.dma_start(woraw[:], wo[bass.ds(h, 1)].rearrange("a p n -> (a p) n")).then_inc(
                        m.wo_in, 16)
                    sp.wait_ge(m.wq_split, h + 2)
                    sp.dma_start(wqraw[:], wq[bass.ds(h + 2, 1)].rearrange("a p k n -> (a p) k n")).then_inc(
                        m.wq_in, 16)

        @block.gpsimd
        def _(pool):
            nc.gpsimd.memset(k.acc[:], 0.0).then_inc(m.wo_split, 1)

            def split_kv(link):
                high_part(k, wkvh[:], kvraw[:]).then_inc(m.link, 1)
                pool.wait_ge(m.link, link)
                nc.gpsimd.tensor_tensor(wkvl[:], kvraw[:], f32(wkvh[:]), ALU.subtract).then_inc(
                    m.kvw_split, 1)

            pool.wait_ge(m.kv_in, 32)
            split_kv(1)
            with nc.gpsimd.Fori(0, L1_GROUPS) as g:
                with nc.gpsimd.Fori(0, ROUNDS) as s:
                    r = g * ROUNDS + s
                    for u in range(UR):
                        h, b = divmod(u, B)
                        pool.wait_ge(m.inv_done, r * UR + u + 1)
                        for q, lo in (((0, 0), (1, P)) if not cross else ((None, 0),)):
                            pv = pb[:, u % 2] if cross else pb[:, u % 2, q, lo:]
                            rv = rinv[:, u % 2] if cross else rinv[:, u % 2, q:q + 1]
                            if cross:
                                last = nc.gpsimd.tensor_tensor(pv, pv, rv.unsqueeze(2).to_broadcast([P, 2, KEYS]),
                                                               ALU.mult)
                            else:
                                last = nc.gpsimd.tensor_tensor(pv, pv, rv.to_broadcast([P, S - lo]), ALU.mult)
                        last.then_inc(m.p_done, 1)
                        H = r * QUAD + h
                        if b < 2:
                            if b == 0:
                                pool.wait_ge(m.wq_in, 16 * H + 48)
                                pool.wait_ge(m.q_ready, 2 * H + 2)
                            kts = slice(2 * b, 2 * b + 2)
                            raw, high, low = wqraw[:, kts], wqh[:, h % 2, kts], wql[:, h % 2, kts]
                            done = m.wq_split
                        else:
                            if b == 2:
                                pool.wait_ge(m.wo_in, 16 * H + 16)
                            cols = slice((b - 2) * 2 * P, (b - 1) * 2 * P)
                            raw, high, low, done = woraw[:, cols], woh[:, h, cols], wol[:, h, cols], m.wo_split
                        high_part(k, high, raw).then_inc(m.link, 1)
                        pool.wait_ge(m.link, r * UR + u + g + 2)
                        last = nc.gpsimd.tensor_tensor(low, raw, f32(high), ALU.subtract)
                        if b % 2:
                            last.then_inc(done, 1)
                pool.wait_ge(m.kv_in, 32 * g + 64)
                pool.wait_ge(m.kv_ready, NKV * (g + 1))
                high_part(k, wkvh[:], kvraw[:]).then_inc(m.link, 1)
                pool.wait_ge(m.link, (g + 1) * ROUNDS * UR + g + 2)
                nc.gpsimd.tensor_tensor(wkvl[:], kvraw[:], f32(wkvh[:]), ALU.subtract).then_inc(
                    m.kvw_split, 1)

        @block.scalar
        def _(act):
            for i in range(2):
                act.wait_ge(m.wq_in, 16 * (i + 1))
                nc.scalar.activation(wqh[:, i], wqraw[:], ACT.Copy).then_inc(m.cst_split, 1)
            act.wait_ge(m.cst, 16 if cross else 64)
            for dst, src in (((ch[:], ctx_raw[:]),) if cross else ((mask[:], mask_f[:]), (pth[:, 0, 3 * P:], uni_f[:]),
                                                                   (pth[:, 1, 3 * P:], uni_f[:]))):
                nc.scalar.activation(dst, src, ACT.Copy).then_inc(m.cst_split, 1)

            def query(H, i, par):
                act.wait_ge(m.q_ready, 2 * H + i + 1)
                nc.scalar.activation(qh[:, par, i * 512:(i + 1) * 512], QB[i][:], ACT.Copy).then_inc(
                    m.q_hi, 1)

            for i in range(2):
                query(0, i, 0)
            with nc.scalar.Fori(0, L1_GROUPS) as g:
                for i, (bank, high, low) in enumerate(kv_parts()):
                    act.wait_ge(m.kv_ready, NKV * g + i + 1)
                    nc.scalar.activation(high, bank, ACT.Copy, scale=scale if i < NKV // 2 else 1.0).then_inc(
                        m.kv_hi, 1)
                    if i == 1:
                        for j in range(0, NVP, 2):
                            bank, lo, hi = v_parts[j]
                            act.wait_ge(m.vt_ready, NVP * g + j + 1)
                            nc.scalar.activation(v_rows[:, lo:hi], bank, ACT.Copy).then_inc(m.vt_done, 1)
                with nc.scalar.Fori(0, ROUNDS) as s:
                    r = g * ROUNDS + s

                    def transposed(u):
                        for j in range(NG):
                            act.wait_ge(m.t_ready, (r * UR + u) * NG + j + 1)
                            if u >= 2 and j == 0:
                                act.wait_ge(m.o_ready, r * UR + u - 1)
                            nc.scalar.activation(pt_part(pth, u, j), t_bank(u, j), ACT.Copy).then_inc(
                                m.t_hi, 1)

                    def attended(u):
                        h, b = divmod(u, B)
                        act.wait_ge(m.o_ready, r * UR + u + 1)
                        nc.scalar.activation(oh[:, h, b * S:(b + 1) * S], OB[u % 2][:, 0:S], ACT.Copy).then_inc(
                            m.o_hi, 1)

                    for u in range(UR):
                        h, b = divmod(u, B)
                        for q in range(2):
                            bank, lo = score_bank(u, q)
                            act.wait_ge(m.max_done, (r * UR + u) * 2 + (q + 1 if cross else 2))
                            if u >= 2 and q == 0:
                                act.wait_ge(m.t_ready, (r * UR + u - 1) * NG)
                            nc.scalar.activation(pb[:, u % 2, q, lo:], bank[:, lo:], ACT.Exp,
                                                 bias=nmax[:, u % 2, q:q + 1],
                                                 accum_out=rsum[:, u % 2, q:q + 1]).then_inc(m.exp_done, 1)
                        if b % 2:
                            query(r * QUAD + h + 1, b // 2, (h + 1) % 2)
                        if u >= 1:
                            transposed(u - 1)
                        if u >= 2:
                            attended(u - 2)
                    attended(UR - 2)
                    transposed(UR - 1)
                    attended(UR - 1)

        @block.vector
        def _(dve):
            nc.vector.memset(rsum[:], 1.0).then_inc(m.y_done, 1)
            for i in range(2):
                dve.wait_ge(m.cst_split, i + 1)
                nc.vector.tensor_tensor(wql[:, i], wqraw[:], f32(wqh[:, i]), ALU.subtract).then_inc(
                    m.wq_split, 1)
            if cross:
                dve.wait_ge(m.cst_split, 3)
                nc.vector.tensor_tensor(cl[:], ctx_raw[:], f32(ch[:]), ALU.subtract).then_inc(m.cst_low, 1)
            else:
                nc.vector.memset(f32(ptl[:, :, 3 * P:]), 0.0).then_inc(m.cst_low, 1)

            def query(H, i, par):
                dve.wait_ge(m.q_hi, 2 * H + i + 1)
                cols = slice(i * 512, (i + 1) * 512)
                nc.vector.tensor_tensor(ql[:, par, cols], QB[i][:], f32(qh[:, par, cols]), ALU.subtract).then_inc(
                    m.q_lo, 1)

            for i in range(2):
                query(0, i, 0)
            with nc.vector.Fori(0, L1_GROUPS) as g:
                for i, (bank, high, low) in enumerate(kv_parts()):
                    dve.wait_ge(m.kv_hi, NKV * g + i + 1)
                    if i < NKV // 2:
                        for b in range(high.shape[1]):
                            last = nc.vector.scalar_tensor_tensor(low[:, b], bank[:, b], scale, f32(high[:, b]),
                                                                  ALU.mult, ALU.subtract)
                        last.then_inc(m.kv_lo, 1)
                    else:
                        nc.vector.tensor_tensor(low, bank, f32(high), ALU.subtract).then_inc(m.kv_lo, 1)
                    if i == 0:
                        bank, lo, hi = v_parts[1]
                        dve.wait_ge(m.vt_ready, NVP * g + 2)
                        nc.vector.tensor_copy(v_rows[:, lo:hi], bank).then_inc(m.vt_done, 1)
                with nc.vector.Fori(0, ROUNDS) as s:
                    r = g * ROUNDS + s

                    def transposed(u):
                        for j in range(NG):
                            dve.wait_ge(m.t_hi, (r * UR + u) * NG + j + 1)
                            nc.vector.tensor_tensor(pt_part(ptl, u, j), t_bank(u, j), f32(pt_part(pth, u, j)),
                                                    ALU.subtract).then_inc(m.t_lo, 1)

                    def attended(u):
                        h, b = divmod(u, B)
                        dve.wait_ge(m.o_hi, r * UR + u + 1)
                        cols = slice(b * S, (b + 1) * S)
                        nc.vector.tensor_tensor(ol[:, h, cols], OB[u % 2][:, 0:S], f32(oh[:, h, cols]),
                                                ALU.subtract).then_inc(m.o_lo, 1)

                    def projected(t):
                        dve.wait_ge(m.y_ready, r * NT + t + 1)
                        nc.vector.tensor_tensor(k.acc[:, t], SB[t % 2][:], k.acc[:, t], ALU.add).then_inc(
                            m.y_done, 1)

                    for u in range(UR):
                        h, b = divmod(u, B)
                        for q in range(2):
                            bank, lo = score_bank(u, q)
                            dve.wait_ge(m.s_ready, (r * UR + u) * 2 + (q + 1 if cross else 2))
                            nc.vector.tensor_reduce(nmax[:, u % 2, q:q + 1], bank[:, lo:], AX.X, ALU.max,
                                                    negate=True).then_inc(m.max_done, 1)
                        if b % 2:
                            query(r * QUAD + h + 1, b // 2, (h + 1) % 2)
                        if u >= 1:
                            transposed(u - 1)
                        dve.wait_ge(m.exp_done, (r * UR + u) * 2 + 2)
                        if cross:
                            nc.vector.reciprocal(rinv[:, u % 2], rsum[:, u % 2]).then_inc(m.inv_done, 1)
                        else:
                            nc.vector.reciprocal(rfirst[:, u % 2], rsum[:, u % 2]).then_inc(m.inv_first, 1)
                            dve.wait_ge(m.inv_first, r * UR + u + 1)
                            nc.vector.tensor_tensor(rinv[:, u % 2], rfirst[:, u % 2], fix[:], ALU.mult).then_inc(
                                m.inv_done, 1)
                        if u >= 2:
                            attended(u - 2)
                    attended(UR - 2)
                    projected(0)
                    projected(1)
                    transposed(UR - 1)
                    projected(2)
                    projected(3)
                    attended(UR - 1)
                    for t in range(4, NT):
                        projected(t)

        @block.tensor
        def _(pe):
            def query(H, i, par, kts=range(KT)):
                if kts[0] == 0:
                    pe.wait_ge(m.wq_split, H + 1)
                cols = slice(i * 512, (i + 1) * 512)
                last = products(nc, QB[i][:], [(wqh[:, par, kt], wql[:, par, kt], k.xh[:, kt, cols], k.xl[:, kt, cols])
                                               for kt in kts], start=kts[0] == 0, stop=kts[-1] == KT - 1)
                if kts[-1] == KT - 1:
                    last.then_inc(m.q_ready, 1)

            for i in range(2):
                query(0, i, 0)
            pe.wait_ge(m.cst_low, 1)
            pe.wait_ge(m.cst_split, 3 if cross else 5)
            with nc.tensor.Fori(0, L1_GROUPS) as g:
                pe.wait_ge(m.kvw_split, g + 1)
                pe.wait_ge(m.y_done, g * ROUNDS * NT + 1)
                for i in range(2):
                    cols = slice(i * 512, (i + 1) * 512)
                    products(nc, TB[i][:], [(wkvh[:, 0, kt], wkvl[:, 0, kt], k.xh[:, kt, cols], k.xl[:, kt, cols])
                                            for kt in range(KT)]).then_inc(m.kv_ready, 1)
                for i in range(2):
                    cols = slice(i * 512, (i + 1) * 512)
                    products(nc, v_parts[i][0], [(wkvh[:, 1, kt], wkvl[:, 1, kt], k.xh[:, kt, cols],
                                                  k.xl[:, kt, cols]) for kt in range(KT)]).then_inc(m.vt_ready, 1)
                if cross:
                    for which, bank, done in ((0, OB[0][:, 0:B * CTX], m.kv_ready), (1, v_parts[2][0], m.vt_ready)):
                        products(nc, bank, [(wkvh[:, which, kt], wkvl[:, which, kt], ch[:, kt], cl[:, kt])
                                            for kt in range(KT)]).then_inc(done, 1)
                pe.wait_ge(m.vt_done, NVP * (g + 1))
                for i in range(2):
                    for t in range(4):
                        at = (4 * i + t) * P
                        last = nc.tensor.transpose(SB[i][:, t * HD:(t + 1) * HD], v_rows[:, at:at + P], k.ident[:])
                    last.then_inc(m.kv_ready, 1)
                if cross:
                    for b in range(B):
                        at = TOK + b * CTX
                        last = nc.tensor.transpose(OB[1][0:CTX, b * HD:(b + 1) * HD], v_rows[:, at:at + CTX],
                                                   k.ident[:])
                    last.then_inc(m.kv_ready, 1)
                with nc.tensor.Fori(0, ROUNDS) as s:
                    r = g * ROUNDS + s

                    def scores(u):
                        h, b = divmod(u, B)
                        if b % 2 == 0:
                            pe.wait_ge(m.q_lo, (r * QUAD + h) * 2 + b // 2 + 1)
                        for q in range(2):
                            if u == 0 and q == 0:
                                pe.wait_ge(m.y_done, r * NT + 1)
                            elif cross and u:
                                pe.wait_ge(m.exp_done, (r * UR + u - 1) * 2 + q + 1)
                            elif u >= 2 and q == 0:
                                pe.wait_ge(m.exp_done, (r * UR + u - 1) * 2)
                            tok = slice(b * S + q * P, b * S + (q + 1) * P)
                            if q == 0 and not cross:
                                diagonal = SB[u % 2][:].rearrange("p (c n) -> p c n", n=P)[:, 0:4:3]
                                nc.tensor.matmul(diagonal, k.ident_r[:], mask[:], start=True, stop=False,
                                                 skip_group_check=True)
                            products(nc, score_bank(u, q)[0], [(qh[:, h % 2, tok], ql[:, h % 2, tok],
                                                                kh[:, b], kl[:, b])], start=cross,
                                     cover=not cross).then_inc(m.s_ready, 1)

                    def transpose(u):
                        pe.wait_ge(m.p_done, r * UR + u + 1)
                        if cross and u >= 1:
                            pe.wait_ge(m.t_lo, (r * UR + u) * NG)
                        elif not cross and u >= 2:
                            pe.wait_ge(m.t_lo, r * UR + u - 1)
                        for j, (rows, width, parts) in enumerate(blocks):
                            for q, key, at in parts:
                                last = nc.tensor.transpose(t_bank(u, j)[:, at:at + P],
                                                           pb[:, u % 2, q, key:key + rows], k.ident[:])
                            last.then_inc(m.t_ready, 1)

                    def attend(u):
                        h, b = divmod(u, B)
                        pe.wait_ge(m.t_lo, (r * UR + u + 1) * NG)
                        if u >= 2:
                            pe.wait_ge(m.o_lo, r * UR + u - 1)
                        out = OB[u % 2][:, 0:S]
                        ph, pl = pth[:, u % 2], ptl[:, u % 2]
                        if cross:
                            v, o = vh, vl
                            last = products(nc, out, [
                                (vh[:, 2 * b], vl[:, 2 * b], ph[:, 0:S], pl[:, 0:S]),
                                (vh[:, 2 * b + 1], vl[:, 2 * b + 1], ph[:, S:2 * S], pl[:, S:2 * S]),
                                (vh[0:CTX, NT + b], vl[0:CTX, NT + b], ph[0:CTX, 2 * S:], pl[0:CTX, 2 * S:])])
                        else:
                            last = products(nc, out, [
                                (vh[:, 2 * b + 1], vl[:, 2 * b + 1], ph[:, 0:S], pl[:, 0:S]),
                                (vh[:, 2 * b], vl[:, 2 * b], ph[:, S:2 * S], pl[:, S:2 * S])])
                        last.then_inc(m.o_ready, 1)

                    def project(t):
                        pe.wait_ge(m.o_lo, r * UR + UR - B + t // 2 + 1)
                        pe.wait_ge(m.exp_done, (r * UR + UR) * 2)
                        if t >= 2:
                            pe.wait_ge(m.y_done, r * NT + t)
                        products(nc, SB[t % 2][:], [(oh[:, h, t * P:(t + 1) * P], ol[:, h, t * P:(t + 1) * P],
                                                     woh[:, h], wol[:, h]) for h in range(QUAD)]).then_inc(
                            m.y_ready, 1)

                    pe.wait_ge(m.kv_lo, NKV * (g + 1))
                    for u in range(UR):
                        h, b = divmod(u, B)
                        scores(u)
                        if b % 2 == 0:
                            pe.wait_ge(m.q_lo, (r * QUAD + h) * 2 + b // 2 + 1)
                        query(r * QUAD + h + 1, b // 2, (h + 1) % 2, range(0, 2) if b % 2 == 0 else range(2, KT))
                        if u >= 1:
                            transpose(u - 1)
                        if u >= 2:
                            attend(u - 2)
                    attend(UR - 2)
                    pe.wait_ge(m.wo_split, (r + 1) * QUAD + 1)
                    project(0)
                    project(1)
                    transpose(UR - 1)
                    project(2)
                    project(3)
                    attend(UR - 1)
                    for t in range(4, NT):
                        project(t)


def build(nc, a, out, stages=6):
    with ExitStack() as ctx:
        def sb(name, shape, dt=F):
            return ctx.enter_context(nc.sbuf_tensor(name, shape, dt))

        k = Core()
        k.nc = nc
        k.x, k.acc = sb("x", [P, NT, D]), sb("acc", [P, NT, D])
        k.xh, k.xl = sb("xT_high", [P, KT, TOK], R), sb("xT_low", [P, KT, TOK], R)
        k.ident, k.ident_r, k.half = sb("ident", [P, P]), sb("ident_r", [P, P], R), sb("minus_half", [P, 1])
        k.one = sb("one", [P, 1])
        k.ps = [ctx.enter_context(nc.psum_tensor(f"bank{i}", [P, 512], F)) for i in range(8)]
        k.ident_in = a["identity"]
        with nc.Block() as block:
            @block.vector
            def _(dve):
                nc.vector.memset(k.half[:], -0.5)
                nc.vector.memset(k.one[:], 1.0)
        l0_self_attention(k, a["x"], a["xT"], a["a0_wq"], a["a0_bq"], a["a0_wk"], a["a0_bk"], a["a0_wv"], a["a0_bv"],
                          a["a0_wo"], a["a0_bo"], a["headmask"], a["causal4"])
        if stages == 1:
            return norm_stage(k, "n1", keep_T=False, out=out)
        norm_stage(k, "n2")
        l0_cross_attention(k, a["ctxT"], a["x0_wk"], a["x0_wq"], a["x0_wv"], a["x0_wo"], a["x0_q_norm"],
                           a["x0_k_norm"], a["x0_mask"])
        if stages == 2:
            return norm_stage(k, "n3", keep_T=False, out=out)
        norm_stage(k, "n4")
        mixture(k, "f0", a["f0_base"], a["f0_bias"], a["f0_small"], a["f0_up"], before=a["before"])
        if stages == 3:
            return norm_stage(k, "n5", keep_T=False, out=out)
        norm_stage(k, "n6")
        l1_attention(k, "a1", a["a1_wq"], a["a1_wk"], a["a1_wv"], a["a1_wo"], HD ** -0.5,
                     anticausal=a["anticausal"], uniform=a["uniform"], last_row=a["last_row"])
        if stages == 4:
            return norm_stage(k, "n7", keep_T=False, out=out)
        norm_stage(k, "n8")
        l1_attention(k, "x1", a["x1_wq"], a["x1_wk"], a["x1_wv"], a["x1_wo"], HD ** -0.5, ctxT=a["ctxT"])
        if stages == 5:
            return norm_stage(k, "n9", keep_T=False, out=out)
        norm_stage(k, "n10")
        mixture(k, "f1", a["f1_base"], a["f1_bias"], a["f1_small"], a["f1_up"], b_thr=a["f1_thr"])
        norm_stage(k, "n11", keep_T=False, out=out)


def kernel(**inputs):
    import numpy as np
    import concourse.bacc as bacc
    from concourse.bass_utils import run_bass_kernel_spmd

    arrays = layouts(np, inputs)
    nc = bacc.Bacc("TRN2", target_bir_lowering=False, num_devices=1)
    args = {n: nc.dram_tensor("in_" + n, v.shape, mybir.dt.from_np(v.dtype), kind="ExternalInput").ap()
            for n, v in arrays.items()}
    out = nc.dram_tensor("out", (TOK, D), F, kind="ExternalOutput").ap()
    build(nc, args, out)
    r = run_bass_kernel_spmd(nc, [{"in_" + n: v for n, v in arrays.items()}], core_ids=[0])
    return r.results[0]["out"].reshape(B, S, D)


def layouts(np, i):
    def parts(w):
        return np.ascontiguousarray(w.reshape(KT, P, -1).transpose(1, 0, 2))

    i = {n: np.asarray(v) for n, v in i.items()}
    x = i["x"].reshape(TOK, D)
    a = {"x": x, "xT": parts(x.T), "identity": np.eye(P, dtype=np.float32)}
    a["a0_wq"] = parts(i["L0_attn_wq_w"].T)
    a["a0_bq"] = np.ascontiguousarray(i["L0_attn_wq_b"].reshape(NCH, P).T)
    for n in "kv":
        a[f"a0_w{n}"] = parts(np.tile(i[f"L0_attn_w{n}_w"], (HPC, 1)).T)
        a[f"a0_b{n}"] = np.tile(i[f"L0_attn_w{n}_b"], HPC).reshape(P, 1)
    a["a0_wo"] = parts(i["L0_attn_wo_w"].T)
    a["a0_bo"] = i["L0_attn_wo_b"]
    a["headmask"] = np.kron(np.eye(HPC), np.ones((HD0, 1))).astype(np.float32)
    later = np.triu(np.ones((P, P)), 1)
    a["causal4"] = np.ascontiguousarray(np.repeat((later * MASKED).astype(np.float32)[:, None], 4, 1))
    c = i["ctx_4096"].reshape(B * CTX, D)
    a["ctxT"] = parts(c.T)

    def heads(w, n, spare):
        h = w.reshape(KT, P, n, HD).transpose(2, 1, 0, 3)
        return np.ascontiguousarray(np.concatenate([h, h[:spare]]))

    a["x0_wk"] = parts(i["L0_xattn_Wk"].T)
    a["x0_wq"] = heads(i["L0_xattn_Wq"].T, NH, X0_AHEAD)
    a["x0_wv"] = parts(i["L0_xattn_Wv"].T)
    wo = np.ascontiguousarray(i["L0_xattn_Wo"].T).reshape(NH, HD, D)
    a["x0_wo"] = np.concatenate([wo, wo[:2]])
    a["x0_q_norm"] = i["L0_xattn_q_norm_w"].reshape(HD, 1)
    a["x0_k_norm"] = i["L0_xattn_k_norm_w"].reshape(HD, 1)
    a["x0_mask"] = i["mask_1x1xSxS2_ff0"].reshape(S, CTX)
    for t, n in (("a1", "L1_attn"), ("x1", "L1_xattn")):
        a[t + "_wq"] = heads(i[n + "_Wq"], NH, WQ_AHEAD)
        a[t + "_wk"] = heads(i[n + "_Wk"], L1_GROUPS, 1)
        a[t + "_wv"] = heads(i[n + "_Wv"], L1_GROUPS, 1)
        a[t + "_wo"] = i[n + "_Wo"].reshape(NH, HD, D)
    a["anticausal"] = (np.tril(np.ones((P, P))) * MASKED).astype(np.float32)
    a["uniform"] = np.zeros((P, P), np.float32)
    a["uniform"][:, P - 1] = 1 / S
    a["last_row"] = np.ones((P, 2), np.float32)
    a["last_row"][P - 1, 1] = P / S
    a["before"] = np.repeat(np.tril(np.ones((NE, NE), np.float32), -1)[None], P, 0)

    def small(A, gate, *thr):
        cols = [A.reshape(ER, D).T, gate.T] + [t.reshape(D, 1) for t in thr]
        have = sum(c.shape[1] for c in cols)
        return parts(np.concatenate(cols + [np.zeros((D, ER + GATE - have), np.float32)], 1))

    def up(w):
        return np.ascontiguousarray(w.transpose(0, 2, 1)).reshape(ER, D)

    a["f0_base"], a["f0_bias"] = parts(i["L0_ffn_W_base"].T), i["L0_ffn_b_base"]
    a["f0_small"], a["f0_up"] = small(i["L0_ffn_A"], i["L0_ffn_W_gate"]), up(i["L0_ffn_B"])
    a["f1_base"], a["f1_bias"] = parts(i["L1_ffn_W_base"].T), i["L1_ffn_b_base"]
    a["f1_small"] = small(i["L1_ffn_A_w"], i["L1_ffn_W_gate"], i["L1_ffn_W_thr"])
    a["f1_up"], a["f1_thr"] = up(i["L1_ffn_B_w"]), i["L1_ffn_b_thr"]
    return a
```

```python
from collections import namedtuple
from contextlib import ExitStack

import concourse.bass as bass
from concourse import mybir

F = mybir.dt.float32
R = mybir.dt.float32r
ALU = mybir.AluOpType
ACT = mybir.ActivationFunctionType
AX = mybir.AxisListType

P = 128
B, S, D = 4, 256, 512
TOK = B * S
NT = TOK // P
KT = D // P
CTX = 64
HD = 128
NH = 32
NE, RANK = 8, 16
ER = NE * RANK
GATE = NE + 2
EPS = 1e-5
MASKED = -1e30


def f32(ap):
    return ap.bitcast(F)


def products(nc, out, terms, start=True, stop=True, cover=False):
    passes = []
    for lh, ll, rh, rl in terms:
        passes += [(lh, rh)] + ([(lh, rl)] if rl is not None else []) + ([(ll, rh)] if ll is not None else [])
    for i, (lhsT, rhs) in enumerate(passes):
        last = nc.tensor.matmul(out, lhsT, rhs, start=start and i == 0, stop=stop and i == len(passes) - 1,
                                skip_group_check=cover)
    return last


class Core:
    pass


def high_part(k, out, raw):
    one = k.one[:]
    while len(one.shape) < len(raw.shape):
        one = one.unsqueeze(1)
    return k.nc.gpsimd.tensor_tensor(out, raw, one.to_broadcast(list(raw.shape)), ALU.mult)


def clear(nc, sems):
    with nc.Block() as block:
        @block.sync
        def _(sp):
            for s in sems:
                nc.sync.sem_clear(s)


HD0 = D // NH
NCH = D // P
HPC = NH // NCH
HALF = D // 2


def l0_self_attention(k, x_nat, xT, wq, bq, wk, bk, wv, bv, wo, bo, headmask, causal4):
    nc = k.nc
    UN = 6
    UB = UN * NCH
    units = [(c, v) for c in range(NCH) for v in range(UN)]

    with ExitStack() as ctx:
        def sb(name, shape, dt=F):
            return ctx.enter_context(nc.sbuf_tensor("a0_" + name, shape, dt))

        def sem(name):
            return ctx.enter_context(nc.semaphore("a0_" + name))

        wraw, woraw = sb("wraw", [P, KT, D]), sb("woraw", [P, KT, D])
        wqh, wql = sb("wqh", [P, KT, D], R), sb("wql", [P, KT, D], R)
        woh, wol = sb("woh", [P, KT, D], R), sb("wol", [P, KT, D], R)
        kvraw = sb("kvraw", [P, 2, KT, P])
        kvh, kvl = sb("kvh", [P, 2, KT, P], R), sb("kvl", [P, 2, KT, P], R)
        bias = sb("bias", [P, NCH + 2])
        bo_b = sb("bo_b", [P, D])
        hm = sb("hm", [P, HPC])
        caus_f, caus = sb("caus_f", [P, 4, P]), sb("caus", [P, 4, P], R)
        xraw = sb("xraw", [P, 2, KT, S])
        kf, kfh, kfl = sb("kf", [P, TOK]), sb("kfh", [P, TOK], R), sb("kfl", [P, TOK], R)
        kdh, kdl = sb("kdh", [P, HPC, S], R), sb("kdl", [P, HPC, S], R)
        STRIPS = 4
        vf, v_rows = sb("vf", [P, TOK]), sb("v_rows", [P, NT, STRIPS * HD0])
        vdh, vdl = sb("vdh", [P, 2, 2, P], R), sb("vdl", [P, 2, 2, P], R)
        qh, ql = sb("qh", [P, 2, S], R), sb("ql", [P, 2, S], R)
        nmax, rsum, rinv = sb("nmax", [P, 4, 4]), sb("rsum", [P, 4, 4]), sb("rinv", [P, 4, 4])
        pb = sb("pb", [P, 4, 4, P])
        pth, ptl = sb("pth", [P, 2, 4, P], R), sb("ptl", [P, 2, 4, P], R)
        oh, ol = sb("oh", [P, NCH, S], R), sb("ol", [P, NCH, S], R)
        SB, TB, OB, XB = k.ps[0:3], k.ps[3:5], k.ps[5:7], k.ps[7]

        STRIP = 2 * HD0

        def strips(t, odd):
            return t[:, :, odd].rearrange("p k (s r) -> p k s r", r=STRIP)[:, :, :, odd * HD0:(odd + 1) * HD0]

        def values(b):
            return v_rows[:, bass.ds(2 * b, 2)].rearrange("p k (s r) -> p k s r", r=HD0)

        def strip_parts(qt, c):
            for i in range(STRIPS):
                rows = slice(i * STRIP, (i + 1) * STRIP)
                yield OB[qt][rows, i * P:(i + 1) * P], rows, slice(qt * P, (qt + 1) * P)

        names = ("cst cst2 wq_in wo_in kv_in x0_in x1_in kv_hi kv_lo x_hi x_lo wq_hi wq_lo wo_hi wo_lo k_made v_made "
                 "kf_done kf_hi kf_lo vf_done vt_ready vt_out cst_split zeroed kd_hi kd_lo vd_hi vd_lo q_ready q_hi "
                 "q_lo s_ready max_done exp_done inv_done p_done t_ready t_hi t_lo o_ready o_hi o_lo y_ready y_done "
                 "bias_done")
        m = namedtuple("Sems", names)(*map(sem, names.split()))

        def shape_of(v):
            return (4 * v, 4, 0, P) if v < 2 else (2 * (v - 2), 2, 1, S)

        ctx.callback(clear, nc, m)
        block = ctx.enter_context(nc.Block())

        @block.sync
        def _(sp):
            sp.dma_start(kvraw[:, 0], wk).then_inc(m.kv_in, 16)
            sp.dma_start(kvraw[:, 1], wv).then_inc(m.kv_in, 16)
            x_in = (m.x0_in, m.x1_in)
            for i in range(2):
                sp.dma_start(xraw[:, i], xT[:, :, i * S:(i + 1) * S]).then_inc(x_in[i], 16)
            for dst, src in ((bias[:, 0:NCH], bq), (bias[:, NCH:NCH + 1], bk), (bias[:, NCH + 1:NCH + 2], bv),
                             (hm[:], headmask), (k.ident[:], k.ident_in), (caus_f[:], causal4)):
                sp.dma_start(dst, src).then_inc(m.cst, 16)
            for i in range(2):
                sp.wait_ge(m.x_lo, i + 1)
                sp.dma_start(xraw[:, i], xT[:, :, (2 + i) * S:(3 + i) * S]).then_inc(x_in[i], 16)
            sp.dma_start(wraw[:], wq).then_inc(m.wq_in, 16)
            sp.dma_start(woraw[:], wo).then_inc(m.wo_in, 16)
            for dst, src in ((bo_b[:], bo.partition_broadcast(P)),
                             (k.acc[:], x_nat.rearrange("(t p) d -> p t d", p=P))):
                sp.dma_start(dst, src).then_inc(m.cst2, 16)

        @block.gpsimd
        def _(pool):
            nc.gpsimd.memset(f32(vdh[:]), 0.0).then_inc(m.zeroed, 1)
            nc.gpsimd.memset(f32(vdl[:]), 0.0).then_inc(m.zeroed, 1)
            pool.wait_ge(m.wo_in, 16)
            high_part(k, woh[:], woraw[:]).then_inc(m.wo_hi, 1)
            pool.wait_ge(m.wo_hi, 1)
            nc.gpsimd.tensor_tensor(wol[:], woraw[:], f32(woh[:]), ALU.subtract).then_inc(m.wo_lo, 1)
            pool.wait_ge(m.cst2, 32)
            pool.wait_ge(m.cst, 96)
            pool.wait_ge(m.kf_lo, 2)
            with nc.gpsimd.Fori(0, B) as b:
                for i in range(2):
                    slots = slice(i * 4, (i + 1) * 4)
                    nc.gpsimd.tensor_tensor(
                        kdl[:, slots], f32(kfl[:, bass.ds(b * S, S)]).unsqueeze(1).to_broadcast([P, 4, S]),
                        hm[:, slots].unsqueeze(2).to_broadcast([P, 4, S]), ALU.mult).then_inc(m.kd_lo, 1)
                for u, (c, v) in enumerate(units):
                    j, n, qt, w = shape_of(v)
                    pool.wait_ge(m.inv_done, b * UB + u + 1)
                    pv = pb[:, u % 4].rearrange("p (n a) q -> p n (a q)", n=n)
                    nc.gpsimd.tensor_tensor(
                        pv, pv, rinv[:, u % 4, 0:n].unsqueeze(2).to_broadcast([P, n, w]), ALU.mult
                    ).then_inc(m.p_done, 1)
                    if u == 0:
                        own = k.acc[:, bass.ds(2 * b, 2), :]
                        nc.gpsimd.tensor_tensor(own, own, bo_b[:].unsqueeze(1).to_broadcast([P, 2, D]),
                                                ALU.add).then_inc(m.bias_done, 1)

        @block.scalar
        def _(act):
            act.wait_ge(m.kv_in, 32)
            nc.scalar.activation(kvh[:], kvraw[:], ACT.Copy).then_inc(m.kv_hi, 1)
            for i in range(B):
                act.wait_ge((m.x0_in, m.x1_in)[i % 2], 16 + i // 2 * 16)
                nc.scalar.activation(k.xh[:, :, i * S:(i + 1) * S], xraw[:, i % 2], ACT.Copy).then_inc(m.x_hi, 1)
            act.wait_ge(m.wq_in, 16)
            nc.scalar.activation(wqh[:], wraw[:], ACT.Copy).then_inc(m.wq_hi, 1)
            for i in range(2):
                act.wait_ge(m.kf_done, i + 1)
                nc.scalar.activation(kfh[:, i * 512:(i + 1) * 512], kf[:, i * 512:(i + 1) * 512],
                                     ACT.Copy).then_inc(m.kf_hi, 1)
            act.wait_ge(m.vt_ready, 1)
            nc.scalar.activation(v_rows[:], OB[0][:].rearrange("p (t n) -> p t n", t=NT), ACT.Copy).then_inc(
                m.vt_out, 1)
            act.wait_ge(m.cst, 96)
            nc.scalar.activation(caus[:], caus_f[:], ACT.Copy).then_inc(m.cst_split, 1)
            nc.scalar.activation(k.ident_r[:], k.ident[:], ACT.Copy).then_inc(m.cst_split, 1)
            act.wait_ge(m.zeroed, 2)
            act.wait_ge(m.kf_hi, 2)
            act.wait_ge(m.vt_out, 1)
            with nc.scalar.Fori(0, B) as b:
                for j in range(HPC):
                    last = nc.scalar.activation(kdh[:, j].unsqueeze(1), f32(kfh[:, bass.ds(b * S, S)]).unsqueeze(1),
                                                ACT.Copy, scale=hm[:, j:j + 1])
                    if j in (3, HPC - 1):
                        last.then_inc(m.kd_hi, 1)
                for odd in range(2):
                    last = nc.scalar.activation(strips(vdh, odd), values(b), ACT.Copy)
                last.then_inc(m.vd_hi, 1)

                def query(c):
                    act.wait_ge(m.q_ready, b * NCH + c + 1)
                    nc.scalar.activation(qh[:, c % 2], XB[:, 0:S], ACT.Identity, bias=bias[:, c:c + 1]).then_inc(
                        m.q_hi, 1)

                def transposed(u):
                    act.wait_ge(m.t_ready, b * UB + u + 1)
                    if u >= 2:
                        act.wait_ge(m.o_ready, b * UB + u - 1)
                    nc.scalar.activation(pth[:, u % 2], TB[u % 2][:].rearrange("p (n q) -> p n q", q=P),
                                         ACT.Copy).then_inc(m.t_hi, 1)

                def attended(c, qt):
                    act.wait_ge(m.o_ready, b * UB + UN * c + (2, UN)[qt])
                    for bank, rows, cols in strip_parts(qt, c):
                        last = nc.scalar.activation(oh[rows, c, cols], bank, ACT.Copy)
                    last.then_inc(m.o_hi, 1)

                query(0)
                for u in range(UB + 3):
                    if u < UB:
                        c, v = units[u]
                        j, n, qt, w = shape_of(v)
                        act.wait_ge(m.max_done, b * UB + u + 1)
                        if u >= 4:
                            act.wait_ge(m.t_ready, b * UB + u - 3)
                        for i in range(n):
                            pv = pb[:, u % 4].rearrange("p (n a) q -> p n (a q)", n=n)
                            last = nc.scalar.activation(
                                pv[:, i], SB[u % 3][:, i * w:(i + 1) * w], ACT.Exp, bias=nmax[:, u % 4, i:i + 1],
                                accum_out=rsum[:, u % 4, i:i + 1])
                        last.then_inc(m.exp_done, 1)
                    if 2 <= u < UB + 2:
                        transposed(u - 2)
                    if u < UB and u % UN == 0 and u // UN + 1 < NCH:
                        query(u // UN + 1)
                    if u >= 3 and (u - 3) % UN in (1, UN - 1):
                        attended((u - 3) // UN, (u - 3) % UN // 2 // 2)

        @block.vector
        def _(dve):
            nc.vector.memset(rsum[:], 1.0).then_inc(m.y_done, 1)
            dve.wait_ge(m.kv_hi, 1)
            nc.vector.tensor_tensor(kvl[:], kvraw[:], f32(kvh[:]), ALU.subtract).then_inc(m.kv_lo, 1)

            def x_low(i):
                dve.wait_ge(m.x_hi, i + 1)
                cols = slice(i * S, (i + 1) * S)
                nc.vector.tensor_tensor(k.xl[:, :, cols], xraw[:, i % 2], f32(k.xh[:, :, cols]),
                                        ALU.subtract).then_inc(m.x_lo, 1)

            def keys_and_values(i):
                cols = slice(i * 512, (i + 1) * 512)
                dve.wait_ge(m.k_made, i + 1)
                nc.vector.tensor_scalar(kf[:, cols], SB[i][:], bias[:, NCH:NCH + 1], HD0 ** -0.5, ALU.add,
                                        ALU.mult).then_inc(m.kf_done, 1)
                dve.wait_ge(m.v_made, i + 1)
                nc.vector.tensor_scalar(vf[:, cols], TB[i][:], bias[:, NCH + 1:NCH + 2], None,
                                        ALU.add).then_inc(m.vf_done, 1)

            for i in range(B):
                x_low(i)
            dve.wait_ge(m.cst, 96)
            keys_and_values(0)
            dve.wait_ge(m.wq_hi, 1)
            nc.vector.tensor_tensor(wql[:], wraw[:], f32(wqh[:]), ALU.subtract).then_inc(m.wq_lo, 1)
            keys_and_values(1)
            for i in range(2):
                dve.wait_ge(m.kf_hi, i + 1)
                cols = slice(i * 512, (i + 1) * 512)
                nc.vector.tensor_tensor(kfl[:, cols], kf[:, cols], f32(kfh[:, cols]), ALU.subtract).then_inc(
                    m.kf_lo, 1)
            dve.wait_ge(m.kf_lo, 2)
            dve.wait_ge(m.zeroed, 2)
            with nc.vector.Fori(0, B) as b:
                def query(c):
                    dve.wait_ge(m.q_hi, b * NCH + c + 1)
                    nc.vector.scalar_tensor_tensor(ql[:, c % 2], XB[:, 0:S], bias[:, c:c + 1], f32(qh[:, c % 2]),
                                                   ALU.add, ALU.subtract).then_inc(m.q_lo, 1)

                def inverse(u):
                    n = shape_of(units[u][1])[1]
                    dve.wait_ge(m.exp_done, b * UB + u + 1)
                    nc.vector.reciprocal(rinv[:, u % 4, 0:n], rsum[:, u % 4, 0:n]).then_inc(m.inv_done, 1)

                query(0)
                dve.wait_ge(m.vd_hi, b + 1)
                for odd in range(2):
                    last = nc.vector.tensor_tensor(strips(vdl, odd), values(b), f32(strips(vdh, odd)), ALU.subtract)
                last.then_inc(m.vd_lo, 1)
                for u in range(UB + 4):
                    if u < UB:
                        c, v = units[u]
                        j, n, qt, w = shape_of(v)
                        dve.wait_ge(m.s_ready, b * UB + u + 1)
                        nc.vector.tensor_reduce(nmax[:, u % 4, 0:n], SB[u % 3][:].rearrange("p (n w) -> p n w", n=n),
                                                AX.X, ALU.max, negate=True).then_inc(m.max_done, 1)
                    if 2 <= u < UB + 2:
                        inverse(u - 2)
                    if 3 <= u < UB + 3:
                        i = u - 3
                        dve.wait_ge(m.t_hi, b * UB + i + 1)
                        nc.vector.tensor_tensor(ptl[:, i % 2], TB[i % 2][:].rearrange("p (n q) -> p n q", q=P),
                                                f32(pth[:, i % 2]), ALU.subtract).then_inc(m.t_lo, 1)
                    if u < UB and u % UN == 1 and u // UN + 1 < NCH:
                        query(u // UN + 1)
                    if u >= 4 and (u - 4) % UN in (1, UN - 1):
                        c, qt = (u - 4) // UN, (u - 4) % UN // 2 // 2
                        dve.wait_ge(m.o_hi, (b * NCH + c) * 2 + qt + 1)
                        for bank, rows, cols in strip_parts(qt, c):
                            last = nc.vector.tensor_tensor(ol[rows, c, cols], bank, f32(oh[rows, c, cols]),
                                                           ALU.subtract)
                        last.then_inc(m.o_lo, 1)
                for t in range(2):
                    dve.wait_ge(m.y_ready, b * 2 + t + 1)
                    dve.wait_ge(m.bias_done, b + 1)
                    own = k.acc[:, bass.ds(b * 2 + t, 1), :]
                    nc.vector.tensor_tensor(own, (SB[0], SB[1])[t][:].unsqueeze(1), own, ALU.add).then_inc(
                        m.y_done, 1)

        @block.tensor
        def _(pe):
            pe.wait_ge(m.kv_lo, 1)
            for i in range(2):
                pe.wait_ge(m.x_lo, 2 * i + 2)
                for which, bank, made in ((0, SB[i], m.k_made), (1, TB[i], m.v_made)):
                    products(nc, bank[:], [(kvh[:, which, kt], kvl[:, which, kt], k.xh[:, kt, i * 512:(i + 1) * 512],
                                            k.xl[:, kt, i * 512:(i + 1) * 512]) for kt in range(KT)]).then_inc(made, 1)
            pe.wait_ge(m.vf_done, 2)
            rows = slice(0, STRIPS * HD0)
            for t in range(NT):
                last = nc.tensor.transpose(OB[0][:, t * STRIPS * HD0:(t + 1) * STRIPS * HD0],
                                           vf[rows, t * P:(t + 1) * P], k.ident[rows, rows])
            last.then_inc(m.vt_ready, 1)
            pe.wait_ge(m.wq_lo, 1)
            pe.wait_ge(m.cst_split, 2)
            with nc.tensor.Fori(0, B) as b:
                def query(c):
                    if c:
                        pe.wait_ge(m.q_lo, b * NCH + c)
                    products(nc, XB[:, 0:S], [(wqh[:, kt, c * P:(c + 1) * P], wql[:, kt, c * P:(c + 1) * P],
                                               k.xh[:, kt, bass.ds(b * S, S)], k.xl[:, kt, bass.ds(b * S, S)])
                                              for kt in range(KT)]).then_inc(m.q_ready, 1)

                def scores(u):
                    c, v = units[u]
                    j, n, qt, w = shape_of(v)
                    if v == 0:
                        pe.wait_ge(m.q_lo, b * NCH + c + 1)
                    if u < 2:
                        pe.wait_ge(m.kd_hi, 2 * b + u + 1)
                        pe.wait_ge(m.kd_lo, 2 * b + u + 1)
                    if u >= 3:
                        pe.wait_ge(m.exp_done, b * UB + u - 2)
                    ql_, qh_ = ql[:, c % 2, qt * P:(qt + 1) * P], qh[:, c % 2, qt * P:(qt + 1) * P]
                    out = SB[u % 3][:].rearrange("p (n w) -> p n w", n=n)
                    products(nc, out, [(qh_, ql_, kdh[:, j:j + n, 0:w], kdl[:, j:j + n, 0:w])])
                    nc.tensor.matmul(out[:, :, w - P:w], k.ident_r[:], caus[:, 0:n], start=False,
                                     stop=True, skip_group_check=True).then_inc(m.s_ready, 1)

                def transpose(u):
                    pe.wait_ge(m.p_done, b * UB + u + 1)
                    if u >= 2:
                        pe.wait_ge(m.t_lo, b * UB + u - 1)
                    for i in range(4):
                        last = nc.tensor.transpose(TB[u % 2][:, i * P:(i + 1) * P], pb[:, u % 4, i], k.ident[:])
                    last.then_inc(m.t_ready, 1)

                def attend(u):
                    c, v = units[u]
                    j, n, qt, w = shape_of(v)
                    pe.wait_ge(m.t_lo, b * UB + u + 1)
                    if u == 0:
                        pe.wait_ge(m.vd_lo, b + 1)
                    if v in (0, 2) and c:
                        pe.wait_ge(m.o_lo, (b * NCH + c) * 2 - 1 + v // 2)
                    odd, block = j // 4, j % 4
                    out = OB[qt][:].rearrange("p (s q) -> p s q", q=P)[:, block:block + n]
                    kts = w // P
                    for kt in range(kts):
                        last = products(nc, out, [(vdh[:, kt, odd], vdl[:, kt, odd], pth[:, u % 2, kt::kts],
                                                   ptl[:, u % 2, kt::kts])], start=v in (0, 2) and kt == 0,
                                        stop=v in (1, UN - 1) and kt == kts - 1, cover=True)
                    last.then_inc(m.o_ready, 1)

                def project(t, chunks):
                    last = products(nc, (SB[0], SB[1])[t][:], [
                        (oh[:, c, t * P:(t + 1) * P], ol[:, c, t * P:(t + 1) * P], woh[:, c], wol[:, c])
                        for c in chunks], start=chunks[0] == 0, stop=chunks[-1] == NCH - 1)
                    if chunks[-1] == NCH - 1:
                        last.then_inc(m.y_ready, 1)

                query(0)
                pe.wait_ge(m.y_done, b * 2 + 1)
                for u in range(UB + 4):
                    if u < UB:
                        scores(u)
                        if units[u][1] == 0 and units[u][0] + 1 < NCH:
                            query(units[u][0] + 1)
                    if 3 <= u < UB + 3:
                        transpose(u - 3)
                    if u >= 4:
                        attend(u - 4)
                    if u in (UB + 1, UB + 2):
                        t = u - UB - 1
                        pe.wait_ge(m.wo_lo, 1)
                        pe.wait_ge(m.exp_done, b * UB + UB - 2 + t)
                        pe.wait_ge(m.o_lo, (b * NCH + NCH - 1) * 2)
                        project(t, range(NCH - 1))
                pe.wait_ge(m.o_lo, (b * NCH + NCH) * 2)
                for t in range(2):
                    project(t, [NCH - 1])


Beside = namedtuple("Beside", "sync scalar gpsimd")


def norm_stage(k, tag, keep_T=True, out=None, beside=None):
    nc = k.nc
    TB = k.ps[0:4]
    HT = NT // 2
    with ExitStack() as ctx:
        def sb(name, shape, dt=F):
            return ctx.enter_context(nc.sbuf_tensor(f"{tag}_{name}", shape, dt))

        def sem(name):
            return ctx.enter_context(nc.semaphore(f"{tag}_{name}"))

        stats, mv = sb("stats", [P, NT, 6]), sb("mv", [P, NT, 2])
        ve, rs = sb("ve", [P, NT]), sb("rs", [P, NT])
        names = "stats aggr var rstd normed tr hi lo stored"
        m = namedtuple("Sems", names)(*map(sem, names.split()))
        ctx.callback(clear, nc, m)
        block = ctx.enter_context(nc.Block())

        @block.vector
        def _(dve):
            def statistics(h):
                for t in range(h * HT, (h + 1) * HT):
                    nc.vector.bn_stats(stats[:, t], k.acc[:, t]).then_inc(m.stats, 1)

            def variances(h):
                dve.wait_ge(m.stats, (h + 1) * HT)
                for t in range(h * HT, (h + 1) * HT):
                    nc.vector.bn_aggr(mv[:, t], stats[:, t]).then_inc(m.aggr, 1)
                dve.wait_ge(m.aggr, (h + 1) * HT)
                own = slice(h * HT, (h + 1) * HT)
                nc.vector.tensor_scalar(ve[:, own].unsqueeze(2), mv[:, own, 1:2], EPS, None, ALU.add).then_inc(
                    m.var, 1)

            def normalise(t):
                nc.vector.tensor_scalar(k.acc[:, t], k.acc[:, t], mv[:, t, 0:1], rs[:, t:t + 1],
                                        ALU.subtract, ALU.mult).then_inc(m.normed, 1)

            def low(t):
                dve.wait_ge(m.hi, t + 1)
                nc.vector.tensor_tensor(k.xl[:, :, t * P:(t + 1) * P], TB[t % 4][:].rearrange("p (c q) -> p c q", c=KT),
                                        f32(k.xh[:, :, t * P:(t + 1) * P]), ALU.subtract).then_inc(m.lo, 1)

            statistics(0)
            variances(0)
            statistics(1)
            dve.wait_ge(m.rstd, 1)
            for t in range(HT):
                normalise(t)
            variances(1)
            dve.wait_ge(m.rstd, 2)
            for t in range(HT, NT):
                if keep_T:
                    low(t - HT)
                normalise(t)
            if keep_T:
                for t in range(HT, NT):
                    low(t)

        @block.gpsimd
        def _(pool):
            for h in range(2):
                own = slice(h * HT, (h + 1) * HT)
                pool.wait_ge(m.var, h + 1)
                nc.gpsimd.tensor_tensor(rs[:, own], ve[:, own], k.half[:].to_broadcast([P, HT]), ALU.pow).then_inc(
                    m.rstd, 1)
            if beside:
                beside.gpsimd(pool)

        if beside:
            @block.sync
            def _(sp):
                beside.sync(sp)

        if keep_T:
            @block.tensor
            def _(pe):
                for t in range(NT):
                    pe.wait_ge(m.normed, t + 1)
                    if t >= 4:
                        pe.wait_ge(m.lo, t - 3)
                    for c in range(KT):
                        last = nc.tensor.transpose(TB[t % 4][:, c * P:(c + 1) * P], k.acc[:, t, c * P:(c + 1) * P],
                                                   k.ident[:])
                    last.then_inc(m.tr, 1)

            @block.scalar
            def _(act):
                if beside:
                    beside.scalar(act)
                for t in range(NT):
                    act.wait_ge(m.tr, t + 1)
                    nc.scalar.activation(k.xh[:, :, t * P:(t + 1) * P], TB[t % 4][:].rearrange(
                        "p (c q) -> p c q", c=KT), ACT.Copy).then_inc(m.hi, 1)
        else:
            @block.sync
            def _(sp):
                for t in range(NT):
                    sp.wait_ge(m.normed, t + 1)
                    sp.dma_start(out[t * P:(t + 1) * P, :], k.acc[:, t]).then_inc(m.stored, 16)
                sp.wait_ge(m.stored, 16 * NT)


X0_GROUPS = 8
X0_PAIRS = NH // X0_GROUPS // 2
X0_AHEAD = 4


def l0_cross_keys(k, st, norm, ctxT, wk, wv, q_norm, k_norm):
    nc = k.nc
    with ExitStack() as ctx:
        def sb(name, shape, dt=F):
            return ctx.enter_context(nc.sbuf_tensor("xk_" + name, shape, dt))

        def sem(name):
            return ctx.enter_context(nc.semaphore("xk_" + name))

        W = X0_GROUPS * HD
        craw, ch, cl = sb("craw", [P, KT, B * CTX]), sb("ch", [P, KT, B * CTX], R), sb("cl", [P, KT, B * CTX], R)
        wkraw, wvraw = sb("wkraw", [P, KT, W]), sb("wvraw", [P, KT, W])
        wkh, wkl = sb("wkh", [P, KT, W], R), sb("wkl", [P, KT, W], R)
        wvh, wvl = sb("wvh", [P, KT, W], R), sb("wvl", [P, KT, W], R)
        sq = sb("sq", [P, 4, 4, HD])
        kn = sq
        ss, rk = sb("ss", [P, 4, 4]), sb("rk", [P, 4, 4])
        norms, w = sb("norms", [P, 2]), sb("w", [P, 1])
        names = ("wk_in wv_in c_in norms_in c_hi c_lo w_hi w_lo sq_done ss_done rk_done w_done k_ready v_ready v_hi "
                 "v_lo kn_done t_ready hi lo link")
        m = namedtuple("Sems", names)(*map(sem, names.split()))
        KB, VB = k.ps[0:4], k.ps[4:8]
        ctx.callback(clear, nc, m)

        def load(sp):
            sp.dma_start(craw[:], ctxT).then_inc(m.c_in, 16)
            sp.dma_start(wkraw[:], wk).then_inc(m.wk_in, 16)
            sp.dma_start(norms[:, 0:1], q_norm).then_inc(m.norms_in, 16)
            sp.dma_start(norms[:, 1:2], k_norm).then_inc(m.norms_in, 16)
            sp.dma_start(wvraw[:], wv).then_inc(m.wv_in, 16)

        def split_high(act):
            act.wait_ge(m.c_in, 16)
            nc.scalar.activation(ch[:], craw[:], ACT.Copy).then_inc(m.c_hi, 1)

        def split_low(pool):
            pool.wait_ge(m.c_hi, 1)
            nc.gpsimd.tensor_tensor(cl[:], craw[:], f32(ch[:]), ALU.subtract).then_inc(m.c_lo, 1)

        norm_stage(k, norm, beside=Beside(load, split_high, split_low))
        block = ctx.enter_context(nc.Block())

        @block.scalar
        def _(act):
            act.wait_ge(m.wk_in, 16)
            for kt in range(KT):
                nc.scalar.activation(wkh[:, kt], wkraw[:, kt], ACT.Copy).then_inc(m.w_hi, 1)
            act.wait_ge(m.wv_in, 16)
            for kt in range(KT):
                nc.scalar.activation(wvh[:, kt], wvraw[:, kt], ACT.Copy).then_inc(m.w_hi, 1)
            for i in range(4):
                act.wait_ge(m.k_ready, i + 1)
                nc.scalar.activation(sq[:, i], KB[i][:].rearrange("p (g d) -> p g d", d=HD),
                                     ACT.Square).then_inc(m.sq_done, 1)
            for i in range(4):
                act.wait_ge(m.v_ready, i + 1)
                nc.scalar.activation(st.vh[:, 2 * i:2 * i + 2], VB[i][:].rearrange("p (g n) -> p g n", g=2),
                                     ACT.Copy).then_inc(m.v_hi, 1)
            act.wait_ge(m.w_done, 1)
            for i in range(4):
                act.wait_ge(m.t_ready, i + 1)
                nc.scalar.activation(st.kh[:, 2 * i:2 * i + 2], VB[i][:].rearrange("p (g n) -> p g n", g=2),
                                     ACT.Copy, scale=w[:]).then_inc(m.hi, 1)

        @block.gpsimd
        def _(pool):
            pool.wait_ge(m.ss_done, 1)
            nc.gpsimd.tensor_tensor(rk[:], ss[:], k.half[:].unsqueeze(2).to_broadcast([P, 4, 4]), ALU.pow).then_inc(
                m.rk_done, 1)

        @block.vector
        def _(dve):
            dve.wait_ge(m.norms_in, 32)
            nc.vector.tensor_scalar(w[:], norms[:, 0:1], norms[:, 1:2], HD ** -0.5, ALU.mult, ALU.mult).then_inc(
                m.w_done, 1)
            for i, (raw, high, low) in enumerate(((wkraw, wkh, wkl), (wvraw, wvh, wvl))):
                for kt in range(KT):
                    dve.wait_ge(m.w_hi, i * KT + kt + 1)
                    nc.vector.tensor_tensor(low[:, kt], raw[:, kt], f32(high[:, kt]), ALU.subtract).then_inc(
                        m.w_lo, 1)
            for i in range(4):
                dve.wait_ge(m.sq_done, i + 1)
                last = nc.vector.tensor_reduce(ss[:, i], sq[:, i], AX.X, ALU.add)
            last.then_inc(m.link, 1)
            dve.wait_ge(m.link, 1)
            nc.vector.tensor_scalar(ss[:], ss[:], 1.0 / HD, EPS, ALU.mult, ALU.add).then_inc(m.ss_done, 1)
            dve.wait_ge(m.rk_done, 1)
            for i in range(4):
                nc.vector.tensor_tensor(kn[:, i], KB[i][:].rearrange("p (g d) -> p g d", d=HD),
                                        rk[:, i].unsqueeze(2).to_broadcast([P, 4, HD]), ALU.mult).then_inc(
                    m.kn_done, 1)
            for i in range(4):
                dve.wait_ge(m.v_hi, i + 1)
                nc.vector.tensor_tensor(st.vl[:, 2 * i:2 * i + 2], VB[i][:].rearrange("p (g n) -> p g n", g=2),
                                        f32(st.vh[:, 2 * i:2 * i + 2]), ALU.subtract).then_inc(m.v_lo, 1)
            for i in range(4):
                dve.wait_ge(m.hi, i + 1)
                nc.vector.scalar_tensor_tensor(st.kl[:, 2 * i:2 * i + 2], VB[i][:].rearrange(
                    "p (g n) -> p g n", g=2), w[:], f32(st.kh[:, 2 * i:2 * i + 2]), ALU.mult,
                    ALU.subtract).then_inc(m.lo, 1)

        @block.tensor
        def _(pe):
            pe.wait_ge(m.c_lo, 1)
            for kt in range(KT):
                pe.wait_ge(m.w_lo, kt + 1)
                for i in range(4):
                    pair, half = divmod(i, 2)
                    rows, cols = slice(pair * P, (pair + 1) * P), slice(half * 512, (half + 1) * 512)
                    last = products(nc, KB[i][:], [(ch[:, kt, rows], cl[:, kt, rows], wkh[:, kt, cols],
                                                    wkl[:, kt, cols])], start=kt == 0, stop=kt == KT - 1)
                    if kt == KT - 1:
                        last.then_inc(m.k_ready, 1)
            pe.wait_ge(m.w_lo, 2 * KT)
            for g in range(X0_GROUPS):
                own = slice(g * HD, (g + 1) * HD)
                last = products(nc, VB[g // 2][:, g % 2 * 256:(g % 2 + 1) * 256],
                                [(wvh[:, kt, own], wvl[:, kt, own], ch[:, kt], cl[:, kt]) for kt in range(KT)])
                if g % 2:
                    last.then_inc(m.v_ready, 1)
            pe.wait_ge(m.kn_done, 4)
            for i in range(4):
                pe.wait_ge(m.v_lo, i + 1)
                for j in range(2):
                    g = 2 * i + j
                    for pair in range(2):
                        last = nc.tensor.transpose(VB[i][:, (2 * j + pair) * P:(2 * j + pair + 1) * P],
                                                   kn[:, 2 * pair + g // 4, g % 4], k.ident[:])
                last.then_inc(m.t_ready, 1)


def l0_cross_attention(k, norm, ctxT, wk, wq, wv, wo, q_norm, k_norm, mask):
    nc = k.nc
    with ExitStack() as ctx:
        def sb(name, shape, dt=F):
            return ctx.enter_context(nc.sbuf_tensor("x0_" + name, shape, dt))

        def sem(name):
            return ctx.enter_context(nc.semaphore("x0_" + name))

        parts = ("kh", "kl", "vh", "vl")
        st = namedtuple("Context", parts)(*(sb(n, [P, X0_GROUPS, B * CTX], R) for n in parts))
        l0_cross_keys(k, st, norm, ctxT, wk, wv, q_norm, k_norm)

        wqraw, woraw = sb("wqraw", [P, 2, KT, HD]), sb("woraw", [P, 2, D])
        wqh, wql = sb("wqh", [P, 2, KT, HD], R), sb("wql", [P, 2, KT, HD], R)
        woh, wol = sb("woh", [P, 2, D], R), sb("wol", [P, 2, D], R)
        PAD = 3 * CTX
        kph, kpl = sb("kph", [P, B, PAD], R), sb("kpl", [P, B, PAD], R)
        vph, vpl = sb("vph", [P, B, PAD], R), sb("vpl", [P, B, PAD], R)
        qh, ql, q2 = sb("qh", [P, 2, TOK], R), sb("ql", [P, 2, TOK], R), sb("q2", [P, 2, TOK])
        ones = sb("ones", [P, 1])
        NS = 2 * NT
        qv, rq, mx, sm, rs = (sb(n, [P, NS]) for n in ("qv", "rq", "mx", "sm", "rs"))
        mask_sb = sb("mask", [P, 2, CTX])
        sT = sb("sT", [P, TOK])
        pb = sb("pb", [P, NT, P])
        pth, ptl = sb("pth", [P, TOK], R), sb("ptl", [P, TOK], R)
        uh, ul = sb("uh", [P, B, D], R), sb("ul", [P, B, D], R)
        QB, TB, SB, UB = k.ps[0:2], k.ps[2:4], k.ps[4:6], k.ps[6:8]
        YB = [UB[0], UB[1], QB[0], QB[1]]

        names = ("wq_a_in wq_b_in wo_in cst zeroed wq_hi wq_a_split wq_b_split wo_split k_placed v_placed q_ready "
                 "q_used q_lo n_ready n_out rq_done st_ready st_out s_ready scaled masked maxed shifted exp_done summed "
                 "inv_done p_done t_ready t_hi t_lo u_ready u_hi u_lo y_ready y_done link")
        m = namedtuple("Sems", names)(*map(sem, names.split()))
        wq_in, wq_split = (m.wq_a_in, m.wq_b_in), (m.wq_a_split, m.wq_b_split)
        ctx.callback(clear, nc, m)
        block = ctx.enter_context(nc.Block())

        def half(ap, h):
            return ap[:, h * 4:h * 4 + 4].rearrange("p t (a n) -> p (t a) n", n=CTX)

        def wide(ap, h):
            return ap[:, h * NT:(h + 1) * NT].unsqueeze(2).to_broadcast([P, NT, CTX])

        def group_rows(t, g):
            return f32(t[:, bass.ds(g, 1), :].rearrange("p a (b n) -> p (a b) n", b=B))

        @block.sync
        def _(sp):
            for par in range(2):
                sp.dma_start(wqraw[:, par], wq[par]).then_inc(wq_in[par], 16)
            sp.dma_start(mask_sb[:], mask.rearrange("(t p) n -> p t n", p=P)).then_inc(m.cst, 16)
            sp.dma_start(woraw[:], wo[0:2].rearrange("a p n -> p a n")).then_inc(m.wo_in, 16)
            for par in range(2):
                sp.wait_ge(wq_split[par], 1)
                sp.dma_start(wqraw[:, par], wq[2 + par]).then_inc(wq_in[par], 16)
            with nc.sync.Fori(0, NH // 2) as p:
                for par in range(2):
                    sp.wait_ge(wq_split[par], p + 2)
                    sp.dma_start(wqraw[:, par], wq[bass.ds(2 * p + par + 4, 1)].rearrange(
                        "a p k n -> (a p) k n")).then_inc(wq_in[par], 16)
                sp.wait_ge(m.wo_split, p + 1)
                sp.dma_start(woraw[:], wo[bass.ds(2 * p + 2, 2)].rearrange("a p n -> p a n")).then_inc(m.wo_in, 16)

        @block.gpsimd
        def _(pool):
            for t in (kph, kpl, vph, vpl):
                last = nc.gpsimd.memset(f32(t[:]), 0.0)
            last.then_inc(m.zeroed, 1)
            nc.gpsimd.memset(f32(pth[:]), 0.0)
            nc.gpsimd.memset(f32(ptl[:]), 0.0).then_inc(m.t_lo, 2)
            nc.gpsimd.memset(f32(uh[:]), 0.0)
            nc.gpsimd.memset(f32(ul[:]), 0.0).then_inc(m.u_lo, B)

            def split_wo(link):
                high_part(k, woh[:], woraw[:]).then_inc(m.link, 1)
                pool.wait_ge(m.link, link)
                nc.gpsimd.tensor_tensor(wol[:], woraw[:], f32(woh[:]), ALU.subtract).then_inc(m.wo_split, 1)

            def split_wq(par, link):
                high_part(k, wqh[:, par], wqraw[:, par]).then_inc(m.link, 1)
                pool.wait_ge(m.link, link)
                nc.gpsimd.tensor_tensor(wql[:, par], wqraw[:, par], f32(wqh[:, par]), ALU.subtract).then_inc(
                    wq_split[par], 1)

            def inverse_root(p):
                pool.wait_ge(m.n_out, p + 1)
                nc.gpsimd.tensor_tensor(rq[:], qv[:], k.half[:].to_broadcast([P, NS]), ALU.pow).then_inc(
                    m.rq_done, 1)

            for par in range(2):
                pool.wait_ge(wq_in[par], 32)
                pool.wait_ge(m.q_ready, 2 * par + 2)
                split_wq(par, par + 1)
            pool.wait_ge(m.wo_in, 16)
            split_wo(3)
            inverse_root(0)
            pool.wait_ge(m.cst, 16)
            pool.wait_ge(m.zeroed, 1)
            with nc.gpsimd.Fori(0, X0_GROUPS) as g:
                for i in range(X0_PAIRS):
                    p = g * X0_PAIRS + i
                    if i == 0:
                        one = k.one[:].unsqueeze(1).to_broadcast([P, B, CTX])
                        nc.gpsimd.tensor_tensor(vph[:, :, CTX:2 * CTX], group_rows(st.vh, g), one, ALU.mult)
                        nc.gpsimd.tensor_tensor(vpl[:, :, CTX:2 * CTX], group_rows(st.vl, g), one,
                                                ALU.mult).then_inc(m.v_placed, 1)
                    for h in range(2):
                        pool.wait_ge(m.scaled, 2 * p + h + 1)
                        pv = pb[:, 4 * h:4 * h + 4].rearrange("p (b q) (a n) -> p q b a n", q=2, n=CTX)
                        for q in range(2):
                            last = nc.gpsimd.tensor_tensor(pv[:, q], pv[:, q], mask_sb[:, q:q + 1].unsqueeze(
                                1).to_broadcast([P, 2, 2, CTX]), ALU.add)
                        last.then_inc(m.masked, 1)
                    pool.wait_ge(m.wq_a_in, 16 * p + 48)
                    pool.wait_ge(m.q_ready, 4 * p + 6)
                    split_wq(0, 3 * p + 4)
                    for h in range(2):
                        pool.wait_ge(m.inv_done, 2 * p + h + 1)
                        nc.gpsimd.tensor_tensor(half(pb, h), half(pb, h), wide(rs, h), ALU.mult).then_inc(
                            m.p_done, 1)
                    pool.wait_ge(m.wq_b_in, 16 * p + 48)
                    pool.wait_ge(m.q_ready, 4 * p + 8)
                    split_wq(1, 3 * p + 5)
                    pool.wait_ge(m.wo_in, 16 * p + 32)
                    pool.wait_ge(m.u_ready, 4 * p + 4)
                    split_wo(3 * p + 6)
                    inverse_root(p + 1)

        @block.scalar
        def _(act):
            for par in range(2):
                act.wait_ge(wq_in[par], 16)
                nc.scalar.activation(wqh[:, par], wqraw[:, par], ACT.Copy).then_inc(m.wq_hi, 1)

            def query(H, i, par):
                cols = slice(i * 512, (i + 1) * 512)
                act.wait_ge(m.q_ready, 2 * H + i + 1)
                nc.scalar.activation(qh[:, par, cols], QB[i][:], ACT.Copy)
                nc.scalar.activation(q2[:, par, cols], QB[i][:], ACT.Square).then_inc(m.q_used, 1)

            for par in range(2):
                for i in range(2):
                    query(par, i, par)
            act.wait_ge(m.zeroed, 1)
            with nc.scalar.Fori(0, X0_GROUPS) as g:
                for j in range(X0_PAIRS):
                    p = g * X0_PAIRS + j
                    if j == 0:
                        nc.scalar.activation(kph[:, :, CTX:2 * CTX], group_rows(st.kh, g), ACT.Copy)
                        nc.scalar.activation(kpl[:, :, CTX:2 * CTX], group_rows(st.kl, g), ACT.Copy).then_inc(
                            m.k_placed, 1)
                    for i in range(2):
                        act.wait_ge(m.st_ready, 2 * p + i + 1)
                        nc.scalar.activation(sT[:, i * 512:(i + 1) * 512], TB[i][:], ACT.Copy).then_inc(
                            m.st_out, 1)
                    for h in range(2):
                        query(2 * p + 2, h, 0)
                        act.wait_ge(m.shifted, 2 * p + h + 1)
                        nc.scalar.activation(half(pb, h), half(pb, h), ACT.Exp).then_inc(m.exp_done, 1)
                    for i in range(2):
                        query(2 * p + 3, i, 1)
                    for b in range(B):
                        act.wait_ge(m.u_ready, 4 * p + b + 1)
                        nc.scalar.activation(uh[:, b], UB[b % 2][:], ACT.Copy).then_inc(m.u_hi, 1)
                    for i in range(2):
                        act.wait_ge(m.t_ready, 2 * p + i + 1)
                        nc.scalar.activation(pth[:, i * 512:(i + 1) * 512], TB[i][:], ACT.Copy).then_inc(
                            m.t_hi, 1)

        @block.vector
        def _(dve):
            nc.vector.memset(ones[:], 1.0)
            for par in range(2):
                dve.wait_ge(m.wq_hi, par + 1)
                nc.vector.tensor_tensor(wql[:, par], wqraw[:, par], f32(wqh[:, par]), ALU.subtract).then_inc(
                    wq_split[par], 1)

            def query(H, i, par):
                cols = slice(i * 512, (i + 1) * 512)
                dve.wait_ge(m.q_used, 2 * H + i + 1)
                nc.vector.tensor_tensor(ql[:, par, cols], QB[i][:], f32(qh[:, par, cols]), ALU.subtract).then_inc(
                    m.q_lo, 1)

            def variance(p):
                dve.wait_ge(m.n_ready, p + 1)
                nc.vector.tensor_scalar(qv[:], QB[0][:, 0:NS], 1.0 / HD, EPS, ALU.mult, ALU.add).then_inc(m.n_out, 1)

            def project(p):
                for t in range(NT):
                    dve.wait_ge(m.y_ready, p * NT + t + 1)
                    nc.vector.tensor_tensor(k.acc[:, t], YB[t % 4][:], k.acc[:, t], ALU.add).then_inc(
                        m.y_done, 1)

            for par in range(2):
                for i in range(2):
                    query(par, i, par)
            variance(0)
            with nc.vector.Fori(0, X0_GROUPS) as g:
                for j in range(X0_PAIRS):
                    p = g * X0_PAIRS + j
                    project(p)
                    dve.wait_ge(m.rq_done, p + 1)
                    for h in range(2):
                        dve.wait_ge(m.s_ready, 2 * p + h + 1)
                        nc.vector.tensor_tensor(half(pb, h), SB[h][:].rearrange("p (t n) -> p t n", n=CTX),
                                                wide(rq, h), ALU.mult).then_inc(m.scaled, 1)
                    for h in range(2):
                        dve.wait_ge(m.masked, 2 * p + h + 1)
                        nc.vector.tensor_reduce(mx[:, h * NT:(h + 1) * NT], half(pb, h), AX.X, ALU.max).then_inc(
                            m.maxed, 1)
                        dve.wait_ge(m.maxed, 2 * p + h + 1)
                        nc.vector.tensor_tensor(half(pb, h), half(pb, h), wide(mx, h), ALU.subtract).then_inc(
                            m.shifted, 1)
                        query(2 * p + 2, h, 0)
                    for h in range(2):
                        dve.wait_ge(m.exp_done, 2 * p + h + 1)
                        own = slice(h * NT, (h + 1) * NT)
                        nc.vector.tensor_reduce(sm[:, own], half(pb, h), AX.X, ALU.add).then_inc(m.summed, 1)
                        dve.wait_ge(m.summed, 2 * p + h + 1)
                        nc.vector.reciprocal(rs[:, own], sm[:, own]).then_inc(m.inv_done, 1)
                    for i in range(2):
                        query(2 * p + 3, i, 1)
                    for b in range(B):
                        dve.wait_ge(m.u_hi, 4 * p + b + 1)
                        nc.vector.tensor_tensor(ul[:, b], UB[b % 2][:], f32(uh[:, b]), ALU.subtract).then_inc(
                            m.u_lo, 1)
                    for i in range(2):
                        cols = slice(i * 512, (i + 1) * 512)
                        dve.wait_ge(m.t_hi, 2 * p + i + 1)
                        nc.vector.tensor_tensor(ptl[:, cols], TB[i][:], f32(pth[:, cols]), ALU.subtract).then_inc(
                            m.t_lo, 1)
                    variance(p + 1)
            project(NH // 2)

        @block.tensor
        def _(pe):
            def query(H, i, par):
                cols = slice(i * 512, (i + 1) * 512)
                products(nc, QB[i][:], [(wqh[:, par, kt], wql[:, par, kt], k.xh[:, kt, cols], k.xl[:, kt, cols])
                                        for kt in range(KT)]).then_inc(m.q_ready, 1)

            def squares(p, first=0, last_tile=NT):
                pe.wait_ge(m.q_lo, 4 * p + (3 if last_tile <= NT // 2 else 4))
                for t in range(first, last_tile):
                    for par in range(2):
                        last = nc.tensor.matmul(QB[0][:, 2 * t + par:2 * t + par + 1],
                                                q2[:, par, t * P:(t + 1) * P], ones[:], start=True, stop=True)
                if last_tile == NT:
                    last.then_inc(m.n_ready, 1)

            def project(p):
                pe.wait_ge(m.t_lo, 2 * p + 2)
                pe.wait_ge(m.u_lo, B * p + B)
                for t in range(NT):
                    if t == 2:
                        pe.wait_ge(m.n_out, p + 1)
                    if t >= 4:
                        pe.wait_ge(m.y_done, NT * p + t - 3)
                    tok, b = slice(t * P, (t + 1) * P), t // 2
                    products(nc, YB[t % 4][:], [(pth[:, tok], ptl[:, tok], uh[:, b], ul[:, b])]).then_inc(
                        m.y_ready, 1)

            for par in range(2):
                pe.wait_ge(wq_split[par], 1)
                for i in range(2):
                    if par:
                        pe.wait_ge(m.q_lo, i + 1)
                    query(par, i, par)
            squares(0)
            with nc.tensor.Fori(0, X0_GROUPS) as g:
                for j in range(X0_PAIRS):
                    p = g * X0_PAIRS + j
                    if j == 0:
                        pe.wait_ge(m.k_placed, g + 1)
                    pe.wait_ge(m.t_lo, 2 * p + 2)
                    for i in range(2):
                        for b in (2 * i, 2 * i + 1):
                            tok = slice(b * S, (b + 1) * S)
                            last = products(nc, TB[i][:, b % 2 * S:(b % 2 + 1) * S], [
                                (kph[:, b, at:at + P], kpl[:, b, at:at + P], qh[:, par, tok], ql[:, par, tok])
                                for par, at in ((0, CTX), (1, 0))])
                        last.then_inc(m.st_ready, 1)
                    project(p)
                    for i in range(2):
                        pe.wait_ge(m.st_out, 2 * p + i + 1)
                        for t in range(4 * i, 4 * i + 4):
                            last = nc.tensor.transpose(SB[i][:, t % 4 * P:(t % 4 + 1) * P], sT[:, t * P:(t + 1) * P],
                                                       k.ident[:])
                        last.then_inc(m.s_ready, 1)
                    pe.wait_ge(m.wq_a_split, p + 2)
                    for i in range(2):
                        pe.wait_ge(m.y_done, NT * p + NT - 1 + i)
                        query(2 * p + 2, i, 0)
                    pe.wait_ge(m.wq_b_split, p + 2)
                    for i in range(2):
                        pe.wait_ge(m.q_lo, 4 * p + 5 + i)
                        query(2 * p + 3, i, 1)
                    pe.wait_ge(m.wo_split, p + 1)
                    if j == 0:
                        pe.wait_ge(m.v_placed, g + 1)
                    for b in range(B):
                        if b >= 2:
                            pe.wait_ge(m.u_lo, B * p + B + b - 1)
                        products(nc, UB[b % 2][:], [
                            (vph[:, b, at:at + P], vpl[:, b, at:at + P], woh[:, par], wol[:, par])
                            for par, at in ((0, CTX), (1, 0))]).then_inc(m.u_ready, 1)
                        if b in (1, 2):
                            squares(p + 1, 2 * b - 2, 2 * b)
                    for i in range(2):
                        pe.wait_ge(m.p_done, 2 * p + i + 1)
                        for t in range(4 * i, 4 * i + 4):
                            last = nc.tensor.transpose(TB[i][:, t % 4 * P:(t % 4 + 1) * P], pb[:, t], k.ident[:])
                        last.then_inc(m.t_ready, 1)
                    squares(p + 1, NT // 2)
            project(NH // 2)


def mixture(k, tag, w_base, b_base, w_small, w_up, expand, b_thr=None, before=None, out=None):
    nc = k.nc
    thresholded = b_thr is not None
    SMALL = ER + GATE
    SCALING = 2.0 if thresholded else 1.0

    with ExitStack() as ctx:
        def sb(name, shape, dt=F):
            return ctx.enter_context(nc.sbuf_tensor(f"{tag}_{name}", shape, dt))

        def sem(name):
            return ctx.enter_context(nc.semaphore(f"{tag}_{name}"))

        braw, bh, bl = sb("braw", [P, KT, D]), sb("bh", [P, KT, D], R), sb("bl", [P, KT, D], R)
        sraw, sh, sl = sb("sraw", [P, KT, SMALL]), sb("sh", [P, KT, SMALL], R), sb("sl", [P, KT, SMALL], R)
        uraw, uh, ul = sb("uraw", [P, D]), sb("uh", [P, D], R), sb("ul", [P, D], R)
        bias = sb("bias", [P, D])
        first = sb("first", [P, NE, NE])
        thr = sb("thr", [P, 1])
        exp_f, exp_r = sb("exp_f", [NE, ER]), sb("exp_r", [NE, ER], R)
        gT = sb("gT", [GATE, TOK])
        hT = sb("hT", [P, TOK])
        hw, hwh, hwl = sb("hw", [P, TOK]), sb("hwh", [P, TOK], R), sb("hwl", [P, TOK], R)
        wTh, wTl = sb("wTh", [NE, TOK], R), sb("wTl", [NE, TOK], R)
        nmax, z, ez, th = (sb(n, [P, NT]) for n in ("nmax", "z", "ez", "th"))
        total, none, inv = (sb(n, [P, NT]) for n in ("total", "none", "inv"))
        e, rank, over, w = (sb(n, [P, NT, NE]) for n in ("e", "rank", "over", "w"))
        more, ties = sb("more", [P, NT, NE, NE]), sb("ties", [P, NT, NE, NE])
        GB, HB, YB = k.ps[0:2], k.ps[2:4], k.ps[4:8]
        NY = len(YB)
        names = ("small_in up_in base_in cst hi_done lo_done exp_split g_ready g_out logits_ready shifted exp_done "
                 "z_done ez_done link w_done wt_ready wt_hi wt_lo h_ready h_out spread hw_done hw_hi hw_lo y_ready "
                 "y_done bias_done stats aggr var rstd normed stored")
        m = namedtuple("Sems", names)(*map(sem, names.split()))
        stats, mv, ve, rs = sb("stats", [P, NT, 6]), sb("mv", [P, NT, 2]), sb("ve", [P, NT]), sb("rs", [P, NT])
        ctx.callback(clear, nc, m)

        loads = ((sraw, sh, sl, w_small, m.small_in), (uraw, uh, ul, w_up, m.up_in), (braw, bh, bl, w_base, m.base_in))

        def load(sp):
            for raw, _, _, src, arrived in loads:
                sp.dma_start(raw[:], src).then_inc(arrived, 16)
            for dst, src in ((bias[:], b_base.partition_broadcast(P)), (exp_f[:], expand),
                             (thr[:], b_thr.partition_broadcast(P)) if thresholded else (first[:], before)):
                sp.dma_start(dst, src).then_inc(m.cst, 16)

        def split_high(act):
            for raw, high, _, _, arrived in loads:
                act.wait_ge(arrived, 16)
                nc.scalar.activation(high[:], raw[:], ACT.Copy).then_inc(m.hi_done, 1)
            act.wait_ge(m.cst, 48)
            nc.scalar.activation(exp_r[:], exp_f[:], ACT.Copy).then_inc(m.exp_split, 1)

        def split_low(pool):
            for i, (raw, high, low, _, _) in enumerate(loads):
                pool.wait_ge(m.hi_done, i + 1)
                nc.gpsimd.tensor_tensor(low[:], raw[:], f32(high[:]), ALU.subtract).then_inc(m.lo_done, 1)

        norm_stage(k, tag + "n", beside=Beside(load, split_high, split_low))

        def wide(ap):
            return ap[:].unsqueeze(2).to_broadcast([P, NT, NE])

        def cols(i):
            return slice(i * 512, (i + 1) * 512)

        logits = GB[0][:, 0:NT * GATE].rearrange("p (t e) -> p t e", t=NT)

        with nc.Block() as block:
            @block.gpsimd
            def _(pool):
                pool.wait_ge(m.cst, 48)
                for t in range(NT):
                    nc.gpsimd.tensor_tensor(k.acc[:, t], k.acc[:, t], bias[:], ALU.add).then_inc(m.bias_done, 1)
                if out is not None:
                    for t in range(NT):
                        pool.wait_ge(m.var, t + 1)
                        nc.gpsimd.tensor_tensor(rs[:, t:t + 1], ve[:, t:t + 1], k.half[:], ALU.pow).then_inc(
                            m.rstd, 1)

            if out is not None:
                @block.sync
                def _(sp):
                    for t in range(NT):
                        sp.wait_ge(m.normed, t + 1)
                        sp.dma_start(out[t * P:(t + 1) * P, :], k.acc[:, t]).then_inc(m.stored, 16)
                    sp.wait_ge(m.stored, 16 * NT)

            @block.scalar
            def _(act):
                for i in range(2):
                    act.wait_ge(m.g_ready, i + 1)
                    nc.scalar.activation(gT[:, cols(i)], GB[i][0:GATE, :], ACT.Copy).then_inc(m.g_out, 1)
                for i in range(2):
                    act.wait_ge(m.h_ready, i + 1)
                    nc.scalar.activation(hT[:, cols(i)], HB[i][:], ACT.Copy).then_inc(m.h_out, 1)
                if thresholded:
                    act.wait_ge(m.z_done, 1)
                    nc.scalar.activation(ez[:], z[:], ACT.Exp, scale=-1.0).then_inc(m.ez_done, 1)
                act.wait_ge(m.shifted, 1)
                nc.scalar.activation(e[:], w[:], ACT.Exp).then_inc(m.exp_done, 1)
                for i in range(2):
                    act.wait_ge(m.wt_ready, i + 1)
                    nc.scalar.activation(wTh[:, cols(i)], GB[i][0:NE, :], ACT.Copy).then_inc(m.wt_hi, 1)
                for i in range(2):
                    act.wait_ge(m.hw_done, i + 1)
                    nc.scalar.activation(hwh[:, cols(i)], hw[:, cols(i)], ACT.Copy).then_inc(m.hw_hi, 1)

            @block.vector
            def _(dve):
                dve.wait_ge(m.cst, 48)
                dve.wait_ge(m.logits_ready, 1)
                if thresholded:
                    nc.vector.tensor_scalar(z[:].unsqueeze(2), logits[:, :, NE:NE + 1], thr[:], None,
                                            ALU.add).then_inc(m.z_done, 1)
                nc.vector.tensor_reduce(nmax[:], logits[:, :, 0:NE], AX.X, ALU.max, negate=True).then_inc(m.link, 1)
                dve.wait_ge(m.link, 1)
                nc.vector.tensor_tensor(w[:], logits[:, :, 0:NE], wide(nmax), ALU.add).then_inc(m.shifted, 1)
                dve.wait_ge(m.exp_done, 1)
                if thresholded:
                    dve.wait_ge(m.ez_done, 1)
                    nc.vector.tensor_scalar(ez[:], ez[:], 1.0, 8.0, ALU.add, ALU.mult).then_inc(m.link, 1)
                    nc.vector.tensor_reduce(total[:], e[:], AX.X, ALU.add).then_inc(m.link, 1)
                    dve.wait_ge(m.link, 3)
                    nc.vector.reciprocal(th[:], ez[:]).then_inc(m.link, 1)
                    nc.vector.reciprocal(inv[:], total[:]).then_inc(m.link, 1)
                    dve.wait_ge(m.link, 5)
                    nc.vector.tensor_tensor(rank[:], e[:], wide(inv), ALU.mult).then_inc(m.link, 1)
                    dve.wait_ge(m.link, 6)
                    nc.vector.tensor_tensor(over[:], rank[:], wide(th), ALU.subtract).then_inc(m.link, 1)
                    dve.wait_ge(m.link, 7)
                    nc.vector.tensor_scalar(rank[:], over[:], 0.0, None, ALU.max).then_inc(m.link, 1)
                    dve.wait_ge(m.link, 8)
                    nc.vector.tensor_reduce(total[:], rank[:], AX.X, ALU.add).then_inc(m.link, 1)
                    dve.wait_ge(m.link, 9)
                    nc.vector.tensor_scalar(none[:], total[:], 0.0, None, ALU.is_equal).then_inc(m.link, 1)
                    dve.wait_ge(m.link, 10)
                    nc.vector.tensor_tensor(total[:], total[:], none[:], ALU.add).then_inc(m.link, 1)
                    links = 11
                else:
                    own = e[:].unsqueeze(3).to_broadcast([P, NT, NE, NE])
                    other = e[:].unsqueeze(2).to_broadcast([P, NT, NE, NE])
                    nc.vector.tensor_tensor(ties[:], other, own, ALU.is_equal).then_inc(m.link, 1)
                    nc.vector.tensor_tensor(more[:], other, own, ALU.is_gt).then_inc(m.link, 1)
                    dve.wait_ge(m.link, 3)
                    nc.vector.tensor_tensor(ties[:], ties[:], first[:].unsqueeze(1).to_broadcast([P, NT, NE, NE]),
                                            ALU.mult).then_inc(m.link, 1)
                    dve.wait_ge(m.link, 4)
                    nc.vector.tensor_tensor(more[:], more[:], ties[:], ALU.add).then_inc(m.link, 1)
                    dve.wait_ge(m.link, 5)
                    nc.vector.tensor_reduce(over[:], more[:], AX.X, ALU.add).then_inc(m.link, 1)
                    dve.wait_ge(m.link, 6)
                    nc.vector.scalar_tensor_tensor(rank[:], over[:], 1.5, e[:], ALU.is_lt, ALU.mult).then_inc(
                        m.link, 1)
                    dve.wait_ge(m.link, 7)
                    nc.vector.tensor_reduce(total[:], rank[:], AX.X, ALU.add).then_inc(m.link, 1)
                    links = 8
                dve.wait_ge(m.link, links)
                nc.vector.reciprocal(inv[:], total[:]).then_inc(m.link, 1)
                dve.wait_ge(m.link, links + 1)
                nc.vector.scalar_tensor_tensor(w[:], rank[:], SCALING, wide(inv), ALU.mult, ALU.mult).then_inc(
                    m.w_done, 1)
                for i in range(2):
                    dve.wait_ge(m.wt_hi, i + 1)
                    nc.vector.tensor_tensor(wTl[:, cols(i)], GB[i][0:NE, :], f32(wTh[:, cols(i)]),
                                            ALU.subtract).then_inc(m.wt_lo, 1)
                for i in range(2):
                    dve.wait_ge(m.spread, i + 1)
                    nc.vector.tensor_tensor(hw[:, cols(i)], HB[i][:], hT[:, cols(i)], ALU.mult).then_inc(
                        m.hw_done, 1)
                for i in range(2):
                    dve.wait_ge(m.hw_hi, i + 1)
                    nc.vector.tensor_tensor(hwl[:, cols(i)], hw[:, cols(i)], f32(hwh[:, cols(i)]),
                                            ALU.subtract).then_inc(m.hw_lo, 1)
                for t in range(NT + 2):
                    if t < NT:
                        dve.wait_ge(m.y_ready, t + 1)
                        dve.wait_ge(m.bias_done, t + 1)
                        nc.vector.tensor_tensor(k.acc[:, t], YB[t % NY][:], k.acc[:, t], ALU.add).then_inc(
                            m.y_done, 1)
                    if out is None:
                        continue
                    if 1 <= t < NT + 1:
                        dve.wait_ge(m.stats, t)
                        nc.vector.bn_aggr(mv[:, t - 1], stats[:, t - 1]).then_inc(m.aggr, 1)
                        dve.wait_ge(m.aggr, t)
                        nc.vector.tensor_scalar(ve[:, t - 1:t], mv[:, t - 1, 1:2], EPS, None, ALU.add).then_inc(
                            m.var, 1)
                    if t < NT:
                        dve.wait_ge(m.y_done, t + 1)
                        nc.vector.bn_stats(stats[:, t], k.acc[:, t]).then_inc(m.stats, 1)
                    if t >= 2:
                        dve.wait_ge(m.rstd, t - 1)
                        nc.vector.tensor_scalar(k.acc[:, t - 2], k.acc[:, t - 2], mv[:, t - 2, 0:1],
                                                rs[:, t - 2:t - 1], ALU.subtract, ALU.mult).then_inc(m.normed, 1)

            @block.tensor
            def _(pe):
                def base(t):
                    tok = slice(t * P, (t + 1) * P)
                    products(nc, YB[t % NY][:], [(k.xh[:, kt, tok], k.xl[:, kt, tok], bh[:, kt], bl[:, kt])
                                                 for kt in range(KT)], stop=False)

                def lift(t):
                    tok = slice(t * P, (t + 1) * P)
                    products(nc, YB[t % NY][:], [(hwh[:, tok], hwl[:, tok], uh[:], ul[:])], start=False).then_inc(
                        m.y_ready, 1)

                pe.wait_ge(m.lo_done, 3)
                pe.wait_ge(m.exp_split, 1)
                for own, banks, rows, ready in ((slice(ER, SMALL), GB, slice(0, GATE), m.g_ready),
                                                (slice(0, ER), HB, slice(0, ER), m.h_ready)):
                    for i in range(2):
                        products(nc, banks[i][rows, :], [(sh[:, kt, own], sl[:, kt, own], k.xh[:, kt, cols(i)],
                                                          k.xl[:, kt, cols(i)]) for kt in range(KT)]).then_inc(
                            ready, 1)
                pe.wait_ge(m.g_out, 2)
                for t in range(NT):
                    last = nc.tensor.transpose(logits[:, t], gT[:, t * P:(t + 1) * P], k.ident[0:GATE, 0:GATE])
                last.then_inc(m.logits_ready, 1)
                for t in range(NY - 1):
                    base(t)
                pe.wait_ge(m.w_done, 1)
                for t in range(NT):
                    last = nc.tensor.transpose(GB[t // 4][0:NE, t % 4 * P:(t % 4 + 1) * P], w[:, t], k.ident[:])
                    if t % 4 == 3:
                        last.then_inc(m.wt_ready, 1)
                base(NY - 1)
                pe.wait_ge(m.h_out, 2)
                for i in range(2):
                    pe.wait_ge(m.wt_lo, i + 1)
                    products(nc, HB[i][:], [(exp_r[:], None, wTh[:, cols(i)], wTl[:, cols(i)])]).then_inc(m.spread, 1)
                pe.wait_ge(m.hw_lo, 1)
                for t in range(NY):
                    lift(t)
                pe.wait_ge(m.hw_lo, 2)
                for t in range(NY, NT):
                    pe.wait_ge(m.y_done, t - NY + 1)
                    base(t)
                    lift(t)


L1_GROUPS = 4
QUAD = 4
ROUNDS = NH // L1_GROUPS // QUAD
WQ_AHEAD = 2


def l1_attention(k, tag, norm, wq, wk, wv, wo, scale, anticausal=None, uniform=None, last_row=None, ctxT=None):
    nc = k.nc
    cross = ctxT is not None
    KEYS = S + CTX if cross else S
    NKV = 6 if cross else 4
    NVT = NT + B if cross else NT
    NG = 2 if cross else 1
    UR = QUAD * B
    PTW = 3 * S if cross else 2 * S

    with ExitStack() as ctx:
        def sb(name, shape, dt=F):
            return ctx.enter_context(nc.sbuf_tensor(f"{tag}_{name}", shape, dt))

        def sem(name):
            return ctx.enter_context(nc.semaphore(f"{tag}_{name}"))

        wqraw, woraw = sb("wqraw", [P, KT, HD]), sb("woraw", [P, D])
        kvraw = sb("kvraw", [P, 2, KT, HD])
        wqh, wql = sb("wqh", [P, 2, KT, HD], R), sb("wql", [P, 2, KT, HD], R)
        woh, wol = sb("woh", [P, QUAD, D], R), sb("wol", [P, QUAD, D], R)
        wkvh, wkvl = sb("wkvh", [P, 2, KT, HD], R), sb("wkvl", [P, 2, KT, HD], R)
        kh, kl = sb("kh", [P, B, KEYS], R), sb("kl", [P, B, KEYS], R)
        vh, vl = sb("vh", [P, NVT, HD], R), sb("vl", [P, NVT, HD], R)
        qh, ql = sb("qh", [P, 2, TOK], R), sb("ql", [P, 2, TOK], R)
        pb = sb("pb", [P, 3, 2, KEYS])
        pth, ptl = sb("pth", [P, 2, PTW], R), sb("ptl", [P, 2, PTW], R)
        oh, ol = sb("oh", [P, QUAD, TOK], R), sb("ol", [P, QUAD, TOK], R)
        nmax, rsum, rinv = sb("nmax", [P, 2, 2]), sb("rsum", [P, 2, 2]), sb("rinv", [P, 3, 2])
        start = sb("start", [P, 1])
        if cross:
            ctx_raw = sb("ctx_raw", [P, KT, B * CTX])
            ch, cl = sb("ch", [P, KT, B * CTX], R), sb("cl", [P, KT, B * CTX], R)
        else:
            mask_f, mask = sb("mask_f", [P, 2, P]), sb("mask", [P, 2, P], R)
            uni_f = sb("uni_f", [P, P])
            fix, rfirst = sb("fix", [P, 2]), sb("rfirst", [P, 2, 2])
        SB, TB, QB, OB = k.ps[0:2], k.ps[2:4], k.ps[4:6], k.ps[6:8]

        names = ("wq_in wo_in kv_in cst cst_low cst_split kvw_split wq_split wo_split kv_ready kv_hi kv_lo q_ready "
                 "q_hi q_lo s_ready max_done exp_done inv_first inv_done p_done t_ready t_hi t_lo o_ready o_hi o_lo "
                 "y_ready y_done link vt_ready vt_done")
        m = namedtuple("Sems", names)(*map(sem, names.split()))

        if cross:
            blocks = [(P, 4 * P, [(q, t * P, t * S + q * P) for t in range(2) for q in range(2)]),
                      (CTX, S, [(q, S, q * P) for q in range(2)])]
        else:
            blocks = [(P, 3 * P, [(0, P, 0), (1, P, P), (0, 0, 2 * P)])]

        def pt_part(t, u, g):
            rows, width, _ = blocks[g]
            return t[0:rows, u % 2, g * 4 * P:g * 4 * P + width]

        def t_bank(u, g):
            rows, width, _ = blocks[g]
            return TB[g if cross else u % 2][0:rows, 0:width]

        def kv_parts():
            for i in range(2):
                yield (TB[i][:].rearrange("p (b s) -> p b s", b=2), kh[:, 2 * i:2 * i + 2, 0:S],
                       kl[:, 2 * i:2 * i + 2, 0:S])
            if cross:
                yield (QB[0][:, 0:B * CTX].rearrange("p (b s) -> p b s", b=B), kh[:, :, S:], kl[:, :, S:])
            for i in range(2):
                yield (OB[i][:].rearrange("p (t d) -> p t d", t=4), vh[:, 4 * i:4 * i + 4], vl[:, 4 * i:4 * i + 4])
            if cross:
                yield (QB[1][0:CTX, :].rearrange("p (t d) -> p t d", t=B), vh[0:CTX, NT:], vl[0:CTX, NT:])

        v_rows = pb[:].rearrange("p a b n -> p (a b n)")
        v_parts = [(SB[0][:], 0, 512), (SB[1][:], 512, 1024)] + (
            [(OB[1][:, 0:B * CTX], TOK, TOK + B * CTX)] if cross else [])
        NVP = len(v_parts)

        def score_bank(u, q):
            return (SB[q][:, 0:KEYS], 0) if cross else (SB[u % 2][:, q * S:(q + 1) * S], q * P)

        ctx.callback(clear, nc, m)

        def load(sp):
            sp.dma_start(wqraw[:], wq[0]).then_inc(m.wq_in, 16)
            for i, w in enumerate((wk, wv)):
                sp.dma_start(kvraw[:, i], w[0]).then_inc(m.kv_in, 16)
            pairs = ((ctx_raw[:], ctxT),) if cross else ((mask_f[:, 0], anticausal), (mask_f[:, 1], anticausal),
                                                             (uni_f[:], uniform), (fix[:], last_row))
            for dst, src in pairs:
                sp.dma_start(dst, src).then_inc(m.cst, 16)
            sp.wait_ge(m.wq_split, 1)
            sp.dma_start(wqraw[:], wq[1]).then_inc(m.wq_in, 16)

        def split_high(act):
            act.wait_ge(m.wq_in, 16)
            nc.scalar.activation(wqh[:, 0], wqraw[:], ACT.Copy).then_inc(m.cst_split, 1)
            act.wait_ge(m.kv_in, 32)
            nc.scalar.activation(wkvh[:], kvraw[:], ACT.Copy).then_inc(m.link, 1)
            act.wait_ge(m.cst, 16 if cross else 64)
            for dst, src in (((ch[:], ctx_raw[:]),) if cross else ((mask[:], mask_f[:]), (pth[:, 0, 3 * P:], uni_f[:]),
                                                                   (pth[:, 1, 3 * P:], uni_f[:]))):
                nc.scalar.activation(dst, src, ACT.Copy).then_inc(m.cst_split, 1)

        def split_low(pool):
            nc.gpsimd.memset(start[:], 0.0).then_inc(m.wo_split, 1)
            pool.wait_ge(m.cst_split, 1)
            nc.gpsimd.tensor_tensor(wql[:, 0], wqraw[:], f32(wqh[:, 0]), ALU.subtract).then_inc(m.wq_split, 1)
            pool.wait_ge(m.link, 1)
            nc.gpsimd.tensor_tensor(wkvl[:], kvraw[:], f32(wkvh[:]), ALU.subtract).then_inc(m.kvw_split, 1)
            if cross:
                pool.wait_ge(m.cst_split, 2)
                nc.gpsimd.tensor_tensor(cl[:], ctx_raw[:], f32(ch[:]), ALU.subtract).then_inc(m.cst_low, 1)
            else:
                nc.gpsimd.memset(f32(ptl[:, :, 3 * P:]), 0.0).then_inc(m.cst_low, 1)
            pool.wait_ge(m.wq_in, 32)
            pool.wait_ge(m.cst_split, 2 if cross else 4)
            high_part(k, wqh[:, 1], wqraw[:]).then_inc(m.cst_split, 1)
            pool.wait_ge(m.cst_split, 3 if cross else 5)
            nc.gpsimd.tensor_tensor(wql[:, 1], wqraw[:], f32(wqh[:, 1]), ALU.subtract).then_inc(m.wq_split, 1)

        norm_stage(k, norm, beside=Beside(load, split_high, split_low))
        block = ctx.enter_context(nc.Block())

        @block.sync
        def _(sp):
            with nc.sync.Fori(0, L1_GROUPS) as g:
                sp.wait_ge(m.kvw_split, g + 1)
                for i, w in enumerate((wk, wv)):
                    sp.dma_start(kvraw[:, i], w[bass.ds(g + 1, 1)].rearrange("a p k n -> (a p) k n")).then_inc(
                        m.kv_in, 16)
                with nc.sync.Fori(0, NH // L1_GROUPS) as i:
                    h = g * (NH // L1_GROUPS) + i
                    sp.wait_ge(m.wo_split, h + 1)
                    sp.dma_start(woraw[:], wo[bass.ds(h, 1)].rearrange("a p n -> (a p) n")).then_inc(
                        m.wo_in, 16)
                    sp.wait_ge(m.wq_split, h + 2)
                    sp.dma_start(wqraw[:], wq[bass.ds(h + 2, 1)].rearrange("a p k n -> (a p) k n")).then_inc(
                        m.wq_in, 16)

        @block.gpsimd
        def _(pool):
            with nc.gpsimd.Fori(0, L1_GROUPS) as g:
                with nc.gpsimd.Fori(0, ROUNDS) as s:
                    r = g * ROUNDS + s
                    for u in range(UR):
                        h, b = divmod(u, B)
                        pool.wait_ge(m.inv_done, r * UR + u + 1)
                        for q, lo in (((0, 0), (1, P)) if not cross else ((None, 0),)):
                            pv = pb[:, u % 3] if cross else pb[:, u % 3, q, lo:]
                            rv = rinv[:, u % 3] if cross else rinv[:, u % 3, q:q + 1]
                            if cross:
                                last = nc.gpsimd.tensor_tensor(pv, pv, rv.unsqueeze(2).to_broadcast([P, 2, KEYS]),
                                                               ALU.mult)
                            else:
                                last = nc.gpsimd.tensor_tensor(pv, pv, rv.to_broadcast([P, S - lo]), ALU.mult)
                        last.then_inc(m.p_done, 1)
                        H = r * QUAD + h
                        if b == 0:
                            pool.wait_ge(m.wq_in, 16 * H + 48)
                            pool.wait_ge(m.q_ready, 2 * H + 2)
                            raw, high, low = wqraw[:], wqh[:, h % 2], wql[:, h % 2]
                        elif b < 3:
                            if b == 1:
                                pool.wait_ge(m.wo_in, 16 * H + 16)
                            cols = slice((b - 1) * 2 * P, b * 2 * P)
                            raw, high, low = woraw[:, cols], woh[:, h, cols], wol[:, h, cols]
                        else:
                            continue
                        high_part(k, high, raw).then_inc(m.link, 1)
                        pool.wait_ge(m.link, (r * QUAD + h) * 3 + b + g + 2)
                        last = nc.gpsimd.tensor_tensor(low, raw, f32(high), ALU.subtract)
                        if b == 0:
                            last.then_inc(m.wq_split, 1)
                        elif b == 2:
                            last.then_inc(m.wo_split, 1)
                pool.wait_ge(m.kv_in, 32 * g + 64)
                pool.wait_ge(m.kv_ready, NKV * (g + 1))
                high_part(k, wkvh[:], kvraw[:]).then_inc(m.link, 1)
                pool.wait_ge(m.link, (g + 1) * ROUNDS * QUAD * 3 + g + 2)
                nc.gpsimd.tensor_tensor(wkvl[:], kvraw[:], f32(wkvh[:]), ALU.subtract).then_inc(
                    m.kvw_split, 1)

        @block.scalar
        def _(act):
            def query(H, i, par):
                act.wait_ge(m.q_ready, 2 * H + i + 1)
                nc.scalar.activation(qh[:, par, i * 512:(i + 1) * 512], QB[i][:], ACT.Copy).then_inc(
                    m.q_hi, 1)

            for i in range(2):
                query(0, i, 0)
            with nc.scalar.Fori(0, L1_GROUPS) as g:
                for i, (bank, high, low) in enumerate(kv_parts()):
                    act.wait_ge(m.kv_ready, NKV * g + i + 1)
                    nc.scalar.activation(high, bank, ACT.Copy, scale=scale if i < NKV // 2 else 1.0).then_inc(
                        m.kv_hi, 1)
                    if i == 0:
                        for j in range(0, NVP, 2):
                            bank, lo, hi = v_parts[j]
                            act.wait_ge(m.vt_ready, NVP * g + j + 1)
                            nc.scalar.activation(v_rows[:, lo:hi], bank, ACT.Copy).then_inc(m.vt_done, 1)
                with nc.scalar.Fori(0, ROUNDS) as s:
                    r = g * ROUNDS + s

                    def transposed(u):
                        for j in range(NG):
                            act.wait_ge(m.t_ready, (r * UR + u) * NG + j + 1)
                            if u >= 2 and j == 0:
                                act.wait_ge(m.o_ready, r * UR + u - 1)
                            nc.scalar.activation(pt_part(pth, u, j), t_bank(u, j), ACT.Copy).then_inc(
                                m.t_hi, 1)

                    def attended(u):
                        h, b = divmod(u, B)
                        act.wait_ge(m.o_ready, r * UR + u + 1)
                        nc.scalar.activation(oh[:, h, b * S:(b + 1) * S], OB[u % 2][:, 0:S], ACT.Copy).then_inc(
                            m.o_hi, 1)

                    for u in range(UR):
                        h, b = divmod(u, B)
                        for q in range(2):
                            bank, lo = score_bank(u, q)
                            act.wait_ge(m.max_done, (r * UR + u) * 2 + (q + 1 if cross else 2))
                            if u >= 3 and q == 0:
                                act.wait_ge(m.t_ready, (r * UR + u - 2) * NG)
                            nc.scalar.activation(pb[:, u % 3, q, lo:], bank[:, lo:], ACT.Exp,
                                                 bias=nmax[:, u % 2, q:q + 1],
                                                 accum_out=rsum[:, u % 2, q:q + 1]).then_inc(m.exp_done, 1)
                        if u >= 2:
                            transposed(u - 2)
                        if u >= 3:
                            attended(u - 3)
                        if b % 2:
                            query(r * QUAD + h + 1, b // 2, (h + 1) % 2)
                    transposed(UR - 2)
                    attended(UR - 3)
                    transposed(UR - 1)
                    attended(UR - 2)
                    attended(UR - 1)

        @block.vector
        def _(dve):
            nc.vector.memset(rsum[:], 1.0).then_inc(m.y_done, 1)

            def query(H, i, par):
                dve.wait_ge(m.q_hi, 2 * H + i + 1)
                cols = slice(i * 512, (i + 1) * 512)
                nc.vector.tensor_tensor(ql[:, par, cols], QB[i][:], f32(qh[:, par, cols]), ALU.subtract).then_inc(
                    m.q_lo, 1)

            for i in range(2):
                query(0, i, 0)
            with nc.vector.Fori(0, L1_GROUPS) as g:
                for i, (bank, high, low) in enumerate(kv_parts()):
                    dve.wait_ge(m.kv_hi, NKV * g + i + 1)
                    if i < NKV // 2:
                        for b in range(high.shape[1]):
                            last = nc.vector.scalar_tensor_tensor(low[:, b], bank[:, b], scale, f32(high[:, b]),
                                                                  ALU.mult, ALU.subtract)
                        last.then_inc(m.kv_lo, 1)
                    else:
                        nc.vector.tensor_tensor(low, bank, f32(high), ALU.subtract).then_inc(m.kv_lo, 1)
                    if i == 0:
                        bank, lo, hi = v_parts[1]
                        dve.wait_ge(m.vt_ready, NVP * g + 2)
                        nc.vector.tensor_copy(v_rows[:, lo:hi], bank).then_inc(m.vt_done, 1)
                with nc.vector.Fori(0, ROUNDS) as s:
                    r = g * ROUNDS + s

                    def transposed(u):
                        for j in range(NG):
                            dve.wait_ge(m.t_hi, (r * UR + u) * NG + j + 1)
                            nc.vector.tensor_tensor(pt_part(ptl, u, j), t_bank(u, j), f32(pt_part(pth, u, j)),
                                                    ALU.subtract).then_inc(m.t_lo, 1)

                    def attended(u):
                        h, b = divmod(u, B)
                        dve.wait_ge(m.o_hi, r * UR + u + 1)
                        cols = slice(b * S, (b + 1) * S)
                        nc.vector.tensor_tensor(ol[:, h, cols], OB[u % 2][:, 0:S], f32(oh[:, h, cols]),
                                                ALU.subtract).then_inc(m.o_lo, 1)

                    def projected(t):
                        dve.wait_ge(m.y_ready, r * NT + t + 1)
                        nc.vector.tensor_tensor(k.acc[:, t], SB[t % 2][:], k.acc[:, t], ALU.add).then_inc(
                            m.y_done, 1)

                    def inverse(u):
                        dve.wait_ge(m.exp_done, (r * UR + u) * 2 + 2)
                        if cross:
                            nc.vector.reciprocal(rinv[:, u % 3], rsum[:, u % 2]).then_inc(m.inv_done, 1)
                        else:
                            nc.vector.reciprocal(rfirst[:, u % 2], rsum[:, u % 2]).then_inc(m.inv_first, 1)
                            dve.wait_ge(m.inv_first, r * UR + u + 1)
                            nc.vector.tensor_tensor(rinv[:, u % 3], rfirst[:, u % 2], fix[:], ALU.mult).then_inc(
                                m.inv_done, 1)

                    def lows(u):
                        if u >= 2:
                            transposed(u - 2)
                        if u >= 3:
                            attended(u - 3)
                        if u % 2:
                            query(r * QUAD + u // B + 1, u % B // 2, (u // B + 1) % 2)

                    for u in range(UR):
                        if cross and u >= 1:
                            inverse(u - 1)
                        for q in range(2):
                            bank, lo = score_bank(u, q)
                            dve.wait_ge(m.s_ready, (r * UR + u) * 2 + (q + 1 if cross else 2))
                            nc.vector.tensor_reduce(nmax[:, u % 2, q:q + 1], bank[:, lo:], AX.X, ALU.max,
                                                    negate=True).then_inc(m.max_done, 1)
                        if cross:
                            lows(u)
                        elif u >= 1:
                            inverse(u - 1)
                            lows(u - 1)
                    inverse(UR - 1)
                    if not cross:
                        lows(UR - 1)
                    transposed(UR - 2)
                    attended(UR - 3)
                    projected(0)
                    transposed(UR - 1)
                    projected(1)
                    attended(UR - 2)
                    projected(2)
                    projected(3)
                    attended(UR - 1)
                    for t in range(4, NT):
                        projected(t)

        @block.tensor
        def _(pe):
            def query(H, i, par, kts=range(KT)):
                if kts[0] == 0:
                    pe.wait_ge(m.wq_split, H + 1)
                cols = slice(i * 512, (i + 1) * 512)
                last = products(nc, QB[i][:], [(wqh[:, par, kt], wql[:, par, kt], k.xh[:, kt, cols], k.xl[:, kt, cols])
                                               for kt in kts], start=kts[0] == 0, stop=kts[-1] == KT - 1)
                if kts[-1] == KT - 1:
                    last.then_inc(m.q_ready, 1)

            for i in range(2):
                query(0, i, 0)
            pe.wait_ge(m.cst_low, 1)
            pe.wait_ge(m.cst_split, 3 if cross else 5)
            with nc.tensor.Fori(0, L1_GROUPS) as g:
                pe.wait_ge(m.kvw_split, g + 1)

                def rows(which, bank, high, low, done):
                    products(nc, bank, [(wkvh[:, which, kt], wkvl[:, which, kt], high[kt], low[kt])
                                        for kt in range(KT)]).then_inc(done, 1)

                def x_half(t, i):
                    return [t[:, kt, i * 512:(i + 1) * 512] for kt in range(KT)]

                rows(0, TB[0][:], x_half(k.xh, 0), x_half(k.xl, 0), m.kv_ready)
                pe.wait_ge(m.y_done, g * ROUNDS * NT + 1)
                for i in range(2):
                    rows(1, v_parts[i][0], x_half(k.xh, i), x_half(k.xl, i), m.vt_ready)
                if cross:
                    in_ctx = [[t[:, kt] for kt in range(KT)] for t in (ch, cl)]
                    rows(1, v_parts[2][0], *in_ctx, m.vt_ready)
                rows(0, TB[1][:], x_half(k.xh, 1), x_half(k.xl, 1), m.kv_ready)
                if cross:
                    pe.wait_ge(m.q_lo, g * ROUNDS * QUAD * 2 + 2)
                    rows(0, QB[0][:, 0:B * CTX], *in_ctx, m.kv_ready)
                pe.wait_ge(m.vt_done, NVP * (g + 1))
                for i in range(2):
                    for t in range(4):
                        at = (4 * i + t) * P
                        last = nc.tensor.transpose(OB[i][:, t * HD:(t + 1) * HD], v_rows[:, at:at + P], k.ident[:])
                    last.then_inc(m.kv_ready, 1)
                if cross:
                    for b in range(B):
                        at = TOK + b * CTX
                        last = nc.tensor.transpose(QB[1][0:CTX, b * HD:(b + 1) * HD], v_rows[:, at:at + CTX],
                                                   k.ident[:])
                    last.then_inc(m.kv_ready, 1)
                with nc.tensor.Fori(0, ROUNDS) as s:
                    r = g * ROUNDS + s

                    def scores(u):
                        h, b = divmod(u, B)
                        if b % 2 == 0:
                            pe.wait_ge(m.q_lo, (r * QUAD + h) * 2 + b // 2 + 1)
                        for q in range(2):
                            if u == 0 and q == 0:
                                pe.wait_ge(m.y_done, r * NT + 1)
                            elif cross and u:
                                pe.wait_ge(m.exp_done, (r * UR + u - 1) * 2 + q + 1)
                            elif u >= 2 and q == 0:
                                pe.wait_ge(m.exp_done, (r * UR + u - 1) * 2)
                            tok = slice(b * S + q * P, b * S + (q + 1) * P)
                            if q == 0 and not cross:
                                diagonal = SB[u % 2][:].rearrange("p (c n) -> p c n", n=P)[:, 0:4:3]
                                nc.tensor.matmul(diagonal, k.ident_r[:], mask[:], start=True, stop=False,
                                                 skip_group_check=True)
                            products(nc, score_bank(u, q)[0], [(qh[:, h % 2, tok], ql[:, h % 2, tok],
                                                                kh[:, b], kl[:, b])], start=cross,
                                     cover=not cross).then_inc(m.s_ready, 1)

                    def transpose(u):
                        pe.wait_ge(m.p_done, r * UR + u + 1)
                        if cross and u >= 1:
                            pe.wait_ge(m.t_lo, (r * UR + u) * NG)
                        elif not cross and u >= 2:
                            pe.wait_ge(m.t_lo, r * UR + u - 1)
                        for j, (rows, width, parts) in enumerate(blocks):
                            for q, key, at in parts:
                                last = nc.tensor.transpose(t_bank(u, j)[:, at:at + P],
                                                           pb[:, u % 3, q, key:key + rows], k.ident[:])
                            last.then_inc(m.t_ready, 1)

                    def attend(u):
                        h, b = divmod(u, B)
                        pe.wait_ge(m.t_lo, (r * UR + u + 1) * NG)
                        if u >= 2:
                            pe.wait_ge(m.o_lo, r * UR + u - 1)
                        out = OB[u % 2][:, 0:S]
                        ph, pl = pth[:, u % 2], ptl[:, u % 2]
                        if cross:
                            last = products(nc, out, [
                                (vh[:, 2 * b], vl[:, 2 * b], ph[:, 0:S], pl[:, 0:S]),
                                (vh[:, 2 * b + 1], vl[:, 2 * b + 1], ph[:, S:2 * S], pl[:, S:2 * S]),
                                (vh[0:CTX, NT + b], vl[0:CTX, NT + b], ph[0:CTX, 2 * S:], pl[0:CTX, 2 * S:])])
                        else:
                            last = products(nc, out, [
                                (vh[:, 2 * b + 1], vl[:, 2 * b + 1], ph[:, 0:S], pl[:, 0:S]),
                                (vh[:, 2 * b], vl[:, 2 * b], ph[:, S:2 * S], pl[:, S:2 * S])])
                        last.then_inc(m.o_ready, 1)

                    def project(t):
                        pe.wait_ge(m.o_lo, r * UR + UR - B + t // 2 + 1)
                        pe.wait_ge(m.exp_done, (r * UR + UR) * 2)
                        if t >= 2:
                            pe.wait_ge(m.y_done, r * NT + t)
                        products(nc, SB[t % 2][:], [(oh[:, h, t * P:(t + 1) * P], ol[:, h, t * P:(t + 1) * P],
                                                     woh[:, h], wol[:, h]) for h in range(QUAD)]).then_inc(
                            m.y_ready, 1)

                    pe.wait_ge(m.kv_lo, NKV * g + NKV // 2)
                    for u in range(UR):
                        h, b = divmod(u, B)
                        scores(u)
                        if u == 2:
                            pe.wait_ge(m.kv_lo, NKV * (g + 1))
                        if b % 2 == 0:
                            pe.wait_ge(m.q_lo, (r * QUAD + h) * 2 + b // 2 + 1)
                        query(r * QUAD + h + 1, b // 2, (h + 1) % 2, range(0, 2) if b % 2 == 0 else range(2, KT))
                        if u >= 2:
                            transpose(u - 2)
                        if u >= 3:
                            attend(u - 3)
                    transpose(UR - 2)
                    attend(UR - 3)
                    pe.wait_ge(m.wo_split, (r + 1) * QUAD + 1)
                    project(0)
                    transpose(UR - 1)
                    project(1)
                    attend(UR - 2)
                    project(2)
                    project(3)
                    attend(UR - 1)
                    for t in range(4, NT):
                        project(t)


def build(nc, a, out, stages=6):
    with ExitStack() as ctx:
        def sb(name, shape, dt=F):
            return ctx.enter_context(nc.sbuf_tensor(name, shape, dt))

        k = Core()
        k.nc = nc
        k.acc = sb("acc", [P, NT, D])
        k.xh, k.xl = sb("xT_high", [P, KT, TOK], R), sb("xT_low", [P, KT, TOK], R)
        k.ident, k.ident_r, k.half = sb("ident", [P, P]), sb("ident_r", [P, P], R), sb("minus_half", [P, 1])
        k.one = sb("one", [P, 1])
        k.ps = [ctx.enter_context(nc.psum_tensor(f"bank{i}", [P, 512], F)) for i in range(8)]
        k.ident_in = a["identity"]
        with nc.Block() as block:
            @block.vector
            def _(dve):
                nc.vector.memset(k.half[:], -0.5)
                nc.vector.memset(k.one[:], 1.0)
        l0_self_attention(k, a["x"], a["xT"], a["a0_wq"], a["a0_bq"], a["a0_wk"], a["a0_bk"], a["a0_wv"], a["a0_bv"],
                          a["a0_wo"], a["a0_bo"], a["headmask"], a["causal4"])
        if stages == 1:
            return norm_stage(k, "n1", keep_T=False, out=out)
        l0_cross_attention(k, "n2", a["ctxT"], a["x0_wk"], a["x0_wq"], a["x0_wv"], a["x0_wo"], a["x0_q_norm"],
                           a["x0_k_norm"], a["x0_mask"])
        if stages == 2:
            return norm_stage(k, "n3", keep_T=False, out=out)
        mixture(k, "f0", a["f0_base"], a["f0_bias"], a["f0_small"], a["f0_up"], a["expand"],
                before=a["before"])
        if stages == 3:
            return norm_stage(k, "n5", keep_T=False, out=out)
        l1_attention(k, "a1", "n6", a["a1_wq"], a["a1_wk"], a["a1_wv"], a["a1_wo"], HD ** -0.5,
                     anticausal=a["anticausal"], uniform=a["uniform"], last_row=a["last_row"])
        if stages == 4:
            return norm_stage(k, "n7", keep_T=False, out=out)
        l1_attention(k, "x1", "n8", a["x1_wq"], a["x1_wk"], a["x1_wv"], a["x1_wo"], HD ** -0.5, ctxT=a["ctxT"])
        if stages == 5:
            return norm_stage(k, "n9", keep_T=False, out=out)
        mixture(k, "f1", a["f1_base"], a["f1_bias"], a["f1_small"], a["f1_up"], a["expand"],
                b_thr=a["f1_thr"], out=out)


def kernel(**inputs):
    import numpy as np
    import concourse.bacc as bacc
    from concourse.bass_utils import run_bass_kernel_spmd

    arrays = layouts(np, inputs)
    nc = bacc.Bacc("TRN2", target_bir_lowering=False, num_devices=1)
    args = {n: nc.dram_tensor("in_" + n, v.shape, mybir.dt.from_np(v.dtype), kind="ExternalInput").ap()
            for n, v in arrays.items()}
    out = nc.dram_tensor("out", (TOK, D), F, kind="ExternalOutput").ap()
    build(nc, args, out)
    r = run_bass_kernel_spmd(nc, [{"in_" + n: v for n, v in arrays.items()}], core_ids=[0])
    return r.results[0]["out"].reshape(B, S, D)


def layouts(np, i):
    def parts(w):
        return np.ascontiguousarray(w.reshape(KT, P, -1).transpose(1, 0, 2))

    i = {n: np.asarray(v) for n, v in i.items()}
    x = i["x"].reshape(TOK, D)
    a = {"x": x, "xT": parts(x.T), "identity": np.eye(P, dtype=np.float32)}
    a["a0_wq"] = parts(i["L0_attn_wq_w"].T)
    a["a0_bq"] = np.ascontiguousarray(i["L0_attn_wq_b"].reshape(NCH, P).T)
    for n in "kv":
        a[f"a0_w{n}"] = parts(np.tile(i[f"L0_attn_w{n}_w"], (HPC, 1)).T)
        a[f"a0_b{n}"] = np.tile(i[f"L0_attn_w{n}_b"], HPC).reshape(P, 1)
    a["a0_wo"] = parts(i["L0_attn_wo_w"].T)
    a["a0_bo"] = i["L0_attn_wo_b"]
    of_head = np.kron(np.eye(HPC), np.ones((HD0, 1))).astype(np.float32)
    a["headmask"] = np.concatenate([of_head[:, 0::2], of_head[:, 1::2]], 1)
    later = np.triu(np.ones((P, P)), 1)
    a["causal4"] = np.ascontiguousarray(np.repeat((later * MASKED).astype(np.float32)[:, None], 4, 1))
    c = i["ctx_4096"].reshape(B * CTX, D)
    a["ctxT"] = parts(c.T)

    def heads(w, n, spare):
        h = w.reshape(KT, P, n, HD).transpose(2, 1, 0, 3)
        return np.ascontiguousarray(np.concatenate([h, h[:spare]]))

    a["x0_wk"] = parts(i["L0_xattn_Wk"].T)
    a["x0_wq"] = heads(i["L0_xattn_Wq"].T, NH, X0_AHEAD)
    a["x0_wv"] = parts(i["L0_xattn_Wv"].T)
    wo = np.ascontiguousarray(i["L0_xattn_Wo"].T).reshape(NH, HD, D)
    a["x0_wo"] = np.concatenate([wo, wo[:2]])
    a["x0_q_norm"] = i["L0_xattn_q_norm_w"].reshape(HD, 1)
    a["x0_k_norm"] = i["L0_xattn_k_norm_w"].reshape(HD, 1)
    a["x0_mask"] = i["mask_1x1xSxS2_ff0"].reshape(S, CTX)
    for t, n in (("a1", "L1_attn"), ("x1", "L1_xattn")):
        a[t + "_wq"] = heads(i[n + "_Wq"], NH, WQ_AHEAD)
        a[t + "_wk"] = heads(i[n + "_Wk"], L1_GROUPS, 1)
        a[t + "_wv"] = heads(i[n + "_Wv"], L1_GROUPS, 1)
        a[t + "_wo"] = i[n + "_Wo"].reshape(NH, HD, D)
    a["anticausal"] = (np.tril(np.ones((P, P))) * MASKED).astype(np.float32)
    a["uniform"] = np.zeros((P, P), np.float32)
    a["uniform"][:, P - 1] = 1 / S
    a["last_row"] = np.ones((P, 2), np.float32)
    a["last_row"][P - 1, 1] = P / S
    a["expand"] = np.kron(np.eye(NE), np.ones((1, RANK))).astype(np.float32)
    a["before"] = np.repeat(np.tril(np.ones((NE, NE), np.float32), -1)[None], P, 0)

    def small(A, gate, *thr):
        cols = [A.reshape(ER, D).T, gate.T] + [t.reshape(D, 1) for t in thr]
        have = sum(c.shape[1] for c in cols)
        return parts(np.concatenate(cols + [np.zeros((D, ER + GATE - have), np.float32)], 1))

    def up(w):
        return np.ascontiguousarray(w.transpose(0, 2, 1)).reshape(ER, D)

    a["f0_base"], a["f0_bias"] = parts(i["L0_ffn_W_base"].T), i["L0_ffn_b_base"]
    a["f0_small"], a["f0_up"] = small(i["L0_ffn_A"], i["L0_ffn_W_gate"]), up(i["L0_ffn_B"])
    a["f1_base"], a["f1_bias"] = parts(i["L1_ffn_W_base"].T), i["L1_ffn_b_base"]
    a["f1_small"] = small(i["L1_ffn_A_w"], i["L1_ffn_W_gate"], i["L1_ffn_W_thr"])
    a["f1_up"], a["f1_thr"] = up(i["L1_ffn_B_w"]), i["L1_ffn_b_thr"]
    return a
```
